# Optimizing a Trainium2 kernel written in Bass

```python
import numpy as np
import jax
import jax.numpy as jnp

def _softmax(x, axis=-1):
    return jax.nn.softmax(x, axis=axis)

def _gelu(x):
    return jax.nn.gelu(x, approximate=True)

def _silu(x):
    return jax.nn.silu(x)

def _sigmoid(x):
    return jax.nn.sigmoid(x)

def _layernorm(x, axis=-1, eps=1e-05):
    m = jnp.mean(x, axis=axis, keepdims=True)
    v = jnp.var(x, axis=axis, keepdims=True)
    return (x - m) / jnp.sqrt(v + eps)

def _scatter_add(tgt, idx, src, axis=0):
    return tgt.at[idx].add(src)

def _segment_sum(src, seg, n):
    return jax.ops.segment_sum(src, seg, n)
kernel_name = 'mk_hybrid_d2_jaxref_r8_fc8d51'

def setup_inputs(seed: int=0):
    np.random.seed(seed)
    _w = jnp.asarray

    def _L0_attn_a_setup():
        import jax, jax.numpy as jnp
        import numpy as np
        D_MODEL, N_HEADS = (128, 16)
        D_H = D_MODEL // N_HEADS
        D_HR = D_H // 2
        D_LATENT = 32
        THETA = 10000.0

        def rope(x, theta=THETA):
            S, d = (x.shape[-2], x.shape[-1])
            inv = theta ** (-jnp.arange(0, d, 2, dtype=jnp.float32) / d)
            ang = jnp.arange(S, dtype=jnp.float32)[:, None] * inv
            cos, sin = (jnp.cos(ang), jnp.sin(ang))
            x1, x2 = (x[..., 0::2], x[..., 1::2])
            r1 = x1 * cos - x2 * sin
            r2 = x1 * sin + x2 * cos
            return jnp.stack([r1, r2], axis=-1).reshape(x.shape)
        key = jax.random.key(seed)
        ks = jax.random.split(key, 9)
        s = lambda fan_in: 1.0 / np.sqrt(fan_in)
        return {'x': jax.random.normal(ks[0], (4, 256, D_MODEL), jnp.float32), 'W_DQ': jax.random.normal(ks[1], (D_MODEL, D_LATENT), jnp.float32) * s(D_MODEL), 'W_UQ': jax.random.normal(ks[2], (D_LATENT, N_HEADS * D_H), jnp.float32) * s(D_LATENT), 'W_QR': jax.random.normal(ks[3], (D_LATENT, N_HEADS * D_HR), jnp.float32) * s(D_LATENT), 'W_DKV': jax.random.normal(ks[4], (D_MODEL, D_LATENT), jnp.float32) * s(D_MODEL), 'W_UK': jax.random.normal(ks[5], (D_LATENT, N_HEADS * D_H), jnp.float32) * s(D_LATENT), 'W_UV': jax.random.normal(ks[6], (D_LATENT, N_HEADS * D_H), jnp.float32) * s(D_LATENT), 'W_KR': jax.random.normal(ks[7], (D_MODEL, D_HR), jnp.float32) * s(D_MODEL), 'W_O': jax.random.normal(ks[8], (N_HEADS * D_H, D_MODEL), jnp.float32) * s(N_HEADS * D_H)}
    _L0_attn_a_in = _L0_attn_a_setup()

    def _L0_attn_b_setup():
        import jax, jax.numpy as jnp
        import numpy as np
        B, T, D, C = (4, 1024, 128, 64)
        key = jax.random.key(seed)
        k1, k2, k3 = jax.random.split(key, 3)
        out = jax.random.normal(k1, (B, T, D), jnp.float32)
        W_write = jax.random.normal(k2, (D, D), jnp.float32) / np.float32(np.sqrt(D))
        W_read = jax.random.normal(k3, (D, D), jnp.float32) / np.float32(np.sqrt(D))
        decay = jnp.float32(4.6)
        log_alpha = jnp.log(jnp.float32(0.03))
        return {'out': out, 'W_write': W_write, 'W_read': W_read, 'decay': decay, 'log_alpha': log_alpha}
    _L0_attn_b_in = _L0_attn_b_setup()

    def _L0_ffn_setup():
        import jax, jax.numpy as jnp
        import numpy as np
        EPS = 1e-05

        def _ln(x, g, b):
            mu = jnp.mean(x, axis=-1, keepdims=True)
            var = jnp.mean(jnp.square(x - mu), axis=-1, keepdims=True)
            return (x - mu) * jax.lax.rsqrt(var + EPS) * g + b

        def _forward(x, index_b, index_t, sw1, sb1, sw2, sb2, sw3, sb3, s_ln_g, s_ln_b, sg_w, sg_b, eg_w, eg_b, exp_bias, ew1, eb1, ew2, eb2, ew3, eb3, sel_ln_g, sel_ln_b):
            x1 = jnp.einsum('btd,hd->bth', x, sw1) + sb1
            x2 = jnp.einsum('btd,hd->bth', x, sw2) + sb2
            sh = _ln(jax.nn.silu(x1) * x2, s_ln_g, s_ln_b)
            shared_out = jnp.einsum('bth,dh->btd', sh, sw3) + sb3
            x_moe = x[index_b, index_t]
            shared_scores = jax.nn.sigmoid(x_moe @ sg_w.T + sg_b)
            expert_scores = jax.nn.sigmoid(x_moe @ eg_w.T + eg_b)
            top1_idx = jnp.argmax(expert_scores + exp_bias, axis=-1)
            top1_score = jnp.take_along_axis(expert_scores, top1_idx[:, None], axis=-1)
            weights = jax.nn.softmax(jnp.concatenate([shared_scores, top1_score], axis=-1), axis=-1)
            shared_w, expert_w = (weights[:, 0], weights[:, 1])
            shared_moe_out = shared_out[index_b, index_t] * shared_w[:, None]
            h1 = jnp.einsum('md,ehd->meh', x_moe, ew1) + eb1
            h2 = jnp.einsum('md,ehd->meh', x_moe, ew2) + eb2
            z = _ln(jax.nn.silu(h1) * h2, sel_ln_g, sel_ln_b)
            out_all = jnp.einsum('meh,edh->med', z, ew3) + eb3
            expert_out = jnp.take_along_axis(out_all, top1_idx[:, None, None], axis=1)[:, 0]
            expert_moe_out = expert_out * expert_w[:, None]
            final_out = shared_out.at[index_b, index_t].set(shared_moe_out + expert_moe_out)
            return final_out
        B, T, D, E, H, M = (2, 256, 128, 8, 64, 256)
        key = jax.random.key(seed)
        ks = jax.random.split(key, 24)
        s = 0.02
        inp = {}
        inp['x'] = jax.random.normal(ks[0], (B, T, D), jnp.float32)
        flat = jnp.arange(M, dtype=jnp.int32) * 2
        inp['index_b'] = flat // T
        inp['index_t'] = flat % T
        inp['sw1'] = jax.random.normal(ks[1], (H, D), jnp.float32) * s
        inp['sb1'] = jnp.zeros((H,), jnp.float32)
        inp['sw2'] = jax.random.normal(ks[2], (H, D), jnp.float32) * s
        inp['sb2'] = jnp.zeros((H,), jnp.float32)
        inp['sw3'] = jax.random.normal(ks[3], (D, H), jnp.float32) * s
        inp['sb3'] = jnp.zeros((D,), jnp.float32)
        inp['s_ln_g'] = jnp.ones((H,), jnp.float32)
        inp['s_ln_b'] = jnp.zeros((H,), jnp.float32)
        inp['sg_w'] = jax.random.normal(ks[4], (1, D), jnp.float32) * s
        inp['sg_b'] = jnp.zeros((1,), jnp.float32)
        inp['eg_w'] = jax.random.normal(ks[5], (E, D), jnp.float32) * s
        inp['eg_b'] = jnp.zeros((E,), jnp.float32)
        inp['exp_bias'] = jnp.zeros((E,), jnp.float32)
        inp['ew1'] = jax.random.normal(ks[6], (E, H, D), jnp.float32) * s
        inp['eb1'] = jnp.zeros((E, H), jnp.float32)
        inp['ew2'] = jax.random.normal(ks[7], (E, H, D), jnp.float32) * s
        inp['eb2'] = jnp.zeros((E, H), jnp.float32)
        inp['ew3'] = jax.random.normal(ks[8], (E, D, H), jnp.float32) * s
        inp['eb3'] = jnp.zeros((E, D), jnp.float32)
        inp['sel_ln_g'] = jnp.ones((H,), jnp.float32)
        inp['sel_ln_b'] = jnp.zeros((H,), jnp.float32)
        return inp
    _L0_ffn_in = _L0_ffn_setup()

    def _L1_attn_a_setup():
        import jax, jax.numpy as jnp
        import numpy as np
        B, N, D_MODEL, H, D_HEAD = (1, 256, 128, 16, 64)
        A0, A1, LIM = (1.0, 1.0, 1.0)

        def _fastmax_causal_p1(q, k, v):
            qn = jnp.max(jnp.linalg.norm(q, axis=-1), axis=-1)[..., None, None]
            kn = jnp.max(jnp.linalg.norm(k, axis=-1), axis=-1)[..., None, None]
            q = LIM * q / qn
            k = LIM * k / kn
            n = q.shape[2]
            kv = jnp.cumsum(k[..., :, None] * v[..., None, :], axis=2)
            num = A0 * jnp.cumsum(v, axis=2) + A1 * jnp.einsum('bhnd,bhnde->bhne', q, kv)
            ksum = jnp.cumsum(k, axis=2)
            den = A0 * jnp.arange(1, n + 1, dtype=q.dtype) + A1 * jnp.einsum('bhnd,bhnd->bhn', q, ksum)
            return num / den[..., None]
        key = jax.random.key(seed)
        ks = jax.random.split(key, 6)
        s = 1.0 / np.sqrt(D_MODEL).astype(np.float32)
        return {'X': jax.random.normal(ks[0], (B, N, D_MODEL), jnp.float32), 'Wq': jax.random.normal(ks[1], (H * D_HEAD, D_MODEL), jnp.float32) * s, 'Wk': jax.random.normal(ks[2], (H * D_HEAD, D_MODEL), jnp.float32) * s, 'Wv': jax.random.normal(ks[3], (H * D_HEAD, D_MODEL), jnp.float32) * s, 'Wo': jax.random.normal(ks[4], (D_MODEL, H * D_HEAD), jnp.float32) * s, 'bo': jnp.zeros((D_MODEL,), jnp.float32)}
    _L1_attn_a_in = _L1_attn_a_setup()

    def _L1_attn_b_setup():
        import jax, jax.numpy as jnp
        import numpy as np
        B, S, H = (8, 256, 128)
        key = jax.random.key(seed)
        k1, k2, k3 = jax.random.split(key, 3)
        x = jax.random.normal(k1, (B, S, H), dtype=jnp.float32)
        W_qkv = jax.random.normal(k2, (3 * H, H), dtype=jnp.float32) / np.sqrt(H)
        W_out = jax.random.normal(k3, (H, H), dtype=jnp.float32) / np.sqrt(H)
        return {'x': x, 'W_qkv': W_qkv, 'W_out': W_out}
    _L1_attn_b_in = _L1_attn_b_setup()

    def _L1_ffn_setup():
        import jax, jax.numpy as jnp
        import numpy as np
        DIM = 128
        INTER = 256
        E = 8
        TOPK = 2
        ROUTE_SCALE = 1.0

        def _mlp(x, w1, w2, w3):
            h = jax.nn.silu(x @ w1.T) * (x @ w3.T)
            return h @ w2.T
        key = jax.random.key(seed)
        ks = jax.random.split(key, 10)
        s_in = 0.02
        return {'x': jax.random.normal(ks[0], (4, 256, DIM), dtype=jnp.float32), 'gate_w': jax.random.normal(ks[1], (E, DIM), dtype=jnp.float32) * s_in, 'gate_bias': jax.random.normal(ks[2], (E,), dtype=jnp.float32) * 0.01, 'w1': jax.random.normal(ks[3], (E, INTER, DIM), dtype=jnp.float32) * s_in, 'w2': jax.random.normal(ks[4], (E, DIM, INTER), dtype=jnp.float32) * s_in, 'w3': jax.random.normal(ks[5], (E, INTER, DIM), dtype=jnp.float32) * s_in, 'sw1': jax.random.normal(ks[6], (INTER, DIM), dtype=jnp.float32) * s_in, 'sw2': jax.random.normal(ks[7], (DIM, INTER), dtype=jnp.float32) * s_in, 'sw3': jax.random.normal(ks[8], (INTER, DIM), dtype=jnp.float32) * s_in}
    _L1_ffn_in = _L1_ffn_setup()
    _d = {'L0_attn_a_x': _L0_attn_a_in['x'], 'L0_attn_a_W_DQ': _L0_attn_a_in['W_DQ'], 'L0_attn_a_W_UQ': _L0_attn_a_in['W_UQ'], 'L0_attn_a_W_QR': _L0_attn_a_in['W_QR'], 'L0_attn_a_W_DKV': _L0_attn_a_in['W_DKV'], 'L0_attn_a_W_UK': _L0_attn_a_in['W_UK'], 'L0_attn_a_W_UV': _L0_attn_a_in['W_UV'], 'L0_attn_a_W_KR': _L0_attn_a_in['W_KR'], 'L0_attn_a_W_O': _L0_attn_a_in['W_O'], 'L0_attn_b_W_write': _L0_attn_b_in['W_write'], 'L0_attn_b_W_read': _L0_attn_b_in['W_read'], 'L0_attn_b_decay': _L0_attn_b_in['decay'], 'L0_attn_b_log_alpha': _L0_attn_b_in['log_alpha'], 'L0_ffn_index_b': _L0_ffn_in['index_b'], 'L0_ffn_index_t': _L0_ffn_in['index_t'], 'L0_ffn_sw1': _L0_ffn_in['sw1'], 'L0_ffn_sb1': _L0_ffn_in['sb1'], 'L0_ffn_sw2': _L0_ffn_in['sw2'], 'L0_ffn_sb2': _L0_ffn_in['sb2'], 'L0_ffn_sw3': _L0_ffn_in['sw3'], 'L0_ffn_sb3': _L0_ffn_in['sb3'], 'L0_ffn_s_ln_g': _L0_ffn_in['s_ln_g'], 'L0_ffn_s_ln_b': _L0_ffn_in['s_ln_b'], 'L0_ffn_sg_w': _L0_ffn_in['sg_w'], 'L0_ffn_sg_b': _L0_ffn_in['sg_b'], 'L0_ffn_eg_w': _L0_ffn_in['eg_w'], 'L0_ffn_eg_b': _L0_ffn_in['eg_b'], 'L0_ffn_exp_bias': _L0_ffn_in['exp_bias'], 'L0_ffn_ew1': _L0_ffn_in['ew1'], 'L0_ffn_eb1': _L0_ffn_in['eb1'], 'L0_ffn_ew2': _L0_ffn_in['ew2'], 'L0_ffn_eb2': _L0_ffn_in['eb2'], 'L0_ffn_ew3': _L0_ffn_in['ew3'], 'L0_ffn_eb3': _L0_ffn_in['eb3'], 'L0_ffn_sel_ln_g': _L0_ffn_in['sel_ln_g'], 'L0_ffn_sel_ln_b': _L0_ffn_in['sel_ln_b'], 'L1_attn_a_Wq': _L1_attn_a_in['Wq'], 'L1_attn_a_Wk': _L1_attn_a_in['Wk'], 'L1_attn_a_Wv': _L1_attn_a_in['Wv'], 'L1_attn_a_Wo': _L1_attn_a_in['Wo'], 'L1_attn_a_bo': _L1_attn_a_in['bo'], 'L1_attn_b_W_qkv': _L1_attn_b_in['W_qkv'], 'L1_attn_b_W_out': _L1_attn_b_in['W_out'], 'L1_ffn_gate_w': _L1_ffn_in['gate_w'], 'L1_ffn_gate_bias': _L1_ffn_in['gate_bias'], 'L1_ffn_w1': _L1_ffn_in['w1'], 'L1_ffn_w2': _L1_ffn_in['w2'], 'L1_ffn_w3': _L1_ffn_in['w3'], 'L1_ffn_sw1': _L1_ffn_in['sw1'], 'L1_ffn_sw2': _L1_ffn_in['sw2'], 'L1_ffn_sw3': _L1_ffn_in['sw3']}
    _x0 = _d['L0_attn_a_x']
    _d['L0_attn_a_x'] = jax.random.normal(jax.random.fold_in(jax.random.key(seed), 1), (1, 2048, 128), dtype=_x0.dtype)
    del _x0
    return _d

def reference(L0_attn_a_x, L0_attn_a_W_DQ, L0_attn_a_W_UQ, L0_attn_a_W_QR, L0_attn_a_W_DKV, L0_attn_a_W_UK, L0_attn_a_W_UV, L0_attn_a_W_KR, L0_attn_a_W_O, L0_attn_b_W_write, L0_attn_b_W_read, L0_attn_b_decay, L0_attn_b_log_alpha, L0_ffn_index_b, L0_ffn_index_t, L0_ffn_sw1, L0_ffn_sb1, L0_ffn_sw2, L0_ffn_sb2, L0_ffn_sw3, L0_ffn_sb3, L0_ffn_s_ln_g, L0_ffn_s_ln_b, L0_ffn_sg_w, L0_ffn_sg_b, L0_ffn_eg_w, L0_ffn_eg_b, L0_ffn_exp_bias, L0_ffn_ew1, L0_ffn_eb1, L0_ffn_ew2, L0_ffn_eb2, L0_ffn_ew3, L0_ffn_eb3, L0_ffn_sel_ln_g, L0_ffn_sel_ln_b, L1_attn_a_Wq, L1_attn_a_Wk, L1_attn_a_Wv, L1_attn_a_Wo, L1_attn_a_bo, L1_attn_b_W_qkv, L1_attn_b_W_out, L1_ffn_gate_w, L1_ffn_gate_bias, L1_ffn_w1, L1_ffn_w2, L1_ffn_w3, L1_ffn_sw1, L1_ffn_sw2, L1_ffn_sw3):

    def _L0_attn_a_ref(x, W_DQ, W_UQ, W_QR, W_DKV, W_UK, W_UV, W_KR, W_O):
        import jax, jax.numpy as jnp
        import numpy as np
        D_MODEL, N_HEADS = (128, 16)
        D_H = D_MODEL // N_HEADS
        D_HR = D_H // 2
        D_LATENT = 32
        THETA = 10000.0

        def rope(x, theta=THETA):
            S, d = (x.shape[-2], x.shape[-1])
            inv = theta ** (-jnp.arange(0, d, 2, dtype=jnp.float32) / d)
            ang = jnp.arange(S, dtype=jnp.float32)[:, None] * inv
            cos, sin = (jnp.cos(ang), jnp.sin(ang))
            x1, x2 = (x[..., 0::2], x[..., 1::2])
            r1 = x1 * cos - x2 * sin
            r2 = x1 * sin + x2 * cos
            return jnp.stack([r1, r2], axis=-1).reshape(x.shape)
        B, S, _ = x.shape
        d_qk = D_H + D_HR
        c_q = x @ W_DQ
        Qc = (c_q @ W_UQ).reshape(B, S, N_HEADS, D_H).transpose(0, 2, 1, 3)
        Qr = (c_q @ W_QR).reshape(B, S, N_HEADS, D_HR).transpose(0, 2, 1, 3)
        Qr = rope(Qr)
        c_kv = x @ W_DKV
        Kc = (c_kv @ W_UK).reshape(B, S, N_HEADS, D_H).transpose(0, 2, 1, 3)
        Kr = rope((x @ W_KR)[:, None, :, :])
        Kr = jnp.broadcast_to(Kr, (B, N_HEADS, S, D_HR))
        V = (c_kv @ W_UV).reshape(B, S, N_HEADS, D_H).transpose(0, 2, 1, 3)
        Q = jnp.concatenate([Qc, Qr], axis=-1)
        K = jnp.concatenate([Kc, Kr], axis=-1)
        scores = jnp.einsum('bhqd,bhkd->bhqk', Q, K)
        scores = jnp.clip(scores, -80.0, 80.0)
        causal = jnp.tril(jnp.ones((S, S), dtype=bool))
        scores = jnp.where(causal, scores, -jnp.inf)
        weights = jax.nn.softmax(scores / jnp.sqrt(jnp.float32(d_qk)), axis=-1)
        attn = jnp.einsum('bhqk,bhkd->bhqd', weights, V)
        attn = attn.transpose(0, 2, 1, 3).reshape(B, S, N_HEADS * D_H)
        return attn @ W_O

    def _L0_attn_b_ref(out, W_write, W_read, decay, log_alpha):
        import jax, jax.numpy as jnp
        import numpy as np
        B, T, D, C = (4, 1024, 128, 64)
        Bd, Td, Dd = out.shape
        nC = Td // C
        out32 = out.astype(jnp.float32)
        gamma = jax.nn.sigmoid(decay)
        log_gamma = jnp.log(gamma)
        v = out32 @ W_write.T
        wk = jnp.pad(out32[:, :-1], ((0, 0), (1, 0), (0, 0)))
        rk = out32
        p = jnp.arange(C)
        diffs = jnp.maximum(p[:, None] - 1 - p[None, :], 0)
        causal = (p[:, None] > p[None, :]).astype(jnp.float32)
        M = jnp.exp(diffs * log_gamma) * causal
        dec_inter = gamma ** p
        gw = gamma ** (C - 1 - p)
        gC = gamma ** C

        def chunk(x):
            return x.reshape(Bd, nC, C, Dd).transpose(1, 0, 2, 3)
        rk_c, wk_c, v_c = (chunk(rk), chunk(wk), chunk(v))

        def body(W, xs):
            r, w, vv = xs
            inter = jnp.einsum('bde,bce->bcd', W, r) * dec_inter[None, :, None]
            S = jnp.einsum('bcd,bed->bce', r, w)
            intra = jnp.einsum('bce,bed->bcd', S * M, vv)
            W_new = gC * W + jnp.einsum('bcd,bce->bde', vv * gw[None, :, None], w)
            return (W_new, inter + intra)
        W0 = jnp.zeros((Bd, Dd, Dd), jnp.float32)
        _, reads = jax.lax.scan(body, W0, (rk_c, wk_c, v_c))
        reads = reads.transpose(1, 0, 2, 3).reshape(Bd, Td, Dd)
        alpha = jnp.exp(log_alpha)
        return out + alpha * (reads @ W_read.T).astype(out.dtype)

    def _L0_ffn_ref(x, index_b, index_t, sw1, sb1, sw2, sb2, sw3, sb3, s_ln_g, s_ln_b, sg_w, sg_b, eg_w, eg_b, exp_bias, ew1, eb1, ew2, eb2, ew3, eb3, sel_ln_g, sel_ln_b):
        import jax, jax.numpy as jnp
        import numpy as np
        EPS = 1e-05

        def _ln(x, g, b):
            mu = jnp.mean(x, axis=-1, keepdims=True)
            var = jnp.mean(jnp.square(x - mu), axis=-1, keepdims=True)
            return (x - mu) * jax.lax.rsqrt(var + EPS) * g + b

        def _forward(x, index_b, index_t, sw1, sb1, sw2, sb2, sw3, sb3, s_ln_g, s_ln_b, sg_w, sg_b, eg_w, eg_b, exp_bias, ew1, eb1, ew2, eb2, ew3, eb3, sel_ln_g, sel_ln_b):
            x1 = jnp.einsum('btd,hd->bth', x, sw1) + sb1
            x2 = jnp.einsum('btd,hd->bth', x, sw2) + sb2
            sh = _ln(jax.nn.silu(x1) * x2, s_ln_g, s_ln_b)
            shared_out = jnp.einsum('bth,dh->btd', sh, sw3) + sb3
            x_moe = x[index_b, index_t]
            shared_scores = jax.nn.sigmoid(x_moe @ sg_w.T + sg_b)
            expert_scores = jax.nn.sigmoid(x_moe @ eg_w.T + eg_b)
            top1_idx = jnp.argmax(expert_scores + exp_bias, axis=-1)
            top1_score = jnp.take_along_axis(expert_scores, top1_idx[:, None], axis=-1)
            weights = jax.nn.softmax(jnp.concatenate([shared_scores, top1_score], axis=-1), axis=-1)
            shared_w, expert_w = (weights[:, 0], weights[:, 1])
            shared_moe_out = shared_out[index_b, index_t] * shared_w[:, None]
            h1 = jnp.einsum('md,ehd->meh', x_moe, ew1) + eb1
            h2 = jnp.einsum('md,ehd->meh', x_moe, ew2) + eb2
            z = _ln(jax.nn.silu(h1) * h2, sel_ln_g, sel_ln_b)
            out_all = jnp.einsum('meh,edh->med', z, ew3) + eb3
            expert_out = jnp.take_along_axis(out_all, top1_idx[:, None, None], axis=1)[:, 0]
            expert_moe_out = expert_out * expert_w[:, None]
            final_out = shared_out.at[index_b, index_t].set(shared_moe_out + expert_moe_out)
            return final_out
        return _forward(x, index_b, index_t, sw1, sb1, sw2, sb2, sw3, sb3, s_ln_g, s_ln_b, sg_w, sg_b, eg_w, eg_b, exp_bias, ew1, eb1, ew2, eb2, ew3, eb3, sel_ln_g, sel_ln_b)

    def _L1_attn_a_ref(X, Wq, Wk, Wv, Wo, bo):
        import jax, jax.numpy as jnp
        import numpy as np
        B, N, D_MODEL, H, D_HEAD = (1, 256, 128, 16, 64)
        A0, A1, LIM = (1.0, 1.0, 1.0)

        def _fastmax_causal_p1(q, k, v):
            qn = jnp.max(jnp.linalg.norm(q, axis=-1), axis=-1)[..., None, None]
            kn = jnp.max(jnp.linalg.norm(k, axis=-1), axis=-1)[..., None, None]
            q = LIM * q / qn
            k = LIM * k / kn
            n = q.shape[2]
            kv = jnp.cumsum(k[..., :, None] * v[..., None, :], axis=2)
            num = A0 * jnp.cumsum(v, axis=2) + A1 * jnp.einsum('bhnd,bhnde->bhne', q, kv)
            ksum = jnp.cumsum(k, axis=2)
            den = A0 * jnp.arange(1, n + 1, dtype=q.dtype) + A1 * jnp.einsum('bhnd,bhnd->bhn', q, ksum)
            return num / den[..., None]
        b, n, _ = X.shape

        def heads(W):
            return (X @ W.T).reshape(b, n, H, D_HEAD).transpose(0, 2, 1, 3)
        q, k, v = (heads(Wq), heads(Wk), heads(Wv))
        vh = _fastmax_causal_p1(q, k, v)
        vh = vh.transpose(0, 2, 1, 3).reshape(b, n, H * D_HEAD)
        return vh @ Wo.T + bo

    def _L1_attn_b_ref(x, W_qkv, W_out):
        import jax, jax.numpy as jnp
        import numpy as np
        B, S, H = (8, 256, 128)
        h = x.shape[-1]
        scale = 1.0 / np.sqrt(h).astype(np.float32)
        y = jnp.einsum('bsh,oh->bso', x, W_qkv).reshape(*x.shape, 3)
        q, k, v = (y[..., 0], y[..., 1], y[..., 2])
        scores = jnp.einsum('bqh,bkh->bqk', q, k) * scale
        attn = jax.nn.softmax(scores, axis=-1)
        ctx = jnp.einsum('bqk,bkh->bqh', attn, v)
        out = jnp.einsum('bsh,oh->bso', ctx, W_out)
        return out

    def _L1_ffn_ref(x, gate_w, gate_bias, w1, w2, w3, sw1, sw2, sw3):
        import jax, jax.numpy as jnp
        import numpy as np
        DIM = 128
        INTER = 256
        E = 8
        TOPK = 2
        ROUTE_SCALE = 1.0

        def _mlp(x, w1, w2, w3):
            h = jax.nn.silu(x @ w1.T) * (x @ w3.T)
            return h @ w2.T
        shape = x.shape
        xt = x.reshape(-1, DIM)
        T = xt.shape[0]
        logits = xt @ gate_w.T
        scores = jax.nn.softmax(logits.astype(jnp.float32), axis=-1)
        original_scores = scores
        biased = scores + gate_bias
        _, indices = jax.lax.top_k(biased, TOPK)
        weights = jnp.take_along_axis(original_scores, indices, axis=1)
        weights = (weights * ROUTE_SCALE).astype(x.dtype)
        combine = (jax.nn.one_hot(indices, E, dtype=weights.dtype) * weights[..., None]).sum(axis=1)
        y = jnp.zeros_like(xt)
        for e in range(E):
            y = y + _mlp(xt, w1[e], w2[e], w3[e]) * combine[:, e:e + 1]
        z = _mlp(xt, sw1, sw2, sw3)
        return (y + z).reshape(shape)
    x = L0_attn_a_x
    x = x + _L0_attn_a_ref(_layernorm(x, axis=-1), L0_attn_a_W_DQ, L0_attn_a_W_UQ, L0_attn_a_W_QR, L0_attn_a_W_DKV, L0_attn_a_W_UK, L0_attn_a_W_UV, L0_attn_a_W_KR, L0_attn_a_W_O)
    x = x + _L0_ffn_ref(_layernorm(x, axis=-1), L0_ffn_index_b, L0_ffn_index_t, L0_ffn_sw1, L0_ffn_sb1, L0_ffn_sw2, L0_ffn_sb2, L0_ffn_sw3, L0_ffn_sb3, L0_ffn_s_ln_g, L0_ffn_s_ln_b, L0_ffn_sg_w, L0_ffn_sg_b, L0_ffn_eg_w, L0_ffn_eg_b, L0_ffn_exp_bias, L0_ffn_ew1, L0_ffn_eb1, L0_ffn_ew2, L0_ffn_eb2, L0_ffn_ew3, L0_ffn_eb3, L0_ffn_sel_ln_g, L0_ffn_sel_ln_b)
    x = x + _L0_attn_b_ref(_layernorm(x, axis=-1), L0_attn_b_W_write, L0_attn_b_W_read, L0_attn_b_decay, L0_attn_b_log_alpha)
    x = x + _L0_ffn_ref(_layernorm(x, axis=-1), L0_ffn_index_b, L0_ffn_index_t, L0_ffn_sw1, L0_ffn_sb1, L0_ffn_sw2, L0_ffn_sb2, L0_ffn_sw3, L0_ffn_sb3, L0_ffn_s_ln_g, L0_ffn_s_ln_b, L0_ffn_sg_w, L0_ffn_sg_b, L0_ffn_eg_w, L0_ffn_eg_b, L0_ffn_exp_bias, L0_ffn_ew1, L0_ffn_eb1, L0_ffn_ew2, L0_ffn_eb2, L0_ffn_ew3, L0_ffn_eb3, L0_ffn_sel_ln_g, L0_ffn_sel_ln_b)
    x = x + _L1_attn_a_ref(_layernorm(x, axis=-1), L1_attn_a_Wq, L1_attn_a_Wk, L1_attn_a_Wv, L1_attn_a_Wo, L1_attn_a_bo)
    x = x + _L1_ffn_ref(_layernorm(x, axis=-1), L1_ffn_gate_w, L1_ffn_gate_bias, L1_ffn_w1, L1_ffn_w2, L1_ffn_w3, L1_ffn_sw1, L1_ffn_sw2, L1_ffn_sw3)
    x = x + _L1_attn_b_ref(_layernorm(x, axis=-1), L1_attn_b_W_qkv, L1_attn_b_W_out)
    x = x + _L1_ffn_ref(_layernorm(x, axis=-1), L1_ffn_gate_w, L1_ffn_gate_bias, L1_ffn_w1, L1_ffn_w2, L1_ffn_w3, L1_ffn_sw1, L1_ffn_sw2, L1_ffn_sw3)
    return x

_drawn_inputs = setup_inputs


def setup_inputs(seed=0):
    import zlib

    import numpy as np

    out = dict(_drawn_inputs(seed))
    spreads = {'L0_ffn_sb1': (0.0, 0.1),
     'L0_ffn_sb2': (0.0, 0.1),
     'L0_ffn_sb3': (0.0, 0.1),
     'L0_ffn_s_ln_g': (1.0, 0.2),
     'L0_ffn_s_ln_b': (0.0, 0.1),
     'L0_ffn_eg_b': (0.0, 0.8),
     'L0_ffn_exp_bias': (0.0, 0.1),
     'L0_ffn_eb1': (0.0, 0.554),
     'L0_ffn_eb2': (0.0, 0.675),
     'L0_ffn_eb3': (0.0, 0.297),
     'L0_ffn_sel_ln_g': (1.0, 0.6),
     'L0_ffn_sel_ln_b': (0.0, 0.8),
     'L1_attn_a_bo': (0.0, 0.1)}
    factors = {'L0_ffn_sg_w': 8.0,
     'L0_ffn_eg_w': 2.699,
     'L1_attn_a_Wq': 7.024,
     'L1_attn_a_Wk': 7.71,
     'L1_ffn_gate_w': 8.0,
     'L1_ffn_gate_bias': 8.0,
     'L1_ffn_w1': 8.0,
     'L1_ffn_w2': 8.0,
     'L1_ffn_w3': 8.0,
     'L1_ffn_sw1': 8.0,
     'L1_ffn_sw2': 8.0,
     'L1_ffn_sw3': 8.0}
    for name, (base, spread) in spreads.items():
        noise = np.random.default_rng([zlib.crc32(name.encode()), seed]).standard_normal(out[name].shape)
        drawn = base * np.exp(spread * noise) if base else spread * noise
        out[name] = jnp.asarray(drawn.astype(out[name].dtype))
    for name, factor in factors.items():
        out[name] = (out[name] * factor).astype(out[name].dtype)
    return out
```

```python
from contextlib import ExitStack

import numpy as np

import concourse.bass as bass
from concourse import mybir

ACT = mybir.ActivationFunctionType
ALU = mybir.AluOpType
F32 = mybir.dt.float32
BF16 = mybir.dt.bfloat16
I32 = mybir.dt.int32
AX = mybir.AxisListType

P = 128
S = 2048
T = S // P
G = 4
NB = 512
XO = 4
EPS = 1e-5
STAGES = 8

NH, DH, DR, DL = 16, 8, 4, 32
DQK = DH + DR
HR = NH * DR
CP = NH * DQK // 2
CLIP = 80.0
NE, FH, M = 8, 64, 256
CD, CE = 64, 65
NX, GI = 9, 256
COMBOS = [(0, 0), (0, 1), (1, 0), (0, 2), (2, 0), (1, 1)]


class Arena:

    def __init__(self, tensor, words):
        self.tensor, self.words, self.at = tensor, words, 0

    def reset(self):
        self.at = 0

    def take(self, *shape, dtype=F32):
        n = int(np.prod(shape))
        words = n if dtype is not BF16 else n // 2
        view = self.tensor[:, self.at:self.at + words]
        self.at += words
        assert self.at <= self.words, (self.at, self.words)
        if dtype is not F32:
            view = view.bitcast(dtype)
        if len(shape) > 1:
            names = "abcde"[:len(shape)]
            view = view.rearrange(f"p ({' '.join(names)}) -> p {' '.join(names)}",
                                  **{c: n for c, n in zip(names, shape)})
        return view


def program(nc, I, out):
    ctx = ExitStack()
    with ctx:
        def sb(name, shape, dt=F32):
            return ctx.enter_context(nc.sbuf_tensor(name, shape, dt))

        def sem(name):
            return ctx.enter_context(nc.semaphore(name))

        pair = [ctx.enter_context(nc.psum_tensor(f"pair{i}", [P, 2, NB], F32)) for i in range(4)]
        bank = [pair[i // 2][:, i % 2, :] for i in range(8)]

        x = sb("x", [P, T, P])
        xn = sb("xn", [P, T, P])
        xnT = sb("xnT", [P, XO + S])
        ident = sb("ident", [P, P])
        stats = sb("stats", [P, T, 6])
        mv = sb("mv", [P, T, 2])
        ve = sb("ve", [P, T])
        rstd = sb("rstd", [P, T])
        mhalf = sb("mhalf", [P, 64])
        ARENA = 46500
        arena = Arena(sb("arena", [P, ARENA]), ARENA)

        x_in = [sem(f"x_in{g}") for g in range(G)]
        x_ready = sem("x_ready")
        ident_done = sem("ident_done")
        ln_stats = sem("ln_stats")
        ln_moments = sem("ln_moments")
        ln_ve = sem("ln_ve")
        ln_rstd = sem("ln_rstd")
        ln_xn = sem("ln_xn")
        ln_turned = sem("ln_turned")
        ln_xnT = sem("ln_xnT")
        stored = sem("stored")

        def xcol(g):
            return slice(XO + NB * g, XO + NB * (g + 1))

        def xtile(t):
            return slice(XO + P * t, XO + P * (t + 1))

        def ln_vector(dve, k):
            def normalise(g):
                dve.wait_ge(ln_rstd, 4 * k + g + 1)
                if g == 0 and k:
                    dve.wait_ge(x_ready, 4 * k)
                for t in range(4 * g, 4 * g + 4):
                    ins = dve.tensor_scalar(xn[:, t, :], x[:, t, :], mv[:, t, 0:1], rstd[:, t:t + 1],
                                            ALU.subtract, ALU.mult)
                ins.then_inc(ln_xn, 1)

            for g in range(G):
                if k == 0:
                    dve.wait_ge(x_in[g], 16)
                else:
                    dve.wait_ge(x_ready, 4 * (k - 1) + g + 1)
                for t in range(4 * g, 4 * g + 4):
                    ins = dve.bn_stats(stats[:, t, :], x[:, t, :])
                ins.then_inc(ln_stats, 1)
                dve.wait_ge(ln_stats, 4 * k + g + 1)
                for t in range(4 * g, 4 * g + 4):
                    ins = dve.bn_aggr(mv[:, t, :], stats[:, t, :])
                ins.then_inc(ln_moments, 1)
                if g:
                    normalise(g - 1)
            normalise(G - 1)

        def ln_gpsimd(pool, k):
            for g in range(G):
                pool.wait_ge(ln_moments, 4 * k + g + 1)
                pool.tensor_scalar(ve[:, 4 * g:4 * g + 4], mv[:, 4 * g:4 * g + 4, 1], EPS, None,
                                   ALU.add).then_inc(ln_ve, 1)
                pool.wait_ge(ln_ve, 4 * k + g + 1)
                pool.tensor_tensor(rstd[:, 4 * g:4 * g + 4], ve[:, 4 * g:4 * g + 4], mhalf[:, 0:4],
                                   ALU.pow).then_inc(ln_rstd, 1)

        def ln_tensor(pe, k):
            for g in range(G):
                pe.wait_ge(ln_xn, 4 * k + g + 1)
                if 4 * k + g >= 2:
                    pe.wait_ge(ln_xnT, 4 * k + g - 1)
                for i in range(4):
                    ins = pe.transpose(bank[6 + g % 2][:, P * i:P * (i + 1)], xn[:, 4 * g + i, :], ident[:, :])
                ins.then_inc(ln_turned, 1)

        def ln_scalar(act, k):
            for g in range(G):
                act.wait_ge(ln_turned, 4 * k + g + 1)
                act.activation(xnT[:, xcol(g)], bank[6 + g % 2][:, :], ACT.Copy).then_inc(ln_xnT, 1)

        arena.reset()
        vpad = arena.take(T, NH, 32)
        stack = [[arena.take(4, S, dtype=BF16) for _ in range(2)] for _ in range(2)]
        arena.at -= 2 * 2 * S
        parts = arena.take(2, 3, S, dtype=BF16)
        arena.at += 2 * 2 * S - 3 * S
        pring = arena.take(6, 2, NB)
        arena.at -= 6 * 2 * NB
        cosT, sinT, zq = arena.take(S), arena.take(S), arena.take(S)
        resid = arena.take(2, NB)
        rope1, rope2 = arena.take(2, NB), arena.take(2, NB)
        oT = arena.take(2, NB)
        attn = arena.take(T, P)
        attnT = rope1
        m_wab = arena.take(2, P)
        m_wq = arena.take(2 * CP)
        m_wkc, m_wkr = arena.take(2 * CP), arena.take(2 * CP)
        m_wv = arena.take(P)
        m_wo = arena.take(P)
        m_dqT = arena.take(P)
        m_dkvT = arena.take(P)
        m_qr2 = arena.take(2 * HR)
        m_uk = arena.take(2 * CP)
        m_uv = arena.take(P)
        rdenA = arena.take(16)
        scratch = nc.dram_tensor("split_parts", [2, 2, 3, CP, S], BF16, kind="Internal").ap()

        a_zero = sem("a_zero")
        a_vzero = sem("a_vzero")
        a_w = sem("a_w")
        a_w2 = sem("a_w2")
        a_fold = sem("a_fold")
        a_folded = sem("a_folded")
        a_ab = sem("a_ab")
        a_rope = sem("a_rope")
        a_cq = sem("a_cq")
        a_z = sem("a_z")
        a_v = sem("a_v")
        a_vcopied = sem("a_vcopied")
        a_qk = sem("a_qk")
        a_hi = sem("a_hi")
        a_res = sem("a_res")
        a_mid = sem("a_mid")
        a_lo = sem("a_lo")
        a_parts = [sem(f"a_parts{i}") for i in range(4)]
        a_stack = [sem(f"a_stack{i}") for i in range(2)]
        a_scores = sem("a_scores")
        a_exp = sem("a_exp")
        a_clip = sem("a_clip")
        a_mask = sem("a_mask")
        a_pv = sem("a_pv")
        a_oT = sem("a_oT")
        a_turned = sem("a_turned")
        a_rden = sem("a_rden")
        a_norm = sem("a_norm")
        a_at = sem("a_at")
        a_atc = sem("a_atc")
        a_wo = sem("a_wo")

        UNITS = [(g, qb, kt) for g in range(4) for qb in range(G) for kt in range(4 * qb + 4)]
        BLOCKS = [(g, qb) for g in range(4) for qb in range(G)]
        first_col = lambda qb, kt: max(0, kt * P - qb * NB)
        last_unit = {}
        for n, (g, qb, kt) in enumerate(UNITS):
            last_unit[(g, qb)] = n
        masked = [kt >= 4 * qb for _, qb, kt in UNITS]
        masks_to = [2 * sum(masked[:n + 1]) for n in range(len(UNITS))]
        QK = [(a, side, b) for a in range(2) for side in range(2) for b in range(G)]

        def mla_load(sp):
            sp.dma_start(m_dqT[0:DL, :], I["WDQT"]).then_inc(a_w, 16)
            sp.dma_start(m_dkvT[0:DL, :], I["WDKVT"]).then_inc(a_w, 16)
            sp.dma_start(m_qr2[0:DL, :], I["WQR2"]).then_inc(a_w, 16)
            sp.dma_start(m_uk[0:DL, :], I["WUKc"]).then_inc(a_w, 16)
            sp.dma_start(m_uv[0:DL, :], I["WUV"]).then_inc(a_w, 16)
            sp.dma_start(m_wab[:, :, HR:P], I["WABr"].rearrange("a p n -> p a n")).then_inc(a_w2, 16)
            sp.dma_start(m_wq, I["WQc"]).then_inc(a_w2, 16)
            sp.dma_start(m_wkr, I["WKsel"]).then_inc(a_w2, 16)
            sp.dma_start(m_wo, I["WO"]).then_inc(a_w2, 16)
            sp.dma_start(cosT[0:96, :], I["cosT"]).then_inc(a_w2, 16)
            sp.dma_start(sinT[0:96, :], I["sinT"]).then_inc(a_w2, 16)

        def mla_sync(sp):
            for n in range(4):
                a, side = divmod(n, 2)
                sp.wait_ge(a_lo, 4 * (n + 1))
                sp.dma_start(scratch[side, a].rearrange("c p n -> p c n"),
                             parts[0:CP, n % 2]).then_inc(a_parts[n], 16)
            for g in range(4):
                sp.wait_ge(a_parts[2 * (g // 2)], 16)
                sp.wait_ge(a_parts[2 * (g // 2) + 1], 16)
                if g < 2:
                    sp.wait_ge(a_zero, g + 1)
                if g >= 2:
                    sp.wait_ge(a_pv, last_unit[(g - 2, G - 1)] + 1)
                for side in range(2):
                    for c, combo in enumerate(COMBOS):
                        src = scratch[side, g // 2, combo[side], (g % 2) * 48:(g % 2) * 48 + 48, :]
                        sp.dma_start(stack[g % 2][side][c * DQK:(c + 1) * DQK],
                                     src.rearrange("(h d) n -> d h n", h=4)).then_inc(a_stack[g % 2], 16)

        def mla_gpsimd(pool):
            for b in range(G):
                pool.wait_ge(a_rope, b + 1)
                pool.tensor_tensor(zq[0:96, NB * b:NB * (b + 1)], rope1[0:96, b % 2], rope2[0:96, b % 2],
                                   ALU.add).then_inc(a_z, 1)
            for n in range(len(QK)):
                a, side, b = QK[n]
                pool.wait_ge(a_mid, n + 1)
                pool.tensor_tensor(parts[0:CP, (n // 4) % 2, 2, NB * b:NB * (b + 1)], resid[0:CP, n % 2],
                                   parts[0:CP, (n // 4) % 2, 1, NB * b:NB * (b + 1)],
                                   ALU.subtract).then_inc(a_lo, 1)
            for n in range(4):
                pool.wait_ge(a_parts[n], 16)
            pool.memset(stack[1][0].bitcast(F32), 0.0)
            pool.memset(stack[1][1].bitcast(F32), 0.0).then_inc(a_zero, 1)
            for n, (g, qb, kt) in enumerate(UNITS):
                if masked[n]:
                    c = first_col(qb, kt)
                    for h in range(2):
                        r = (2 * n + h) % 6
                        pool.wait_ge(a_clip, 2 * n + h + 1)
                        pool.affine_select(out=pring[:, r, :, c:c + P], in_=pring[:, r, :, c:c + P],
                                           compare_op=ALU.is_ge, fill=0.0, base=0,
                                           pattern=[[0, 2], [1, P]], channel_multiplier=-1).then_inc(a_mask, 1)

        def mla_scalar(act):
            act.wait_ge(a_fold, 3)
            act.wait_ge(a_w2, 96)
            act.activation(m_wab[:, :, 0:HR], bank[0][:, 0:2 * HR].rearrange("p (a n) -> p a n", a=2),
                           ACT.Copy).then_inc(a_folded, 1)
            act.activation(m_wkc, bank[1][:, 0:2 * CP], ACT.Copy).then_inc(a_folded, 1)
            act.activation(m_wv, bank[2][:, 0:P], ACT.Copy).then_inc(a_folded, 1)
            for b in range(G):
                act.wait_ge(a_ab, b + 1)
                act.activation(zq[96:P, NB * b:NB * (b + 1)], bank[2 * (b % 2)][96:P, :], ACT.Copy).then_inc(a_cq, 1)
            for g in range(G):
                act.wait_ge(a_v, g + 1)
                if g == 0:
                    act.wait_ge(a_vzero, 2)
                act.activation(vpad[:, 4 * g:4 * g + 4, :, 0:DH],
                               bank[4 + g % 2][:, :].rearrange("p (t h d) -> p t h d", t=4, h=NH),
                               ACT.Copy).then_inc(a_vcopied, 1)
            for n in range(len(QK)):
                a, side, b = QK[n]
                half = n // 4
                act.wait_ge(a_qk, n + 1)
                if n >= 8 and n % 4 == 0:
                    act.wait_ge(a_parts[half - 2], 16)
                act.activation(parts[0:CP, half % 2, 0, NB * b:NB * (b + 1)], bank[n % 4][0:CP, :],
                               ACT.Copy).then_inc(a_hi, 1)
                act.wait_ge(a_res, n + 1)
                act.activation(parts[0:CP, half % 2, 1, NB * b:NB * (b + 1)], resid[0:CP, n % 2],
                               ACT.Copy).then_inc(a_mid, 1)
            for n, (g, qb, kt) in enumerate(UNITS):
                c = first_col(qb, kt)
                for h in range(2):
                    m = 2 * n + h
                    act.wait_ge(a_scores, m + 1)
                    if m >= 6:
                        act.wait_ge(a_pv, (m - 6) // 2 + 1)
                    act.activation(pring[:, m % 6, :, c:NB], pair[m % 3][:, :, c:NB], ACT.Exp,
                                   scale=float(1.0 / np.sqrt(np.float32(DQK)))).then_inc(a_exp, 1)
            for g in range(G):
                act.wait_ge(a_at, g + 1)
                act.activation(oT[:, g % 2], bank[6 + g % 2][:, :], ACT.Copy).then_inc(a_atc, 1)

        def mla_vector(dve):
            dve.wait_ge(a_w2, 96)
            for b in range(G):
                dve.wait_ge(a_ab, b + 1)
                if b >= 2:
                    dve.wait_ge(a_z, b - 1)
                dve.tensor_tensor(rope1[0:96, b % 2], bank[2 * (b % 2)][0:96, :], cosT[0:96, NB * b:NB * (b + 1)],
                                  ALU.mult)
                dve.tensor_tensor(rope2[0:96, b % 2], bank[2 * (b % 2) + 1][0:96, :],
                                  sinT[0:96, NB * b:NB * (b + 1)], ALU.mult).then_inc(a_rope, 1)
            for n in range(len(QK)):
                a, side, b = QK[n]
                dve.wait_ge(a_hi, n + 1)
                if n >= 2:
                    dve.wait_ge(a_lo, n - 1)
                dve.tensor_tensor(resid[0:CP, n % 2], bank[n % 4][0:CP, :],
                                  parts[0:CP, (n // 4) % 2, 0, NB * b:NB * (b + 1)], ALU.subtract).then_inc(a_res, 1)
            top = float(np.exp(np.float32(CLIP) / np.sqrt(np.float32(DQK))))

            def out_block(j):
                dve.wait_ge(a_pv, last_unit[BLOCKS[j]] + 1)
                if j >= 2:
                    dve.wait_ge(a_turned, j - 1)
                dve.tensor_copy(oT[:, j % 2], bank[6 + j % 2][:, :]).then_inc(a_oT, 1)

            def norm_block(j):
                g, qb = BLOCKS[j]
                o = bank[6 + j % 2][:, :].rearrange("p (i h d) -> p i h d", i=4, h=4)
                dve.wait_ge(a_turned, j + 1)
                dve.reciprocal(rdenA[:, :].rearrange("p (i h) -> p i h", i=4), o[:, :, :, DH]).then_inc(a_rden, 1)
                dve.wait_ge(a_rden, j + 1)
                for i in range(4):
                    ins = dve.tensor_tensor(
                        attn[:, 4 * qb + i, 32 * g:32 * g + 32].rearrange("p (h d) -> p h d", h=4), o[:, i, :, 0:DH],
                        rdenA[:, 4 * i:4 * i + 4].unsqueeze(2).broadcast_to([P, 4, DH]), ALU.mult)
                ins.then_inc(a_norm, 1)

            done = {last_unit[b]: j for j, b in enumerate(BLOCKS)}
            for n, (g, qb, kt) in enumerate(UNITS):
                c = first_col(qb, kt)
                for h in range(2):
                    m = 2 * n + h
                    dve.wait_ge(a_exp, m + 1)
                    dve.tensor_scalar(pring[:, m % 6, :, c:NB], pring[:, m % 6, :, c:NB], 1.0 / top, top,
                                      ALU.max, ALU.min).then_inc(a_clip, 1)
                if n - 2 in done:
                    out_block(done[n - 2])
                if n - 4 in done:
                    norm_block(done[n - 4])
            out_block(len(BLOCKS) - 1)
            norm_block(len(BLOCKS) - 1)
            for g in range(G):
                dve.wait_ge(a_wo, g + 1)
                dve.tensor_tensor(x[:, 4 * g:4 * g + 4, :], bank[g][:, :].rearrange("p (t n) -> p t n", t=4),
                                  x[:, 4 * g:4 * g + 4, :], ALU.add).then_inc(x_ready, 1)

        def mla_tensor(pe):
            pe.wait_ge(a_w, 80)
            pe.matmul(bank[0][:, 0:2 * HR], m_dqT[0:DL, :], m_qr2[0:DL, :]).then_inc(a_fold, 1)
            pe.matmul(bank[1][:, 0:2 * CP], m_dkvT[0:DL, :], m_uk[0:DL, :]).then_inc(a_fold, 1)
            pe.matmul(bank[2][:, 0:P], m_dkvT[0:DL, :], m_uv[0:DL, :]).then_inc(a_fold, 1)
            pe.wait_ge(a_folded, 3)
            for b in range(G):
                pe.wait_ge(ln_xnT, b + 1)
                if b >= 2:
                    pe.wait_ge(a_rope, b - 1)
                    pe.wait_ge(a_cq, b - 1)
                pe.matmul(bank[2 * (b % 2)][:, :], m_wab[:, 0, :], xnT[:, xcol(b)])
                pe.matmul(bank[2 * (b % 2) + 1][:, :], m_wab[:, 1, :], xnT[:, xcol(b)]).then_inc(a_ab, 1)
            for g in range(G):
                if g >= 2:
                    pe.wait_ge(a_vcopied, g - 1)
                for i in range(4):
                    ins = pe.matmul(bank[4 + g % 2][:, P * i:P * (i + 1)], xnT[:, xtile(4 * g + i)], m_wv)
                ins.then_inc(a_v, 1)
            for n in range(len(QK)):
                a, side, b = QK[n]
                if n < 4:
                    pe.wait_ge(a_z, b + 1)
                    pe.wait_ge(a_cq, b + 1)
                if n == 0:
                    pe.wait_ge(a_rope, G)
                    pe.wait_ge(a_cq, G)
                if n >= 4:
                    pe.wait_ge(a_res, n - 3)
                cols = slice(CP * a, CP * (a + 1))
                if side == 0:
                    pe.matmul(bank[n % 4][0:CP, :], m_wq[:, cols], zq[:, NB * b:NB * (b + 1)]).then_inc(a_qk, 1)
                else:
                    pe.matmul(bank[n % 4][0:CP, :], m_wkc[:, cols], xnT[:, xcol(b)], start=True, stop=False)
                    pe.matmul(bank[n % 4][0:CP, :], m_wkr[:, cols], zq[:, NB * b:NB * (b + 1)],
                              start=False, stop=True).then_inc(a_qk, 1)

            def scores(n):
                g, qb, kt = UNITS[n]
                c = first_col(qb, kt)
                if kt == 0 and qb == 0:
                    pe.wait_ge(a_stack[g % 2], 192 * (g // 2 + 1))
                for h in range(2):
                    m = 2 * n + h
                    if m >= 3:
                        pe.wait_ge(a_exp, m - 2)
                    for i in range(2):
                        head = 2 * h + i
                        ins = pe.matmul(pair[m % 3][:, i, c:NB], stack[g % 2][1][:, head, P * kt:P * (kt + 1)],
                                        stack[g % 2][0][:, head, NB * qb + c:NB * (qb + 1)])
                    ins.then_inc(a_scores, 1)

            def values(n):
                g, qb, kt = UNITS[n]
                c = first_col(qb, kt)
                j = BLOCKS.index((g, qb))
                if kt == 0 and j >= 2:
                    pe.wait_ge(a_norm, j - 1)
                pe.wait_ge(a_clip, 2 * n + 2)
                if masked[n]:
                    pe.wait_ge(a_mask, masks_to[n])
                for head in range(4):
                    m = 2 * n + head // 2
                    ins = pe.matmul(bank[6 + j % 2][32 * head:32 * head + 32, c:NB], vpad[:, kt, 4 * g + head, :],
                                    pring[:, m % 6, head % 2, c:NB], start=(kt == 0), stop=(kt == 4 * qb + 3),
                                    tile_position=(0, 32 * head))
                ins.then_inc(a_pv, 1)

            def turn(j):
                pe.wait_ge(a_oT, j + 1)
                for i in range(4):
                    ins = pe.transpose(bank[6 + j % 2][:, P * i:P * (i + 1)], oT[:, j % 2, P * i:P * (i + 1)], ident[:, :])
                ins.then_inc(a_turned, 1)

            done = {last_unit[b]: j for j, b in enumerate(BLOCKS)}
            pe.wait_ge(a_res, len(QK))
            pe.wait_ge(a_vcopied, G)
            for n in range(len(UNITS)):
                scores(n)
                if n:
                    values(n - 1)
                if n - 4 in done:
                    turn(done[n - 4])
            values(len(UNITS) - 1)
            turn(len(BLOCKS) - 1)
            pe.wait_ge(a_norm, len(BLOCKS))
            for g in range(G):
                if g >= 2:
                    pe.wait_ge(a_atc, g - 1)
                for i in range(4):
                    ins = pe.transpose(bank[6 + g % 2][:, P * i:P * (i + 1)], attn[:, 4 * g + i, :], ident[:, :])
                ins.then_inc(a_at, 1)
                pe.wait_ge(a_atc, g + 1)
                for i in range(4):
                    ins = pe.matmul(bank[g][:, P * i:P * (i + 1)], oT[:, g % 2, P * i:P * (i + 1)], m_wo)
                ins.then_inc(a_wo, 1)


        a_words = arena.at

        f_w12 = arena.take(2, NE + 1, FH)
        f_b12 = arena.take(2, NE + 1, FH)
        f_w3raw = arena.take(5, P)
        f_w3 = arena.take(5, P)
        f_bsel = arena.take(5, NE + 1)
        f_gcol = arena.take(5)
        f_wg = arena.take(NE + 1)
        f_bg = arena.take(NE + 1)
        f_bx = arena.take(NE)
        f_pref = arena.take(NE)
        f_idx = arena.take(2, M + 2, dtype=I32)
        f_notin = arena.take(T)
        f_rcnt = arena.take(2)
        f_scol = arena.take(T)
        later_words = arena.at
        arena.reset()
        f_gt = arena.take(T, M)
        f_gm = arena.take(2, S)
        keep_words = arena.at
        f_i1, f_i2, f_i3 = arena.take(2, M + 2), arena.take(M + 2), arena.take(M + 2)
        f_row = arena.take(M + 2)
        f_srow = arena.take(S)
        f_srowi = arena.take(S, dtype=I32)
        f_scoli = arena.take(T, dtype=I32)
        arena.at = keep_words
        f_hb = arena.take(T, 2, FH)
        f_sg = arena.take(T, FH)
        f_u = arena.take(T, FH)
        f_st = arena.take(T, 6)
        f_mv = arena.take(T, 2)
        f_rs = arena.take(T)
        f_rv = arena.take(T)
        f_sh = arena.take(T, FH + 1)
        f_shT = arena.take(S)
        f_xm = arena.take(M)
        f_sc = arena.take(24, 2, NE + 1)
        f_hm = arena.take(2, 2, NE + 1, FH)
        f_sm = arena.take(2, NE + 1, FH)
        f_um = arena.take(2, NE + 1, FH)
        f_stm = arena.take(2 * (NE + 1), 6)
        f_mvm = arena.take(2 * (NE + 1), 2)
        f_rsm = arena.take(2, NE + 1)
        f_z = arena.take(2, (NE + 1) * FH + NE + 1)
        f_zT = arena.take(5, M)
        f_moe = arena.take(2, P)

        f_w = sem("f_w")
        f_c = sem("f_c")
        f_pc = sem("f_pc")
        f_iota = sem("f_iota")
        f_prep = sem("f_prep")
        f_fold = sem("f_fold")
        f_hs = sem("f_hs")
        f_hsb = sem("f_hsb")
        f_silu = sem("f_silu")
        f_stat = sem("f_stat")
        f_rstd = sem("f_rstd")
        f_shn = sem("f_shn")
        f_sturn = sem("f_sturn")
        f_sT = sem("f_sT")
        f_gath = sem("f_gath")
        f_xmc = sem("f_xmc")
        f_gate = sem("f_gate")
        f_lg = sem("f_lg")
        f_ex = sem("f_ex")
        f_hid = sem("f_hid")
        f_hmb = sem("f_hmb")
        f_zd = sem("f_zd")
        f_zturn = sem("f_zturn")
        f_zc = sem("f_zc")
        f_mo = sem("f_mo")
        f_moc = sem("f_moc")
        f_out = sem("f_out")
        count = {"f_c": 0, "f_pc": 0, "f_ex": 0, "f_lg": 0}

        def link(eng, s, name, ins):
            count[name] += 1
            ins.then_inc(s, 1)
            eng.wait_ge(s, count[name])

        def ffn_load(sp):
            bc = lambda ap: ap.partition_broadcast(P)
            sp.dma_start(f_w12, I["F_w12"]).then_inc(f_w, 16)
            sp.dma_start(f_b12.rearrange("p a e h -> p (a e h)"), bc(I["F_b12"])).then_inc(f_w, 16)
            sp.dma_start(f_w3raw, I["F_w3"]).then_inc(f_w, 16)
            sp.dma_start(f_bsel, I["F_bsel"]).then_inc(f_w, 16)
            sp.dma_start(f_gcol, I["F_gcol"]).then_inc(f_w, 16)
            sp.dma_start(f_wg, I["F_wg"]).then_inc(f_w, 16)
            sp.dma_start(f_bg, bc(I["F_bg"])).then_inc(f_w, 16)
            sp.dma_start(f_bx, bc(I["F_bx"])).then_inc(f_w, 16)
            sp.dma_start(f_pref, bc(I["F_pref"])).then_inc(f_w, 16)
            for i, name in enumerate(("F_ib", "F_it")):
                sp.dma_start(f_idx[:, i, 0:M], bc(I[name])).then_inc(f_w, 16)
                sp.dma_start(f_idx[:, i, M:M + 2], I[name + "c"]).then_inc(f_w, 16)

        def ffn_prepare_gpsimd(pool):
            pool.wait_ge(x_ready, 4)
            pool.iota(f_srowi, [[1, S]], base=0, channel_multiplier=0)
            pool.iota(f_scoli, [[P, T]], base=0, channel_multiplier=1).then_inc(f_iota, 1)

        def ffn_prepare_vector(dve):
            c = lambda ins: link(dve, f_c, "f_c", ins)
            dve.wait_ge(f_w, 13 * 16)
            dve.wait_ge(f_iota, 1)
            dve.tensor_copy(f_srow, f_srowi)
            dve.tensor_copy(f_scol, f_scoli)
            c(dve.tensor_copy(f_i1, f_idx))
            dve.tensor_scalar(f_i2, f_i1[:, 1], 0.0, float(S), ALU.is_lt, ALU.mult)
            dve.tensor_scalar(f_i3, f_i1[:, 0], 0.0, None, ALU.is_equal)
            c(dve.tensor_scalar(f_row, f_i1[:, 0], -1.0, None, ALU.is_equal))
            c(dve.tensor_tensor(f_i3, f_i3, f_row, ALU.add))
            c(dve.scalar_tensor_tensor(f_i2, f_i2, 1.0, f_i1[:, 1], ALU.add, ALU.add))
            c(dve.tensor_tensor(f_i2, f_i2, f_i3, ALU.mult))
            c(dve.tensor_scalar(f_row, f_i2, -1.0, None, ALU.add))
            for t in range(T):
                dve.tensor_scalar(f_gt[:, t, :], f_row[:, 0:M], f_scol[:, t:t + 1], None, ALU.is_equal)
            for m in range(2):
                dve.tensor_scalar(f_gm[:, m, :], f_srow, f_row[:, M + m:M + m + 1], None, ALU.is_equal)
            for m in range(2):
                c(dve.tensor_scalar(f_i2[:, 0:M], f_row[:, 0:M], f_row[:, M + m:M + m + 1], None,
                                    ALU.is_equal))
                c(dve.tensor_reduce(f_i3[:, m:m + 1], f_i2[:, 0:M], AX.X, ALU.add))
            c(dve.reciprocal(f_rcnt, f_i3[:, 0:2]))
            c(dve.tensor_reduce(f_notin, f_gt, AX.X, ALU.max))
            c(dve.tensor_scalar(f_notin, f_notin, -1.0, 1.0, ALU.mult, ALU.add))
            for kt in range(5):
                ins = dve.tensor_scalar(f_w3[:, kt, :], f_w3raw[:, kt, :], f_gcol[:, kt:kt + 1], None, ALU.mult)
            c(ins)
            dve.wait_ge(f_fold, 1)
            dve.tensor_tensor(f_w3[64:64 + NE + 1, 4, :], bank[5][64:64 + NE + 1, 0:P],
                              f_w3raw[64:64 + NE + 1, 4, :], ALU.add).then_inc(f_prep, 1)

        def ffn_gpsimd(pool, rep):
            k = 2 * rep + 1
            if rep == 0:
                ffn_prepare_gpsimd(pool)
            c = lambda ins: link(pool, f_pc, "f_pc", ins)
            pool.wait_ge(f_stat, 2 * rep + 1)
            c(pool.tensor_scalar(f_rv, f_mv[:, :, 1], EPS, None, ALU.add))
            c(pool.tensor_tensor(f_rs, f_rv, mhalf[:, 0:T], ALU.pow))
            pool.tensor_tensor(f_rs, f_rs, f_notin, ALU.mult).then_inc(f_rstd, 1)
            pool.wait_ge(f_stat, 2 * rep + 2)
            mvm = f_mvm[:, :, 1]
            flat = f_rsm.rearrange("p m e -> p (m e)")
            c(pool.tensor_scalar(flat, mvm, EPS, None, ALU.add))
            c(pool.tensor_tensor(flat, flat, mhalf[:, 0:2 * (NE + 1)], ALU.pow))
            pool.tensor_tensor(f_rsm, f_rsm, f_sc[:, FAC], ALU.mult).then_inc(f_rstd, 1)

        def ffn_scalar(act, rep):
            act.wait_ge(f_gath, rep + 1)
            act.activation(f_xm, bank[4][:, 0:M], ACT.Copy).then_inc(f_xmc, 1)
            act.wait_ge(f_lg, 2 * rep + 1)
            act.activation(f_sc[:, 1], f_sc[:, 0], ACT.Exp, scale=-1.0).then_inc(f_ex, 1)
            act.wait_ge(f_lg, 2 * rep + 2)
            act.activation(f_sc[:, 12, :, 0:2], f_sc[:, 11, :, 0:2], ACT.Exp).then_inc(f_ex, 1)
            for g in range(G):
                act.wait_ge(f_hsb, 4 * rep + g + 1)
                act.activation(f_sg[:, 4 * g:4 * g + 4, :], f_hb[:, 4 * g:4 * g + 4, 0, :], ACT.Silu
                               ).then_inc(f_silu, 1)
            for m in range(2):
                act.wait_ge(f_hmb, 2 * rep + m + 1)
                act.activation(f_sm[:, m], f_hm[:, m, 0], ACT.Silu).then_inc(f_silu, 1)
            for g in range(G):
                act.wait_ge(f_sturn, 4 * rep + g + 1)
                act.activation(f_shT[0:FH + 1, NB * g:NB * (g + 1)], bank[6 + g % 2][0:FH + 1, :], ACT.Copy
                               ).then_inc(f_sT, 1)
            act.wait_ge(f_zturn, rep + 1)
            for kt in range(4):
                act.activation(f_zT[:, kt, :], bank[kt // 2][:, M * (kt % 2):M * (kt % 2 + 1)], ACT.Copy)
            act.activation(f_zT[0:FH + NE + 1, 4, :], bank[4][0:FH + NE + 1, 0:M], ACT.Copy).then_inc(f_zc, 1)
            act.wait_ge(f_mo, rep + 1)
            act.activation(f_moe, bank[5][:, 0:2 * P].rearrange("p (m n) -> p m n", m=2), ACT.Copy
                           ).then_inc(f_moc, 1)

        LOG, SIG, BIA, FAC = 0, 3, 4, 20

        def ffn_vector(dve, rep):
            c = lambda ins: link(dve, f_c, "f_c", ins)
            if rep == 0:
                ffn_prepare_vector(dve)
            for g in range(G):
                dve.wait_ge(f_hs, 4 * rep + g + 1)
                dve.tensor_tensor(f_hb[:, 4 * g:4 * g + 4], bank[g][:, :].rearrange("p (t a h) -> p t a h", t=4, a=2),
                                  f_b12[:, :, NE, :].unsqueeze(1).broadcast_to([P, 4, 2, FH]), ALU.add
                                  ).then_inc(f_hsb, 1)
            sc = f_sc
            dve.wait_ge(f_gate, rep + 1)
            dve.tensor_tensor(sc[:, LOG], bank[5][:, 0:2 * (NE + 1)].rearrange("p (m e) -> p m e", m=2),
                              f_bg.unsqueeze(1).broadcast_to([P, 2, NE + 1]), ALU.add).then_inc(f_lg, 1)
            dve.wait_ge(f_ex, 2 * rep + 1)
            c(dve.tensor_scalar(sc[:, 2], sc[:, 1], 1.0, None, ALU.add))
            c(dve.reciprocal(sc[:, SIG], sc[:, 2]))
            c(dve.tensor_tensor(sc[:, BIA, :, 0:NE], sc[:, SIG, :, 0:NE], f_bx.unsqueeze(1).broadcast_to([P, 2, NE]), ALU.add))
            c(dve.tensor_reduce(sc[:, 5, :, 0], sc[:, BIA, :, 0:NE], AX.X, ALU.max))
            c(dve.tensor_tensor(sc[:, 6, :, 0:NE], sc[:, BIA, :, 0:NE], sc[:, 5, :, 0:1].broadcast_to([P, 2, NE]), ALU.is_equal))
            c(dve.tensor_tensor(sc[:, 7, :, 0:NE], sc[:, 6, :, 0:NE], f_pref.unsqueeze(1).broadcast_to([P, 2, NE]), ALU.mult))
            c(dve.tensor_reduce(sc[:, 8, :, 0], sc[:, 7, :, 0:NE], AX.X, ALU.max))
            c(dve.tensor_tensor(sc[:, 9, :, 0:NE], sc[:, 7, :, 0:NE], sc[:, 8, :, 0:1].broadcast_to([P, 2, NE]), ALU.is_equal))
            c(dve.tensor_tensor(sc[:, 10, :, 0:NE], sc[:, 9, :, 0:NE], sc[:, SIG, :, 0:NE], ALU.mult))
            dve.tensor_copy(sc[:, 11, :, 0:1], sc[:, SIG, :, NE:NE + 1])
            c(dve.tensor_reduce(sc[:, 11, :, 1], sc[:, 10, :, 0:NE], AX.X, ALU.add))
            dve.tensor_copy(sc[:, 13, :, 0:1], sc[:, 11, :, 0:1]).then_inc(f_lg, 1)
            dve.wait_ge(f_ex, 2 * rep + 2)
            c(dve.tensor_reduce(sc[:, 14, :, 0], sc[:, 12, :, 0:2], AX.X, ALU.add))
            c(dve.reciprocal(sc[:, 15, :, 0], sc[:, 14, :, 0]))
            c(dve.tensor_tensor(sc[:, 16, :, 0], sc[:, 15, :, 0], f_rcnt, ALU.mult))
            c(dve.tensor_tensor(sc[:, 17, :, 0:2], sc[:, 12, :, 0:2], sc[:, 16, :, 0:1].broadcast_to([P, 2, 2]), ALU.mult))
            dve.tensor_copy(sc[:, FAC, :, NE:NE + 1], sc[:, 17, :, 0:1])
            c(dve.tensor_tensor(sc[:, FAC, :, 0:NE], sc[:, 9, :, 0:NE], sc[:, 17, :, 1:2].broadcast_to([P, 2, NE]), ALU.mult))
            for m in range(2):
                for a in range(2):
                    dve.wait_ge(f_hid, 4 * rep + 2 * m + a + 1)
                    dve.tensor_tensor(f_hm[:, m, a, 0:NE, :], bank[2 * m + a][:, :].rearrange("p (e h) -> p e h", e=NE),
                                      f_b12[:, a, 0:NE, :], ALU.add)
                dve.tensor_tensor(f_hm[:, m, :, NE, :], bank[5][:, 256 + 128 * m:384 + 128 * m].rearrange("p (a h) -> p a h", a=2),
                                  f_b12[:, :, NE, :], ALU.add).then_inc(f_hmb, 1)
            for g in range(G):
                dve.wait_ge(f_silu, 6 * rep + g + 1)
                ins = dve.tensor_tensor(f_u[:, 4 * g:4 * g + 4, :], f_sg[:, 4 * g:4 * g + 4, :],
                                        f_hb[:, 4 * g:4 * g + 4, 1, :], ALU.mult)
            c(ins)
            for t in range(T):
                ins = dve.bn_stats(f_st[:, t, :], f_u[:, t, :])
            c(ins)
            for t in range(T):
                ins = dve.bn_aggr(f_mv[:, t, :], f_st[:, t, :])
            ins.then_inc(f_stat, 1)
            for m in range(2):
                dve.wait_ge(f_silu, 6 * rep + 4 + m + 1)
                ins = dve.tensor_tensor(f_um[:, m], f_sm[:, m], f_hm[:, m, 1], ALU.mult)
            c(ins)
            for n in range(2 * (NE + 1)):
                ins = dve.bn_stats(f_stm[:, n, :], f_um[:, n // (NE + 1), n % (NE + 1), :])
            c(ins)
            for n in range(2 * (NE + 1)):
                ins = dve.bn_aggr(f_mvm[:, n, :], f_stm[:, n, :])
            ins.then_inc(f_stat, 1)
            dve.wait_ge(f_rstd, 2 * rep + 1)
            dve.tensor_copy(f_sh[:, :, FH:FH + 1], f_notin.unsqueeze(2))
            for t in range(T):
                ins = dve.tensor_scalar(f_sh[:, t, 0:FH], f_u[:, t, :], f_mv[:, t, 0:1], f_rs[:, t:t + 1],
                                        ALU.subtract, ALU.mult)
                if t % 4 == 3:
                    ins.then_inc(f_shn, 1)
            dve.wait_ge(f_rstd, 2 * rep + 2)
            for m in range(2):
                for e in range(NE + 1):
                    n = m * (NE + 1) + e
                    dve.tensor_scalar(f_z[:, m, FH * e:FH * (e + 1)], f_um[:, m, e, :], f_mvm[:, n, 0:1],
                                      f_rsm[:, m, e:e + 1], ALU.subtract, ALU.mult)
                dve.tensor_copy(f_z[:, m, FH * (NE + 1):FH * (NE + 1) + 1], sc[:, FAC, m, NE:NE + 1])
                ins = dve.tensor_copy(f_z[:, m, FH * (NE + 1) + 1:], sc[:, FAC, m, 0:NE])
            ins.then_inc(f_zd, 1)
            for g in range(G):
                dve.wait_ge(f_out, 4 * rep + g + 1)
                dve.tensor_tensor(x[:, 4 * g:4 * g + 4, :], bank[g][:, :].rearrange("p (t n) -> p t n", t=4),
                                  x[:, 4 * g:4 * g + 4, :], ALU.add).then_inc(x_ready, 1)

        def ffn_tensor(pe, rep):
            k = 2 * rep + 1
            if rep == 0:
                pe.wait_ge(f_w, 13 * 16)
                for kt in range(5):
                    rows = P if kt < 4 else FH
                    ins = pe.matmul(bank[5][64:64 + NE + 1, 0:P], f_bsel[0:rows, kt, :], f_w3raw[0:rows, kt, :],
                                    start=(kt == 0), stop=(kt == 4), tile_position=(0, 64))
                ins.then_inc(f_fold, 1)
            for g in range(G):
                pe.wait_ge(ln_xnT, 4 * k + g + 1)
                for i in range(4):
                    ins = pe.matmul(bank[g][:, P * i:P * (i + 1)], xnT[:, xtile(4 * g + i)], f_w12[:, :, NE, :])
                ins.then_inc(f_hs, 1)
            if rep == 0:
                pe.wait_ge(f_prep, 1)
            for t in range(T):
                ins = pe.matmul(bank[4][:, 0:M], xn[:, t, :], f_gt[:, t, :], start=(t == 0), stop=(t == T - 1))
            ins.then_inc(f_gath, 1)
            pe.wait_ge(f_xmc, rep + 1)
            for m in range(2):
                pe.matmul(bank[5][:, (NE + 1) * m:(NE + 1) * (m + 1)], f_xm[:, P * m:P * (m + 1)], f_wg)
                ins = pe.matmul(bank[5][:, 256 + 128 * m:384 + 128 * m], f_xm[:, P * m:P * (m + 1)], f_w12[:, :, NE, :])
            ins.then_inc(f_gate, 1)
            for m in range(2):
                for a in range(2):
                    pe.wait_ge(f_hsb, 4 * rep + 2 * m + a + 1)
                    pe.matmul(bank[2 * m + a][:, :], f_xm[:, P * m:P * (m + 1)],
                              f_w12[:, a, 0:NE, :]).then_inc(f_hid, 1)
            for g in range(G):
                pe.wait_ge(f_shn, 4 * rep + g + 1)
                if g >= 2:
                    pe.wait_ge(f_sT, 4 * rep + g - 1)
                for i in range(4):
                    ins = pe.transpose(bank[6 + g % 2][0:FH + 1, P * i:P * (i + 1)], f_sh[:, 4 * g + i, :], ident[:, :])
                ins.then_inc(f_sturn, 1)
            pe.wait_ge(f_zd, rep + 1)
            for m in range(2):
                for kt in range(4):
                    pe.transpose(bank[kt // 2][:, M * (kt % 2) + P * m:M * (kt % 2) + P * (m + 1)],
                                 f_z[:, m, P * kt:P * (kt + 1)], ident[:, :])
                ins = pe.transpose(bank[4][0:FH + NE + 1, P * m:P * (m + 1)], f_z[:, m, 4 * P:], ident[:, :])
            ins.then_inc(f_zturn, 1)
            pe.wait_ge(f_zc, rep + 1)
            for m in range(2):
                for kt in range(5):
                    rows = P if kt < 4 else FH + NE + 1
                    ins = pe.matmul(bank[5][:, P * m:P * (m + 1)], f_zT[0:rows, kt, P * m:P * (m + 1)],
                                    f_w3[0:rows, kt, :], start=(kt == 0), stop=(kt == 4))
            ins.then_inc(f_mo, 1)
            pe.wait_ge(f_moc, rep + 1)
            for g in range(G):
                pe.wait_ge(f_sT, 4 * rep + g + 1)
                for i in range(4):
                    t = 4 * g + i
                    o = bank[g][:, P * i:P * (i + 1)]
                    pe.matmul(o, f_shT[0:FH + 1, P * t:P * (t + 1)], f_w3[0:FH + 1, 4, :], start=True, stop=False)
                    pe.matmul(o, f_gm[:, 0, P * t:P * (t + 1)], f_moe[:, 0, :], start=False, stop=False)
                    ins = pe.matmul(o, f_gm[:, 1, P * t:P * (t + 1)], f_moe[:, 1, :], start=False, stop=True)
                ins.then_inc(f_out, 1)


        arena.at = later_words
        b_ww, b_wr = arena.take(P), arena.take(P)
        b_in = arena.take(2)
        b_sm = arena.take(8)
        later_words2 = arena.at
        arena.at = keep_words
        b_expo = arena.take(2 * P + 2)
        b_expoi = arena.take(2 * P + 2, dtype=I32)
        b_pow = arena.take(2 * P + 2)
        b_wv = arena.take(P)
        b_v = arena.take(T, P)
        b_wtok = arena.take(T, P)
        b_sm2 = arena.take(T, P)
        b_xdec = arena.take(T, P)
        b_state = arena.take(T, P)

        b_w = sem("b_w")
        b_iota = sem("b_iota")
        b_c = sem("b_c")
        b_s = sem("b_s")
        b_powd = sem("b_powd")
        b_mask = sem("b_mask")
        b_fold = sem("b_fold")
        b_wvd = sem("b_wvd")
        b_vm = sem("b_vm")
        b_vc = sem("b_vc")
        b_wt = sem("b_wt")
        b_wtc = sem("b_wtc")
        b_scm = sem("b_scm")
        b_smd = sem("b_smd")
        b_um = sem("b_um")
        b_st = sem("b_st")
        b_xd = sem("b_xd")
        b_xz = sem("b_xz")
        b_out = sem("b_out")
        count["b_c"] = 0

        def shifted(t):
            return slice(XO - 1 + P * t, XO - 1 + P * (t + 1))

        def dla_load(sp):
            sp.dma_start(b_ww, I["B_ww"]).then_inc(b_w, 16)
            sp.dma_start(b_wr, I["B_wrT"]).then_inc(b_w, 16)
            sp.dma_start(b_in[:, 0:1], I["B_decay"].partition_broadcast(P)).then_inc(b_w, 16)
            sp.dma_start(b_in[:, 1:2], I["B_la"].partition_broadcast(P)).then_inc(b_w, 16)

        def dla_gpsimd(pool):
            pool.wait_ge(x_ready, 8)
            pool.iota(b_expoi[:, 0:P], [[1, P]], base=-1, channel_multiplier=-1)
            pool.iota(b_expoi[:, P:2 * P], [[1, P]], base=0, channel_multiplier=0)
            pool.iota(b_expoi[:, 2 * P:2 * P + 1], [[1, 1]], base=P - 1, channel_multiplier=-1)
            pool.iota(b_expoi[:, 2 * P + 1:2 * P + 2], [[1, 1]], base=P, channel_multiplier=0).then_inc(b_iota, 1)
            pool.wait_ge(b_powd, 1)
            pool.affine_select(out=b_pow[:, 0:P], in_=b_pow[:, 0:P], compare_op=ALU.is_ge, fill=0.0, base=-1,
                               pattern=[[1, P]], channel_multiplier=-1).then_inc(b_mask, 1)
            for g in range(G):
                pool.wait_ge(ln_xnT, 8 + g + 1)
                pool.tensor_tensor(b_xdec[:, 4 * g:4 * g + 4, :], xnT[:, xcol(g)].rearrange("p (t n) -> p t n", t=4),
                                   b_pow[:, P:2 * P].unsqueeze(1).broadcast_to([P, 4, P]), ALU.mult).then_inc(b_xd, 1)

        def dla_scalar(act):
            act.wait_ge(b_st, 1)
            act.activation(b_sm[:, 2:3], b_sm[:, 1:2], ACT.Exp, scale=-1.0).then_inc(b_s, 1)
            act.activation(b_sm[:, 6:7], b_in[:, 1:2], ACT.Exp).then_inc(b_s, 1)
            act.wait_ge(b_s, 2)
            act.activation(b_sm[:, 3:4], b_sm[:, 2:3], ACT.Ln, bias=1.0).then_inc(b_s, 1)
            act.wait_ge(b_st, 2)
            act.activation(b_pow, b_expo, ACT.Exp, scale=b_sm[:, 4:5]).then_inc(b_powd, 1)
            for g in range(G):
                act.wait_ge(b_vm, g + 1)
                act.activation(b_v[:, 4 * g:4 * g + 4, :], bank[g][:, :].rearrange("p (t n) -> p t n", t=4), ACT.Copy
                               ).then_inc(b_vc, 1)

        def dla_vector(dve):
            c = lambda ins: link(dve, b_c, "b_c", ins)
            dve.wait_ge(b_w, 64)
            c(dve.tensor_scalar(b_sm[:, 0:1], b_in[:, 0:1], -1.0, None, ALU.mult))
            dve.tensor_tensor(b_sm[:, 1:2], b_sm[:, 0:1], b_in[:, 0:1], ALU.max).then_inc(b_st, 1)
            dve.wait_ge(b_iota, 1)
            c(dve.tensor_scalar(b_expo, b_expoi, 0.0, None, ALU.max))
            dve.wait_ge(b_s, 3)
            dve.scalar_tensor_tensor(b_sm[:, 4:5], b_in[:, 0:1], 0.0, b_sm[:, 3:4], ALU.min, ALU.subtract
                                     ).then_inc(b_st, 1)
            dve.wait_ge(b_fold, 1)
            dve.tensor_scalar(b_wv, bank[0][:, 0:P], b_sm[:, 6:7], None, ALU.mult).then_inc(b_wvd, 1)
            dve.memset(b_state[:, 0, :], 0.0)
            dve.wait_ge(b_powd, 1)
            for g in range(G):
                dve.wait_ge(b_wt, g + 1)
                dve.tensor_scalar(b_wtok[:, 4 * g:4 * g + 4, :], bank[4 + g % 2][:, :].rearrange("p (t n) -> p t n", t=4),
                                  b_pow[:, 2 * P:2 * P + 1], None, ALU.mult).then_inc(b_wtc, 1)
            dve.wait_ge(b_mask, 1)
            for g in range(G):
                dve.wait_ge(b_scm, g + 1)
                dve.tensor_tensor(b_sm2[:, 4 * g:4 * g + 4, :], bank[g][:, :].rearrange("p (t n) -> p t n", t=4),
                                  b_pow[:, 0:P].unsqueeze(1).broadcast_to([P, 4, P]), ALU.mult).then_inc(b_smd, 1)
            for t in range(T - 1):
                dve.wait_ge(b_um, t // 4 + 1)
                ins = dve.scalar_tensor_tensor(b_state[:, t + 1, :], b_state[:, t, :], b_pow[:, 2 * P + 1:2 * P + 2],
                                               bank[4 + t // 4][:, P * (t % 4):P * (t % 4 + 1)], ALU.mult, ALU.add)
                ins.then_inc(b_st, 1)
                dve.wait_ge(b_st, 2 + t + 1)
            for g in range(G):
                xg = x[:, 4 * g:4 * g + 4, :]
                c(dve.tensor_tensor(xg, xg, xn[:, 4 * g:4 * g + 4, :], ALU.add))
            for g in range(G):
                xg = x[:, 4 * g:4 * g + 4, :]
                dve.wait_ge(b_out, g + 1)
                dve.tensor_tensor(xg, bank[g][:, :].rearrange("p (t n) -> p t n", t=4), xg, ALU.add
                                  ).then_inc(x_ready, 1)

        def dla_tensor(pe):
            pe.wait_ge(b_w, 64)
            pe.matmul(bank[0][:, 0:P], b_ww, b_wr).then_inc(b_fold, 1)
            pe.wait_ge(b_wvd, 1)
            for g in range(G):
                pe.wait_ge(ln_xnT, 8 + g + 1)
                for i in range(4):
                    ins = pe.matmul(bank[g][:, P * i:P * (i + 1)], xnT[:, xtile(4 * g + i)], b_wv)
                ins.then_inc(b_vm, 1)
                if g >= 2:
                    pe.wait_ge(b_wtc, g - 1)
                for i in range(4):
                    ins = pe.transpose(bank[4 + g % 2][:, P * i:P * (i + 1)], xnT[:, shifted(4 * g + i)], ident[:, :])
                ins.then_inc(b_wt, 1)
            for g in range(G):
                pe.wait_ge(b_vc, g + 1)
                for i in range(4):
                    t = 4 * g + i
                    ins = pe.matmul(bank[g][:, P * i:P * (i + 1)], xnT[:, shifted(t)], xnT[:, xtile(t)])
                ins.then_inc(b_scm, 1)
            pe.wait_ge(b_wtc, G)
            for g in range(G):
                for i in range(4):
                    t = 4 * g + i
                    ins = pe.matmul(bank[4 + g][:, P * i:P * (i + 1)], b_wtok[:, t, :], b_v[:, t, :])
                ins.then_inc(b_um, 1)
            for g in range(G):
                pe.wait_ge(b_smd, g + 1)
                pe.wait_ge(b_xd, g + 1)
                pe.wait_ge(b_st, 2 + min(4 * g + 3, T - 1))
                for i in range(4):
                    t = 4 * g + i
                    o = bank[g][:, P * i:P * (i + 1)]
                    pe.matmul(o, b_sm2[:, t, :], b_v[:, t, :], start=True, stop=(t == 0))
                    if t:
                        ins = pe.matmul(o, b_xdec[:, t, :], b_state[:, t, :], start=False, stop=True)
                ins.then_inc(b_out, 1)


        arena.at = 24500
        g_w13 = arena.take(2, NX, GI)
        g_w2 = arena.take(NX, 2, P)
        g_gw = arena.take(NE)
        g_gb = arena.take(NE)
        g_pref = arena.take(NE)
        c_wnat = arena.take(2, NH // 2, P)
        c_wvT = arena.take(NH, CE)
        c_woT = arena.take(NH // 2, P)
        c_bo = arena.take(P)
        d_w = arena.take(4, P)
        assert arena.at <= a_words, (arena.at, a_words)
        later_load = sem("later_load")
        qk_load = sem("qk_load")

        def later_weights(sp):
            sp.wait_ge(x_ready, 4)
            sp.dma_start(c_wnat, I["C_wnat"]).then_inc(later_load, 16)
            sp.dma_start(c_wvT, I["C_wvT"]).then_inc(later_load, 16)
            sp.dma_start(c_woT, I["C_woT"]).then_inc(later_load, 16)
            sp.dma_start(c_bo, I["C_bo"].partition_broadcast(P)).then_inc(later_load, 16)
            sp.dma_start(g_w13, I["G_w13"]).then_inc(later_load, 16)
            sp.dma_start(g_w2, I["G_w2"]).then_inc(later_load, 16)
            sp.dma_start(g_gw, I["G_gw"]).then_inc(later_load, 16)
            sp.dma_start(g_gb, I["G_gb"].partition_broadcast(P)).then_inc(later_load, 16)
            sp.dma_start(g_pref, I["F_pref"].partition_broadcast(P)).then_inc(later_load, 16)
            sp.dma_start(d_w, I["D_w"]).then_inc(later_load, 16)
            sp.wait_ge(x_ready, 16)
            sp.dma_start(c_wqkT, I["C_wqkT"]).then_inc(qk_load, 16)
        LATER = 160

        arena.reset()
        c_wqkT = arena.take(2, NH * CD)
        c_as = arena.take(NH, P)
        c_sq = arena.take(2, NH * CD)
        c_n2 = arena.take(T, 2 * NH)
        c_mx = arena.take(2 * NH)
        c_r = arena.take(4)
        c_diag = arena.take(2 * NH)
        c_rr = arena.take(2 * NH)
        c_ch = arena.take(NH)
        c_ones = arena.take(P)
        c_mask = arena.take(P)
        c_cnt = arena.take(T)
        c_cnti = arena.take(T, dtype=I32)
        c_cum = arena.take(S)
        c_zero = arena.take(S)
        c_v = arena.take(2, NH, CE)
        c_a = arena.take(NH, P)
        c_s = arena.take(NH, P)
        c_kv = arena.take(NH, CE)
        c_vh = arena.take(NH, CD)
        c_vhT = arena.take(NH // 2, P)
        c_den = arena.take(NH)
        c_rden = arena.take(NH)
        assert arena.at <= 24500, arena.at

        c_c = sem("c_c")
        c_pc = sem("c_pc")
        c_consts = sem("c_consts")
        c_qk = sem("c_qk")
        c_sqd = sem("c_sqd")
        c_n2d = sem("c_n2d")
        c_mxd = sem("c_mxd")
        c_mxt = sem("c_mxt")
        c_mxr = sem("c_mxr")
        c_rd = sem("c_rd")
        c_dg = sem("c_dg")
        c_bc = sem("c_bc")
        c_am = sem("c_am")
        c_asd = sem("c_asd")
        c_apm = sem("c_apm")
        c_apc = sem("c_apc")
        c_vm = sem("c_vm")
        c_vc = sem("c_vc")
        c_scm = sem("c_scm")
        c_scd = sem("c_scd")
        c_num = sem("c_num")
        c_vhd = sem("c_vhd")
        c_kvm = sem("c_kvm")
        c_kvd = sem("c_kvd")
        c_tr = sem("c_tr")
        c_trc = sem("c_trc")
        c_out = sem("c_out")
        c_xadd = sem("c_xadd")
        count["c_c"] = 0

        def cla_gpsimd(pool):
            pool.wait_ge(x_ready, 16)
            pool.memset(c_ones, 1.0)
            pool.memset(c_zero, 0.0)
            pool.memset(c_mask, 1.0)
            pool.iota(c_cnti, [[P, T]], base=1, channel_multiplier=1)
            pool.memset(c_v, 1.0).then_inc(c_consts, 1)
            pool.wait_ge(c_consts, 1)
            pool.affine_select(out=c_mask, in_=c_mask, compare_op=ALU.is_ge, fill=0.0, base=0,
                               pattern=[[1, P]], channel_multiplier=-1).then_inc(c_consts, 1)
            pool.wait_ge(c_mxr, 1)
            pool.tensor_tensor(c_r[0:2 * NH, 1:2], c_r[0:2 * NH, 0:1], mhalf[0:2 * NH, 0:1], ALU.pow).then_inc(c_rd, 1)

        def cla_scalar(act):
            for n in range(2 * T):
                act.wait_ge(c_qk, n + 1)
                if n >= 2:
                    act.wait_ge(c_n2d, n - 1)
                act.activation(c_sq[:, n % 2, :].rearrange("p (a n) -> p a n", a=2), pair[n % 4][:, :, :], ACT.Square
                               ).then_inc(c_sqd, 1)
            for t in range(T):
                for i in range(4):
                    act.wait_ge(c_apm, 4 * t + i + 1)
                    if t:
                        act.wait_ge(c_num, 4 * t)
                    act.activation(c_a[:, 4 * i:4 * i + 4, :], bank[i].rearrange("p (h n) -> p h n", h=4), ACT.Copy
                                   ).then_inc(c_apc, 1)
                act.wait_ge(c_vm, t + 1)
                if t >= 2:
                    act.wait_ge(c_kvm, 4 * (t - 1))
                act.activation(c_v[:, t % 2, :, 0:CD], pair[2][:, :, :].rearrange("p a (h d) -> p (a h) d", d=CD),
                               ACT.Copy).then_inc(c_vc, 1)
                act.wait_ge(c_tr, t + 1)
                if t:
                    act.wait_ge(c_out, t)
                act.activation(c_vhT.rearrange("p (a h) n -> p a (h n)", a=2), pair[2][:, :, :], ACT.Copy
                               ).then_inc(c_trc, 1)

        def cla_vector(dve):
            c = lambda ins: link(dve, c_c, "c_c", ins)
            dve.wait_ge(later_load, LATER)
            dve.wait_ge(c_consts, 2)
            dve.wait_ge(ln_xn, 20)
            for g in range(G):
                xg = x[:, 4 * g:4 * g + 4, :]
                dve.tensor_tensor(xg, xg, c_bo.unsqueeze(1).broadcast_to([P, 4, P]), ALU.add)
            dve.tensor_copy(c_cnt, c_cnti)
            dve.memset(c_kv, 0.0)
            dve.wait_ge(ln_xnT, 20)
            c(dve.tensor_tensor_scan(c_cum, xnT[:, XO:XO + S], c_zero, 0.0, ALU.add, ALU.add))
            for n in range(2 * T):
                dve.wait_ge(c_sqd, n + 1)
                t, side = divmod(n, 2)
                dve.tensor_reduce(c_n2[:, t, NH * side:NH * (side + 1)],
                                  c_sq[:, n % 2, :].rearrange("p (h d) -> p h d", d=CD), AX.X, ALU.add
                                  ).then_inc(c_n2d, 1)
            dve.wait_ge(c_n2d, 2 * T)
            dve.tensor_reduce(c_mx, c_n2.rearrange("p t h -> p h t"), AX.X, ALU.max).then_inc(c_mxd, 1)
            dve.wait_ge(c_mxt, 1)
            dve.tensor_reduce(c_r[0:2 * NH, 0:1], bank[4][0:2 * NH, 0:P], AX.X, ALU.max).then_inc(c_mxr, 1)
            dve.wait_ge(c_rd, 1)
            dve.tensor_scalar(c_diag[0:2 * NH, :], ident[0:2 * NH, 0:2 * NH], c_r[0:2 * NH, 1:2], None, ALU.mult
                              ).then_inc(c_dg, 1)
            dve.wait_ge(c_bc, 1)
            c(dve.tensor_copy(c_rr, bank[4][:, 128:128 + 2 * NH]))
            c(dve.tensor_tensor(c_ch, c_rr[:, 0:NH], c_rr[:, NH:2 * NH], ALU.mult))
            for i in range(4):
                dve.wait_ge(c_am, i + 1)
                hs = c_as.rearrange("p (a j o) n -> p a j o n", a=2, o=2)[:, i % 2, :, i // 2, :]
                ch = c_ch.rearrange("p (a j o) -> p a j o", a=2, o=2)[:, i % 2, :, i // 2]
                dve.tensor_tensor(hs, bank[i].rearrange("p (h n) -> p h n", h=4),
                                  ch.unsqueeze(2).broadcast_to([P, 4, P]), ALU.mult).then_inc(c_asd, 1)
            for t in range(T):
                for i in range(4):
                    dve.wait_ge(c_scm, 4 * t + i + 1)
                    if t:
                        dve.wait_ge(c_num, 4 * t)
                    dve.tensor_tensor(c_s[:, 4 * i:4 * i + 4, :], bank[i].rearrange("p (h n) -> p h n", h=4),
                                      c_mask.unsqueeze(1).broadcast_to([P, 4, P]), ALU.mult).then_inc(c_scd, 1)
                for i in range(4):
                    hs = slice(4 * i, 4 * i + 4)
                    o = bank[NUMBANK[i]][:, 0:4 * CE].rearrange("p (h d) -> p h d", h=4)
                    dve.wait_ge(c_num, 4 * t + i + 1)
                    if t:
                        dve.wait_ge(c_tr, t)
                    c(dve.tensor_scalar(c_den[:, hs], o[:, :, CD], c_cnt[:, t:t + 1], None, ALU.add))
                    c(dve.reciprocal(c_rden[:, hs], c_den[:, hs]))
                    dve.tensor_tensor(c_vh[:, hs, :], o[:, :, 0:CD], c_rden[:, hs].unsqueeze(2).broadcast_to([P, 4, CD]),
                                      ALU.mult).then_inc(c_vhd, 1)
                if t < T - 1:
                    for i in range(4):
                        hs = slice(4 * i, 4 * i + 4)
                        dve.wait_ge(c_kvm, 4 * t + i + 1)
                        if t:
                            dve.wait_ge(c_kvd, 4 * t)
                        dve.tensor_tensor(c_kv[:, hs, :], bank[i][:, 0:4 * CE].rearrange("p (h d) -> p h d", h=4),
                                          c_kv[:, hs, :], ALU.add).then_inc(c_kvd, 1)
                dve.wait_ge(c_out, t + 1)
                ins = dve.tensor_tensor(x[:, t, :], bank[6][:, 0:P], x[:, t, :], ALU.add)
                ins.then_inc(c_xadd, 1)
            dve.wait_ge(c_xadd, T)
            dve.tensor_copy(c_den[:, 0:1], c_den[:, 1:2]).then_inc(x_ready, 4)

        NUMBANK = [6, 7, 4, 5]

        def cla_tensor(pe):
            pe.wait_ge(later_load, LATER)
            pe.wait_ge(qk_load, 16)
            pe.wait_ge(ln_xnT, 20)
            for n in range(2 * T):
                t, side = divmod(n, 2)
                if n >= 4:
                    pe.wait_ge(c_sqd, n - 3)
                for a in range(2):
                    ins = pe.matmul(pair[n % 4][:, a, :], xnT[:, xtile(t)], c_wqkT[:, side, NB * a:NB * (a + 1)])
                ins.then_inc(c_qk, 1)
            pe.wait_ge(c_sqd, 2 * T)
            for i in range(4):
                rows = slice(CD * (i // 2), CD * (i // 2 + 1))
                for j in range(4):
                    ins = pe.matmul(bank[i][:, P * j:P * (j + 1)], c_wnat[rows, 0, 4 * (i % 2) + j, :],
                                    c_wnat[rows, 1, 4 * (i % 2) + j, :])
                ins.then_inc(c_am, 1)
            pe.wait_ge(c_mxd, 1)
            pe.transpose(bank[4][0:2 * NH, 0:P], c_mx, ident[:, :]).then_inc(c_mxt, 1)
            pe.wait_ge(c_dg, 1)
            pe.matmul(bank[4][:, 128:128 + 2 * NH], c_ones[0:2 * NH, :], c_diag[0:2 * NH, :]).then_inc(c_bc, 1)

            def project(t):
                for i in range(4):
                    if t == 0:
                        pe.wait_ge(c_asd, 4)
                    elif t < T:
                        pe.wait_ge(c_kvd, 4 * (t - 1) + i + 1)
                    for j in range(4):
                        ins = pe.matmul(bank[i][:, P * j:P * (j + 1)], c_as[:, 4 * i + j, :], xnT[:, xtile(t)])
                    ins.then_inc(c_apm, 1)

            def finish(t):
                pe.wait_ge(c_trc, t + 1)
                for j in range(NH // 2):
                    ins = pe.matmul(bank[6][:, 0:P], c_vhT[:, j, :], c_woT[:, j, :], start=(j == 0), stop=(j == NH // 2 - 1))
                ins.then_inc(c_out, 1)

            for t in range(T):
                project(t)
                if t:
                    finish(t - 1)
                for a in range(2):
                    ins = pe.matmul(pair[2][:, a, :].rearrange("p (h d) -> p h d", d=CD), xnT[:, xtile(t)],
                                    c_wvT[:, 8 * a:8 * (a + 1), 0:CD])
                ins.then_inc(c_vm, 1)
                for i in range(4):
                    pe.wait_ge(c_apc, 4 * t + i + 1)
                    pe.matmul(bank[i], xnT[:, xtile(t)], c_a[:, 4 * i:4 * i + 4, :]).then_inc(c_scm, 1)
                pe.wait_ge(c_vc, t + 1)
                for i in range(4):
                    o = bank[NUMBANK[i]][:, 0:4 * CE]
                    if i == 0 and t:
                        pe.wait_ge(c_xadd, t)
                    pe.matmul(o, c_cumtile(t), c_wvT[:, 4 * i:4 * i + 4, :], start=True, stop=False, skip_group_check=True)
                    for j in range(4):
                        h = 4 * i + j
                        if t:
                            if j == 0:
                                pe.wait_ge(c_kvd, 4 * (t - 1) + i + 1)
                            pe.matmul(o[:, CE * j:CE * (j + 1)], c_a[:, h, :], c_kv[:, h, :], start=False, stop=False,
                                      skip_group_check=True)
                    pe.wait_ge(c_scd, 4 * t + i + 1)
                    for j in range(4):
                        h = 4 * i + j
                        ins = pe.matmul(o[:, CE * j:CE * (j + 1)], c_s[:, h, :], c_v[:, t % 2, h, :], start=False,
                                        stop=(j == 3), skip_group_check=True)
                    ins.then_inc(c_num, 1)
                if t < T - 1:
                    for i in range(4):
                        pe.matmul(bank[i][:, 0:4 * CE], xn[:, t, :], c_v[:, t % 2, 4 * i:4 * i + 4, :]).then_inc(c_kvm, 1)
                pe.wait_ge(c_vhd, 4 * t + 4)
                for j in range(NH // 2):
                    ins = pe.transpose(bank[4 + j // 4][:, P * (j % 4):P * (j % 4 + 1)],
                                       c_vh[:, 2 * j:2 * j + 2, :].rearrange("p h d -> p (h d)"), ident[:, :])
                ins.then_inc(c_tr, 1)
            finish(T - 1)

        c_cumtile = lambda t: c_cum[:, P * t:P * (t + 1)]

        arena.reset()
        g_lg = arena.take(20, T, NE)
        g_red = arena.take(8, T)
        g_s = arena.take(3, NB)
        g_h = arena.take(3, 2, NB)
        assert arena.at <= 24500

        g_c = sem("g_c")
        g_gate = sem("g_gate")
        g_gd = sem("g_gd")
        g_ge = sem("g_ge")
        g_hm = sem("g_hm")
        g_silu = sem("g_silu")
        g_mul = sem("g_mul")
        g_y = sem("g_y")
        g_add = sem("g_add")
        count["g_c"] = 0
        STEPS = 4 * NX

        def moe_scalar(act, rep):
            act.wait_ge(g_gd, rep + 1)
            act.activation(g_lg[:, 2], g_lg[:, 1], ACT.Exp).then_inc(g_ge, 1)
            for n in range(STEPS):
                for i in range(2):
                    m = 2 * STEPS * rep + 2 * n + i
                    act.wait_ge(g_hm, m + 1)
                    if m >= 3:
                        act.wait_ge(g_mul, m - 2)
                    act.activation(g_s[:, m % 3, :], pair[m % 3][:, 0, :], ACT.Silu).then_inc(g_silu, 1)

        def moe_vector(dve, rep):
            c = lambda ins: link(dve, g_c, "g_c", ins)
            L = g_lg
            over = lambda col: col.unsqueeze(2).broadcast_to([P, T, NE])
            along = lambda row: row.unsqueeze(1).broadcast_to([P, T, NE])
            k = 5 + 2 * rep
            dve.wait_ge(g_gate, rep + 1)
            if rep == 0:
                dve.wait_ge(later_load, LATER)
            lg = bank[5][:, 0:T * NE].rearrange("p (t e) -> p t e", e=NE)
            c(dve.tensor_reduce(g_red[:, 0], lg, AX.X, ALU.max))
            dve.tensor_tensor(L[:, 1], lg, over(g_red[:, 0]), ALU.subtract).then_inc(g_gd, 1)
            dve.wait_ge(g_ge, rep + 1)
            c(dve.tensor_reduce(g_red[:, 1], L[:, 2], AX.X, ALU.add))
            c(dve.reciprocal(g_red[:, 2], g_red[:, 1]))
            c(dve.tensor_tensor(L[:, 3], L[:, 2], over(g_red[:, 2]), ALU.mult))
            c(dve.tensor_tensor(L[:, 4], L[:, 3], along(g_gb), ALU.add))

            def best(src, at, red):
                c(dve.tensor_reduce(g_red[:, red], L[:, src], AX.X, ALU.max))
                c(dve.tensor_tensor(L[:, at], L[:, src], over(g_red[:, red]), ALU.is_equal))
                c(dve.tensor_tensor(L[:, at + 1], L[:, at], along(g_pref), ALU.mult))
                c(dve.tensor_reduce(g_red[:, red + 1], L[:, at + 1], AX.X, ALU.max))
                c(dve.tensor_tensor(L[:, at + 2], L[:, at + 1], over(g_red[:, red + 1]), ALU.is_equal))

            best(4, 5, 3)
            c(dve.scalar_tensor_tensor(L[:, 8], L[:, 7], -1e30, L[:, 4], ALU.mult, ALU.add))
            best(8, 9, 5)
            c(dve.tensor_tensor(L[:, 12], L[:, 7], L[:, 11], ALU.add))
            c(dve.tensor_tensor(L[:, 13], L[:, 3], L[:, 12], ALU.mult))

            def add(n):
                e, b = divmod(n, 4)
                nn = STEPS * rep + n
                dve.wait_ge(g_y, nn + 1)
                if e:
                    dve.wait_ge(g_add, nn - 3)
                y = bank[6 + nn % 2]
                for i in range(4):
                    t = 4 * b + i
                    w = L[:, 13, t, e:e + 1] if e < NE else 1.0
                    ins = dve.scalar_tensor_tensor(x[:, t, :], y[:, P * i:P * (i + 1)], w, x[:, t, :], ALU.mult, ALU.add)
                ins.then_inc(g_add, 1)

            dve.wait_ge(ln_xn, 4 * k + 4)
            for n in range(STEPS):
                for i in range(2):
                    m = 2 * STEPS * rep + 2 * n + i
                    nn = STEPS * rep + n
                    dve.wait_ge(g_silu, m + 1)
                    if nn >= 3:
                        dve.wait_ge(g_y, nn - 2)
                    dve.tensor_tensor(g_h[:, nn % 3, i, :], pair[m % 3][:, 1, :], g_s[:, m % 3, :], ALU.mult
                                      ).then_inc(g_mul, 1)
                if n:
                    add(n - 1)
            add(STEPS - 1)
            dve.wait_ge(g_add, STEPS * (rep + 1))
            dve.tensor_copy(g_red[:, 7], g_red[:, 0]).then_inc(x_ready, 4)

        def moe_tensor(pe, rep):
            k = 5 + 2 * rep
            pe.wait_ge(later_load, LATER)
            for t in range(T):
                if t % 4 == 0:
                    pe.wait_ge(ln_xnT, 4 * k + t // 4 + 1)
                ins = pe.matmul(bank[5][:, NE * t:NE * (t + 1)], xnT[:, xtile(t)], g_gw)
            ins.then_inc(g_gate, 1)

            def down(n):
                e, b = divmod(n, 4)
                nn = STEPS * rep + n
                pe.wait_ge(g_mul, 2 * nn + 2)
                if nn >= 2:
                    pe.wait_ge(g_add, nn - 1)
                for i in range(4):
                    for j in range(2):
                        ins = pe.matmul(bank[6 + nn % 2][:, P * i:P * (i + 1)], g_h[:, nn % 3, j, P * i:P * (i + 1)],
                                        g_w2[:, e, j, :], start=(j == 0), stop=(j == 1))
                ins.then_inc(g_y, 1)

            for n in range(STEPS):
                e, b = divmod(n, 4)
                for i in range(2):
                    m = 2 * STEPS * rep + 2 * n + i
                    if m >= 3:
                        pe.wait_ge(g_mul, m - 2)
                    if m % 3 == 2 and m < 3 + 2 * STEPS * rep:
                        pe.wait_ge(g_gd, rep + 1)
                    for a in range(2):
                        ins = pe.matmul(pair[m % 3][:, a, :], g_w13[:, a, e, P * i:P * (i + 1)], xnT[:, xcol(b)])
                    ins.then_inc(g_hm, 1)
                if n:
                    down(n - 1)
            down(STEPS - 1)

        arena.reset()
        d_a = arena.take(P)
        d_b = arena.take(P)
        d_aT = arena.take(S)
        d_v = arena.take(T, P)
        d_p = arena.take(2, S)
        d_pT = arena.take(4, NB)
        d_m = arena.take(T, 8)
        assert arena.at <= 24500
        d_c = sem("d_c")
        d_fold = sem("d_fold")
        d_foldc = sem("d_foldc")
        d_pre = sem("d_pre")
        d_prec = sem("d_prec")
        d_s = sem("d_s")
        d_max = sem("d_max")
        d_bias = sem("d_bias")
        d_exp = sem("d_exp")
        d_tr = sem("d_tr")
        d_trA = sem("d_trA")
        d_trB = sem("d_trB")
        d_pv = sem("d_pv")
        d_x = sem("d_x")
        count["d_c"] = 0
        SC7 = float(np.float32(1.0) / np.sqrt(np.float32(P)))

        def soft_scalar(act):
            act.wait_ge(d_fold, 1)
            act.activation(d_a, bank[0][:, 0:P], ACT.Copy)
            act.activation(d_b, bank[0][:, P:2 * P], ACT.Copy).then_inc(d_foldc, 1)
            for n in range(8):
                act.wait_ge(d_pre, n + 1)
                dst = d_aT[:, NB * n:NB * (n + 1)] if n < 4 else d_v[:, 4 * (n - 4):4 * (n - 3), :].rearrange("p t n -> p (t n)")
                act.activation(dst, bank[n % 4], ACT.Copy).then_inc(d_prec, 1)

            def turned(t):
                for i in range(2):
                    j = 4 * t + 2 * i
                    act.wait_ge(d_tr, j + 1)
                    if j >= 4:
                        act.wait_ge(d_pv, j - 3)
                    act.activation(d_pT[:, j % 4, :], bank[4 + j % 2], ACT.Copy).then_inc(d_trA, 1)

            for t in range(T):
                act.wait_ge(d_bias, t + 1)
                if t >= 2:
                    act.wait_ge(d_tr, 4 * (t - 1))
                for a in range(2):
                    act.activation(d_p[:, t % 2, 2 * NB * a:2 * NB * (a + 1)].rearrange("p (a n) -> p a n", a=2),
                                   pair[a][:, :, :], ACT.Exp, bias=d_m[:, t, 3:4], scale=SC7,
                                   accum_out=d_m[:, t, 4 + a:5 + a]).then_inc(d_exp, 1)
                if t:
                    turned(t - 1)
            turned(T - 1)

        def soft_vector(dve):
            c = lambda ins: link(dve, d_c, "d_c", ins)

            def turned(t):
                for i in range(2):
                    j = 4 * t + 2 * i + 1
                    dve.wait_ge(d_tr, j + 1)
                    if j >= 4:
                        dve.wait_ge(d_pv, j - 3)
                    dve.tensor_copy(d_pT[:, j % 4, :], bank[4 + j % 2]).then_inc(d_trB, 1)

            def finish(t):
                dve.wait_ge(d_exp, 2 * t + 2)
                c(dve.tensor_reduce(d_m[:, t, 6:7], d_m[:, t, 4:6], AX.X, ALU.add))
                c(dve.reciprocal(d_m[:, t, 7:8], d_m[:, t, 6:7]))
                dve.wait_ge(d_pv, 4 * t + 4)
                ins = dve.scalar_tensor_tensor(x[:, t, :], bank[6 + t % 2][:, 0:P], d_m[:, t, 7:8], x[:, t, :],
                                               ALU.mult, ALU.add)
                ins.then_inc(d_x, 1)

            dve.wait_ge(ln_xn, 28)
            for t in range(T):
                for a in range(2):
                    dve.wait_ge(d_s, 2 * t + a + 1)
                    dve.tensor_reduce(d_m[:, t, a:a + 1], pair[a][:, :, :], AX.XY, ALU.max).then_inc(d_max, 1)
                dve.wait_ge(d_max, 2 * t + 2)
                c(dve.tensor_reduce(d_m[:, t, 2:3], d_m[:, t, 0:2], AX.X, ALU.max))
                dve.tensor_scalar(d_m[:, t, 3:4], d_m[:, t, 2:3], -SC7, None, ALU.mult).then_inc(d_bias, 1)
                if t:
                    turned(t - 1)
                if t >= 1:
                    finish(t - 1)
            turned(T - 1)
            finish(T - 1)
            dve.wait_ge(d_x, T)
            dve.tensor_copy(d_m[:, 0, 0:1], d_m[:, 0, 1:2]).then_inc(x_ready, 4)

        def soft_tensor(pe):
            pe.wait_ge(ln_xnT, 25)
            pe.matmul(bank[0][:, 0:P], d_w[:, 0, :], d_w[:, 1, :])
            pe.matmul(bank[0][:, P:2 * P], d_w[:, 2, :], d_w[:, 3, :]).then_inc(d_fold, 1)
            pe.wait_ge(d_foldc, 1)
            for n in range(8):
                pe.wait_ge(ln_xnT, 24 + n % 4 + 1)
                if n >= 4:
                    pe.wait_ge(d_prec, n - 3)
                if n < 4:
                    ins = pe.matmul(bank[n % 4], d_a, xnT[:, xcol(n)])
                else:
                    for i in range(4):
                        ins = pe.matmul(bank[n % 4][:, P * i:P * (i + 1)], xnT[:, xtile(4 * (n - 4) + i)], d_b)
                ins.then_inc(d_pre, 1)
            pe.wait_ge(d_prec, 8)

            def scores(t):
                for a in range(2):
                    if t:
                        pe.wait_ge(d_exp, 2 * (t - 1) + a + 1)
                    for b in range(2):
                        ins = pe.matmul(pair[a][:, b, :], d_aT[:, P * t:P * (t + 1)], xnT[:, xcol(2 * a + b)])
                    ins.then_inc(d_s, 1)

            def turn(t, i):
                j = 4 * t + i
                if i % 2 == 0:
                    pe.wait_ge(d_exp, 2 * t + i // 2 + 1)
                if j >= 2:
                    pe.wait_ge(d_trA if j % 2 == 0 else d_trB, (j - 2) // 2 + 1)
                for q in range(4):
                    ins = pe.transpose(bank[4 + j % 2][:, P * q:P * (q + 1)],
                                       d_p[:, t % 2, NB * i + P * q:NB * i + P * (q + 1)], ident[:, :])
                ins.then_inc(d_tr, 1)

            def values(t, i):
                j = 4 * t + i
                pe.wait_ge(d_trA if j % 2 == 0 else d_trB, j // 2 + 1)
                if i == 0 and t >= 2:
                    pe.wait_ge(d_x, t - 1)
                for q in range(4):
                    ins = pe.matmul(bank[6 + t % 2][:, 0:P], d_pT[:, j % 4, P * q:P * (q + 1)], d_v[:, 4 * i + q, :],
                                    start=(i == 0 and q == 0), stop=(i == 3 and q == 3))
                ins.then_inc(d_pv, 1)

            scores(0)
            for t in range(T):
                if t + 1 < T:
                    scores(t + 1)
                turn(t, 0)
                turn(t, 1)
                for i in range(4):
                    values(t, i)
                    if i < 2:
                        turn(t, i + 2)

        def later_stages(n):
            ffn = lambda rep: {"pool": lambda e: ffn_gpsimd(e, rep), "act": lambda e: ffn_scalar(e, rep),
                               "dve": lambda e: ffn_vector(e, rep), "pe": lambda e: ffn_tensor(e, rep)}
            dla = {"pool": dla_gpsimd, "act": dla_scalar, "dve": dla_vector, "pe": dla_tensor}
            moe = lambda rep: {"act": lambda e: moe_scalar(e, rep), "pool": lambda e: None,
                               "dve": lambda e: moe_vector(e, rep), "pe": lambda e: moe_tensor(e, rep)}
            cla = {"pool": cla_gpsimd, "act": cla_scalar, "dve": cla_vector, "pe": cla_tensor}
            soft = {"pool": lambda e: None, "act": soft_scalar, "dve": soft_vector, "pe": soft_tensor}
            return [ffn(0), dla, ffn(1), cla, moe(0), soft, moe(1)][:n - 1]

        block = ctx.enter_context(nc.Block())

        @block.sync
        def _(sp):
            for g in range(G):
                sp.dma_start(x[:, 4 * g:4 * g + 4, :], I["x"][NB * g:NB * (g + 1), :].rearrange("(t p) d -> p t d", p=P)
                             ).then_inc(x_in[g], 16)
            mla_load(sp)
            ffn_load(sp)
            dla_load(sp)
            mla_sync(sp)
            if STAGES > 4:
                later_weights(sp)
            for g in range(G):
                sp.wait_ge(x_ready, 4 * (STAGES - 1) + g + 1)
                sp.dma_start(out[NB * g:NB * (g + 1), :].rearrange("(t p) d -> p t d", p=P),
                             x[:, 4 * g:4 * g + 4, :]).then_inc(stored, 16)
            sp.wait_ge(stored, 64)

        @block.gpsimd
        def _(pool):
            pool.memset(ident[:, :], 0.0).then_inc(ident_done, 1)
            pool.memset(mhalf[:, :], -0.5).then_inc(ident_done, 1)
            pool.wait_ge(ident_done, 2)
            pool.affine_select(out=ident[:, :], in_=ident[:, :], compare_op=ALU.not_equal, fill=1.0, base=0,
                               pattern=[[-1, P]], channel_multiplier=1).then_inc(ident_done, 1)
            pool.memset(stack[0][0].bitcast(F32), 0.0)
            pool.memset(stack[0][1].bitcast(F32), 0.0).then_inc(a_zero, 1)
            ln_gpsimd(pool, 0)
            mla_gpsimd(pool)
            for k, stage in enumerate(later_stages(STAGES)):
                ln_gpsimd(pool, k + 1)
                stage["pool"](pool)

        @block.scalar
        def _(act):
            ln_scalar(act, 0)
            mla_scalar(act)
            for k, stage in enumerate(later_stages(STAGES)):
                ln_scalar(act, k + 1)
                stage["act"](act)

        @block.vector
        def _(dve):
            dve.memset(xnT[:, 0:XO], 0.0)
            dve.memset(vpad, 0.0).then_inc(a_vzero, 1)
            dve.wait_ge(a_vzero, 1)
            dve.memset(vpad[:, :, :, DH:DH + 1], 1.0).then_inc(a_vzero, 1)
            ln_vector(dve, 0)
            mla_vector(dve)
            for k, stage in enumerate(later_stages(STAGES)):
                ln_vector(dve, k + 1)
                stage["dve"](dve)

        @block.tensor
        def _(pe):
            pe.wait_ge(ident_done, 3)
            ln_tensor(pe, 0)
            mla_tensor(pe)
            for k, stage in enumerate(later_stages(STAGES)):
                ln_tensor(pe, k + 1)
                stage["pe"](pe)


def host_layout(inputs):
    f = lambda name: np.asarray(inputs[name])
    z = lambda *shape: np.zeros(shape, np.float32)
    A = {}
    A["x"] = f("L0_attn_a_x").reshape(S, P)
    wdq, wdkv = f("L0_attn_a_W_DQ"), f("L0_attn_a_W_DKV")
    wqr, wkr = f("L0_attn_a_W_QR"), f("L0_attn_a_W_KR")
    A["WDQT"], A["WDKVT"] = wdq.T, wdkv.T
    swap = np.arange(HR).reshape(-1, 2)[:, ::-1].reshape(-1)
    A["WQR2"] = np.concatenate([wqr, wqr[:, swap]], axis=1)
    ab = z(2, P, P - HR)
    ab[0, :, 0:DR] = wkr
    ab[1, :, 0:DR] = wkr[:, swap[:DR]]
    ab[0, :, 32:64] = wdq
    A["WABr"] = ab
    A["WUV"] = f("L0_attn_a_W_UV")
    uk = z(DL, NH, DQK)
    uk[:, :, 0:DH] = f("L0_attn_a_W_UK").reshape(DL, NH, DH)
    A["WUKc"] = uk.reshape(DL, NH * DQK)
    wq, wks = z(P, NH, DQK), z(P, NH, DQK)
    wq[96:P, :, 0:DH] = f("L0_attn_a_W_UQ").reshape(DL, NH, DH)
    for h in range(NH):
        for i in range(DR):
            wq[DR * h + i, h, DH + i] = 1.0
            wks[HR + i, h, DH + i] = 1.0
    A["WQc"], A["WKsel"] = wq.reshape(P, -1), wks.reshape(P, -1)
    A["WO"] = f("L0_attn_a_W_O")
    inv = np.float32(10000.0) ** (-np.arange(0, DR, 2, dtype=np.float32) / np.float32(DR))
    angle = np.arange(S, dtype=np.float32)[:, None] * inv
    cos, sin = z(96, S), z(96, S)
    for r in range(HR + DR):
        cos[r] = np.cos(angle[:, (r % DR) // 2])
        sin[r] = np.sin(angle[:, (r % DR) // 2]) * (1.0 if r % 2 else -1.0)
    A["cosT"], A["sinT"] = cos, sin
    e1, e2, e3 = f("L0_ffn_ew1"), f("L0_ffn_ew2"), f("L0_ffn_ew3")
    w12 = z(P, 2, NE + 1, FH)
    b12 = z(2, NE + 1, FH)
    for a, (w, b, sw, sb) in enumerate(((e1, "L0_ffn_eb1", "L0_ffn_sw1", "L0_ffn_sb1"),
                                        (e2, "L0_ffn_eb2", "L0_ffn_sw2", "L0_ffn_sb2"))):
        w12[:, a, 0:NE] = w.transpose(2, 0, 1)
        w12[:, a, NE] = f(sw).T
        b12[a, 0:NE], b12[a, NE] = f(b), f(sb)
    A["F_w12"], A["F_b12"] = w12, b12.reshape(-1)
    w3 = z(P, 5, P)
    w3[:, 0:4] = e3.transpose(0, 2, 1).reshape(4, P, P).transpose(1, 0, 2)
    w3[0:FH, 4] = f("L0_ffn_sw3").T
    w3[FH, 4] = f("L0_ffn_sb3")
    w3[FH + 1:FH + 1 + NE, 4] = f("L0_ffn_eb3")
    A["F_w3"] = w3
    bsel, gcol = z(P, 5, NE + 1), z(P, 5)
    for kt in range(4):
        for half in range(2):
            rows = slice(FH * half, FH * (half + 1))
            bsel[rows, kt, 1 + 2 * kt + half] = f("L0_ffn_sel_ln_b")
            gcol[rows, kt] = f("L0_ffn_sel_ln_g")
    bsel[0:FH, 4, 0] = f("L0_ffn_s_ln_b")
    gcol[0:FH, 4] = f("L0_ffn_s_ln_g")
    A["F_bsel"], A["F_gcol"] = bsel, gcol
    A["F_wg"] = np.concatenate([f("L0_ffn_eg_w").T, f("L0_ffn_sg_w").T], axis=1)
    A["F_bg"] = np.concatenate([f("L0_ffn_eg_b"), f("L0_ffn_sg_b")])
    A["F_bx"] = f("L0_ffn_exp_bias")
    A["F_pref"] = np.arange(NE, 0, -1).astype(np.float32)
    for name, rows in (("F_ib", f("L0_ffn_index_b")), ("F_it", f("L0_ffn_index_t"))):
        A[name], A[name + "c"] = rows, rows.reshape(2, P).T
    A["B_ww"], A["B_wrT"] = f("L0_attn_b_W_write"), f("L0_attn_b_W_read").T
    A["B_decay"], A["B_la"] = f("L0_attn_b_decay").reshape(1), f("L0_attn_b_log_alpha").reshape(1)
    wq, wk, wv, wo = (f("L1_attn_a_" + n) for n in ("Wq", "Wk", "Wv", "Wo"))
    A["C_wnat"] = np.stack([w.reshape(NH // 2, P, P).transpose(1, 0, 2) for w in (wq, wk)], axis=1)
    A["C_wqkT"] = np.stack([wq.T, wk.T], axis=1)
    wvT = z(P, NH, CE)
    wvT[:, :, 0:CD] = wv.T.reshape(P, NH, CD)
    A["C_wvT"] = wvT
    A["C_woT"] = wo.T.reshape(NH // 2, P, P).transpose(1, 0, 2)
    A["C_bo"] = f("L1_attn_a_bo")
    w13, w2 = z(P, 2, NX, GI), z(P, NX, 2, P)
    for a, n in enumerate(("1", "3")):
        w13[:, a, 0:NE] = f("L1_ffn_w" + n).transpose(2, 0, 1)
        w13[:, a, NE] = f("L1_ffn_sw" + n).T
    w2[:, 0:NE] = f("L1_ffn_w2").transpose(0, 2, 1).reshape(NE, 2, P, P).transpose(2, 0, 1, 3)
    w2[:, NE] = f("L1_ffn_sw2").T.reshape(2, P, P).transpose(1, 0, 2)
    A["G_w13"], A["G_w2"] = w13, w2
    A["G_gw"], A["G_gb"] = f("L1_ffn_gate_w").T, f("L1_ffn_gate_bias")
    qkv = f("L1_attn_b_W_qkv")
    A["D_w"] = np.stack([qkv[0::3], qkv[1::3], qkv[2::3], f("L1_attn_b_W_out").T], axis=1)
    return {k: np.ascontiguousarray(v) for k, v in A.items()}


def kernel(**inputs):
    import concourse.bacc as _bacc
    from concourse.bass_utils import run_bass_kernel_spmd as _run

    nc = _bacc.Bacc("TRN2", target_bir_lowering=False, num_devices=1)
    arrays = host_layout(inputs)
    aps = {name: nc.dram_tensor(f"in_{name}", a.shape, mybir.dt.from_np(a.dtype), kind="ExternalInput").ap()
           for name, a in arrays.items()}
    out = nc.dram_tensor("out", (S, P), F32, kind="ExternalOutput").ap()
    program(nc, aps, out)
    r = _run(nc, [{f"in_{name}": a for name, a in arrays.items()}], core_ids=[0])
    return r.results[0]["out"].reshape(1, S, P)
```

```python
from contextlib import ExitStack

import numpy as np

import concourse.bass as bass
from concourse import mybir

ACT = mybir.ActivationFunctionType
ALU = mybir.AluOpType
F32 = mybir.dt.float32
BF16 = mybir.dt.bfloat16
I32 = mybir.dt.int32
F32R = mybir.dt.float32r
AX = mybir.AxisListType

P = 128
S = 2048
T = S // P
G = 4
NB = 512
SPLIT = 5
XO = 4
EPS = 1e-5
STAGES = 8

NH, DH, DR, DL = 16, 8, 4, 32
DQK = DH + DR
HR = NH * DR
CP = NH * DQK // 2
CLIP = 80.0
NE, FH, M = 8, 64, 256
CD, CE = 64, 65
NX, GI = 9, 256
PARTS = [(0, 0), (0, 1), (1, 0)]
COMBOS = [(0, 0), (0, 1), (1, 0), (0, 2), (2, 0), (1, 1)]


class Arena:

    def __init__(self, tensor, words, native=F32):
        self.tensor, self.words, self.native, self.at = tensor, words, native, 0

    def reset(self):
        self.at = 0

    def take(self, *shape, dtype=None):
        n = int(np.prod(shape))
        words = n if dtype is not BF16 else n // 2
        view = self.tensor[:, self.at:self.at + words]
        self.at += words
        assert self.at <= self.words, (self.at, self.words)
        if dtype not in (None, self.native):
            view = view.bitcast(dtype)
        if len(shape) > 1:
            names = "abcde"[:len(shape)]
            view = view.rearrange(f"p ({' '.join(names)}) -> p {' '.join(names)}",
                                  **{c: n for c, n in zip(names, shape)})
        return view


def program(nc, I, out):
    ctx = ExitStack()
    with ctx:
        def sb(name, shape, dt=F32):
            return ctx.enter_context(nc.sbuf_tensor(name, shape, dt))

        def sem(name):
            return ctx.enter_context(nc.semaphore(name))

        pair = [ctx.enter_context(nc.psum_tensor(f"pair{i}", [P, 2, NB], F32)) for i in range(4)]
        bank = [pair[i // 2][:, i % 2, :] for i in range(8)]

        x = sb("x", [P, T, P])
        xn = sb("xn", [P, T, P])
        xnT = sb("xnT", [P, XO + S])
        ident = sb("ident", [P, P])
        stats = sb("stats", [P, T, 6])
        mv = sb("mv", [P, T, 2])
        ve = sb("ve", [P, T])
        rstd = sb("rstd", [P, T])
        mhalf = sb("mhalf", [P, 64])
        ROUND = 4 * S
        ARENA = 46500 - ROUND
        LATER_AT = 21344
        arena = Arena(sb("arena", [P, ARENA]), ARENA)
        rounded = Arena(sb("rounded", [P, ROUND], F32R), ROUND, F32R)
        xr = rounded.take(2, S)
        XR_WORDS = rounded.at
        rounded.reset()

        x_in = [sem(f"x_in{g}") for g in range(G)]
        x_ready = sem("x_ready")
        ident_done = sem("ident_done")
        ln_stats = sem("ln_stats")
        ln_moments = sem("ln_moments")
        ln_ve = sem("ln_ve")
        ln_rstd = sem("ln_rstd")
        ln_xn = sem("ln_xn")
        ln_turned = sem("ln_turned")
        ln_xnT = sem("ln_xnT")
        ln_hi = sem("ln_hi")
        ln_lo = sem("ln_lo")
        stored = sem("stored")

        def xcol(g):
            return slice(XO + NB * g, XO + NB * (g + 1))

        def xtile(t):
            return slice(XO + P * t, XO + P * (t + 1))

        def ln_moment(dve, k, g):
            if k == 0:
                dve.wait_ge(x_in[g], 16)
            else:
                dve.wait_ge(x_ready, 4 * (k - 1) + g + 1)
            for t in range(4 * g, 4 * g + 4):
                ins = dve.bn_stats(stats[:, t, :], x[:, t, :])
            ins.then_inc(ln_stats, 1)
            dve.wait_ge(ln_stats, 4 * k + g + 1)
            for t in range(4 * g, 4 * g + 4):
                ins = dve.bn_aggr(mv[:, t, :], stats[:, t, :])
            ins.then_inc(ln_moments, 1)

        def ln_normalise(dve, k, g):
            dve.wait_ge(ln_rstd, 4 * k + g + 1)
            for t in range(4 * g, 4 * g + 4):
                ins = dve.tensor_scalar(xn[:, t, :], x[:, t, :], mv[:, t, 0:1], rstd[:, t:t + 1],
                                        ALU.subtract, ALU.mult)
            ins.then_inc(ln_xn, 1)

        def ln_vector(dve, k):
            for g in range(G):
                ln_moment(dve, k, g)
                if g == 1 and k:
                    dve.wait_ge(x_ready, 4 * k)
                if g:
                    ln_normalise(dve, k, g - 1)
            ln_normalise(dve, k, G - 1)

        def ln_follow(dve, k, g):
            if k < STAGES:
                ln_moment(dve, k, g)
                if g:
                    ln_normalise(dve, k, g - 1)
                if g == G - 1:
                    ln_normalise(dve, k, g)

        def ln_gpsimd(pool, k):
            for g in range(G):
                pool.wait_ge(ln_moments, 4 * k + g + 1)
                pool.tensor_scalar(ve[:, 4 * g:4 * g + 4], mv[:, 4 * g:4 * g + 4, 1], EPS, None,
                                   ALU.add).then_inc(ln_ve, 1)
                pool.wait_ge(ln_ve, 4 * k + g + 1)
                pool.tensor_tensor(rstd[:, 4 * g:4 * g + 4], ve[:, 4 * g:4 * g + 4], mhalf[:, 0:4],
                                   ALU.pow).then_inc(ln_rstd, 1)

        def ln_low(pool, k):
            for g in range(G):
                pool.wait_ge(ln_xnT, 4 * k + g + 1)
                pool.tensor_tensor(xr[:, 1, NB * g:NB * (g + 1)], xnT[:, xcol(g)],
                                   xr[:, 0, NB * g:NB * (g + 1)].bitcast(F32), ALU.subtract).then_inc(ln_lo, 1)

        def ln_tensor(pe, k):
            for g in range(G):
                pe.wait_ge(ln_xn, 4 * k + g + 1)
                if 4 * k + g >= 2:
                    pe.wait_ge(ln_xnT, 4 * k + g - 1)
                for i in range(4):
                    ins = pe.transpose(bank[6 + g % 2][:, P * i:P * (i + 1)], xn[:, 4 * g + i, :], ident[:, :])
                ins.then_inc(ln_turned, 1)

        def ln_scalar(act, k):
            for g in range(G):
                act.wait_ge(ln_turned, 4 * k + g + 1)
                if k >= SPLIT:
                    act.activation(xr[:, 0, NB * g:NB * (g + 1)], bank[6 + g % 2][:, :], ACT.Copy).then_inc(ln_hi, 1)
                act.activation(xnT[:, xcol(g)], bank[6 + g % 2][:, :], ACT.Copy).then_inc(ln_xnT, 1)

        arena.reset()
        vpad = arena.take(T, NH, 32)
        stack = [[a.take(4, S, dtype=BF16) for _ in range(2)] for a in (rounded, arena)]
        arena.at -= 2 * 2 * S
        parts = arena.take(2, 3, S, dtype=BF16)
        arena.at += 2 * 2 * S - 3 * S
        pring = arena.take(6, 2, NB)
        arena.at -= 6 * 2 * NB
        cosT, sinT, zq = arena.take(S), arena.take(S), arena.take(S)
        resid_words = arena.at
        resid = arena.take(2, NB)
        rope1, rope2 = arena.take(2, NB), arena.take(2, NB)
        oT = arena.take(2, NB)
        attn = arena.take(T, P)
        m_wab = arena.take(2, P)
        m_wq = arena.take(2 * CP)
        m_wkc, m_wkr = arena.take(2 * CP), arena.take(2 * CP)
        m_wv = arena.take(P)
        m_wo = arena.take(P)
        m_dqT = arena.take(P)
        m_dkvT = arena.take(P)
        m_qr2 = arena.take(2 * HR)
        m_uk = arena.take(2 * CP)
        m_uv = arena.take(P)
        rdenA = arena.take(16)
        scratch = nc.dram_tensor("split_parts", [2, 2, 3, CP, S], BF16, kind="Internal").ap()

        a_zero = sem("a_zero")
        a_vzero = sem("a_vzero")
        a_w = sem("a_w")
        a_w2 = sem("a_w2")
        a_fold = sem("a_fold")
        a_folded = sem("a_folded")
        a_ab = sem("a_ab")
        a_rope = sem("a_rope")
        a_cq = sem("a_cq")
        a_z = sem("a_z")
        a_v = sem("a_v")
        a_vcopied = sem("a_vcopied")
        a_qk = sem("a_qk")
        a_hi = sem("a_hi")
        a_res = sem("a_res")
        a_mid = sem("a_mid")
        a_lo = sem("a_lo")
        a_parts = [sem(f"a_parts{i}") for i in range(4)]
        a_stack = [sem(f"a_stack{i}") for i in range(2)]
        a_scores = sem("a_scores")
        a_exp = sem("a_exp")
        a_clip = sem("a_clip")
        a_mask = sem("a_mask")
        a_pv = sem("a_pv")
        a_oT = sem("a_oT")
        a_turned = sem("a_turned")
        a_rden = sem("a_rden")
        a_norm = sem("a_norm")
        a_at = sem("a_at")
        a_atc = sem("a_atc")
        a_wo = sem("a_wo")

        UNITS = [(g, qb, kt) for g in range(4) for qb in range(G) for kt in range(4 * qb + 4)]
        BLOCKS = [(g, qb) for g in range(4) for qb in range(G)]
        first_col = lambda qb, kt: max(0, kt * P - qb * NB)
        last_unit = {}
        for n, (g, qb, kt) in enumerate(UNITS):
            last_unit[(g, qb)] = n
        masked = [kt >= 4 * qb for _, qb, kt in UNITS]
        masks_to = [2 * sum(masked[:n + 1]) for n in range(len(UNITS))]
        QK = [(a, side, b) for a in range(2) for side in range(2) for b in range(G)]

        def mla_load(sp):
            sp.dma_start(m_dqT[0:DL, :], I["WDQT"]).then_inc(a_w, 16)
            sp.dma_start(m_dkvT[0:DL, :], I["WDKVT"]).then_inc(a_w, 16)
            sp.dma_start(m_qr2[0:DL, :], I["WQR2"]).then_inc(a_w, 16)
            sp.dma_start(m_uk[0:DL, :], I["WUKc"]).then_inc(a_w, 16)
            sp.dma_start(m_uv[0:DL, :], I["WUV"]).then_inc(a_w, 16)
            sp.dma_start(m_wab[:, :, HR:P], I["WABr"].rearrange("a p n -> p a n")).then_inc(a_w2, 16)
            sp.dma_start(m_wq, I["WQc"]).then_inc(a_w2, 16)
            sp.dma_start(m_wkr, I["WKsel"]).then_inc(a_w2, 16)
            sp.dma_start(m_wo, I["WO"]).then_inc(a_w2, 16)
            sp.dma_start(cosT[0:96, :], I["cosT"]).then_inc(a_w2, 16)
            sp.dma_start(sinT[0:96, :], I["sinT"]).then_inc(a_w2, 16)

        def mla_sync(sp):
            for n in range(4):
                a, side = divmod(n, 2)
                sp.wait_ge(a_lo, 4 * (n + 1))
                sp.dma_start(scratch[side, a].rearrange("c p n -> p c n"),
                             parts[0:CP, n % 2]).then_inc(a_parts[n], 16)
            for g in range(4):
                sp.wait_ge(a_parts[2 * (g // 2)], 16)
                sp.wait_ge(a_parts[2 * (g // 2) + 1], 16)
                if g < 2:
                    sp.wait_ge(a_zero, g + 1)
                if g >= 2:
                    sp.wait_ge(a_pv, last_unit[(g - 2, G - 1)] + 1)
                for side in range(2):
                    for c, combo in enumerate(COMBOS):
                        src = scratch[side, g // 2, combo[side], (g % 2) * 48:(g % 2) * 48 + 48, :]
                        sp.dma_start(stack[g % 2][side][c * DQK:(c + 1) * DQK],
                                     src.rearrange("(h d) n -> d h n", h=4)).then_inc(a_stack[g % 2], 16)

        def mla_gpsimd(pool, loop_hook):
            for b in range(G):
                pool.wait_ge(a_rope, b + 1)
                pool.tensor_tensor(zq[0:96, NB * b:NB * (b + 1)], rope1[0:96, b % 2], rope2[0:96, b % 2],
                                   ALU.add).then_inc(a_z, 1)
            for n in range(len(QK)):
                a, side, b = QK[n]
                pool.wait_ge(a_mid, n + 1)
                pool.tensor_tensor(parts[0:CP, (n // 4) % 2, 2, NB * b:NB * (b + 1)], resid[0:CP, n % 2],
                                   parts[0:CP, (n // 4) % 2, 1, NB * b:NB * (b + 1)],
                                   ALU.subtract).then_inc(a_lo, 1)
            for n in range(4):
                pool.wait_ge(a_parts[n], 16)
            pool.memset(stack[1][0].bitcast(F32), 0.0)
            pool.memset(stack[1][1].bitcast(F32), 0.0).then_inc(a_zero, 1)
            for n, (g, qb, kt) in enumerate(UNITS):
                if masked[n]:
                    c = first_col(qb, kt)
                    for h in range(2):
                        r = (2 * n + h) % 6
                        pool.wait_ge(a_clip, 2 * n + h + 1)
                        pool.affine_select(out=pring[:, r, :, c:c + P], in_=pring[:, r, :, c:c + P],
                                           compare_op=ALU.is_ge, fill=0.0, base=0,
                                           pattern=[[0, 2], [1, P]], channel_multiplier=-1).then_inc(a_mask, 1)
                loop_hook(n)

        def mla_scalar(act):
            act.wait_ge(a_fold, 3)
            act.wait_ge(a_w2, 96)
            act.activation(m_wab[:, :, 0:HR], bank[0][:, 0:2 * HR].rearrange("p (a n) -> p a n", a=2),
                           ACT.Copy).then_inc(a_folded, 1)
            act.activation(m_wkc, bank[1][:, 0:2 * CP], ACT.Copy).then_inc(a_folded, 1)
            act.activation(m_wv, bank[2][:, 0:P], ACT.Copy).then_inc(a_folded, 1)
            for b in range(G):
                act.wait_ge(a_ab, b + 1)
                act.activation(zq[96:P, NB * b:NB * (b + 1)], bank[2 * (b % 2)][96:P, :], ACT.Copy).then_inc(a_cq, 1)
            for g in range(G):
                act.wait_ge(a_v, g + 1)
                if g == 0:
                    act.wait_ge(a_vzero, 2)
                act.activation(vpad[:, 4 * g:4 * g + 4, :, 0:DH],
                               bank[4 + g % 2][:, :].rearrange("p (t h d) -> p t h d", t=4, h=NH),
                               ACT.Copy).then_inc(a_vcopied, 1)
            for n in range(len(QK)):
                a, side, b = QK[n]
                half = n // 4
                act.wait_ge(a_qk, n + 1)
                if n >= 8 and n % 4 == 0:
                    act.wait_ge(a_parts[half - 2], 16)
                act.activation(parts[0:CP, half % 2, 0, NB * b:NB * (b + 1)], bank[n % 4][0:CP, :],
                               ACT.Copy).then_inc(a_hi, 1)
                act.wait_ge(a_res, n + 1)
                act.activation(parts[0:CP, half % 2, 1, NB * b:NB * (b + 1)], resid[0:CP, n % 2],
                               ACT.Copy).then_inc(a_mid, 1)
            for n, (g, qb, kt) in enumerate(UNITS):
                c = first_col(qb, kt)
                for h in range(2):
                    m = 2 * n + h
                    act.wait_ge(a_scores, m + 1)
                    if m >= 6:
                        act.wait_ge(a_pv, (m - 6) // 2 + 1)
                    act.activation(pring[:, m % 6, :, c:NB], pair[m % 3][:, :, c:NB], ACT.Exp,
                                   scale=float(1.0 / np.sqrt(np.float32(DQK)))).then_inc(a_exp, 1)
            for g in range(G):
                act.wait_ge(a_at, g + 1)
                act.activation(oT[:, g % 2], bank[6 + g % 2][:, :], ACT.Copy).then_inc(a_atc, 1)

        def mla_vector(dve):
            dve.wait_ge(a_w2, 96)
            for b in range(G):
                dve.wait_ge(a_ab, b + 1)
                if b >= 2:
                    dve.wait_ge(a_z, b - 1)
                dve.tensor_tensor(rope1[0:96, b % 2], bank[2 * (b % 2)][0:96, :], cosT[0:96, NB * b:NB * (b + 1)],
                                  ALU.mult)
                dve.tensor_tensor(rope2[0:96, b % 2], bank[2 * (b % 2) + 1][0:96, :],
                                  sinT[0:96, NB * b:NB * (b + 1)], ALU.mult).then_inc(a_rope, 1)
            for n in range(len(QK)):
                a, side, b = QK[n]
                dve.wait_ge(a_hi, n + 1)
                if n >= 2:
                    dve.wait_ge(a_lo, n - 1)
                dve.tensor_tensor(resid[0:CP, n % 2], bank[n % 4][0:CP, :],
                                  parts[0:CP, (n // 4) % 2, 0, NB * b:NB * (b + 1)], ALU.subtract).then_inc(a_res, 1)
            top = float(np.exp(np.float32(CLIP) / np.sqrt(np.float32(DQK))))

            def out_block(j):
                dve.wait_ge(a_pv, last_unit[BLOCKS[j]] + 1)
                if j >= 2:
                    dve.wait_ge(a_turned, j - 1)
                dve.tensor_copy(oT[:, j % 2], bank[6 + j % 2][:, :]).then_inc(a_oT, 1)

            def norm_block(j):
                g, qb = BLOCKS[j]
                o = bank[6 + j % 2][:, :].rearrange("p (i h d) -> p i h d", i=4, h=4)
                dve.wait_ge(a_turned, j + 1)
                dve.reciprocal(rdenA[:, :].rearrange("p (i h) -> p i h", i=4), o[:, :, :, DH]).then_inc(a_rden, 1)
                dve.wait_ge(a_rden, j + 1)
                for i in range(4):
                    ins = dve.tensor_tensor(
                        attn[:, 4 * qb + i, 32 * g:32 * g + 32].rearrange("p (h d) -> p h d", h=4), o[:, i, :, 0:DH],
                        rdenA[:, 4 * i:4 * i + 4].unsqueeze(2).broadcast_to([P, 4, DH]), ALU.mult)
                ins.then_inc(a_norm, 1)

            done = {last_unit[b]: j for j, b in enumerate(BLOCKS)}
            for n, (g, qb, kt) in enumerate(UNITS):
                c = first_col(qb, kt)
                for h in range(2):
                    m = 2 * n + h
                    dve.wait_ge(a_exp, m + 1)
                    dve.tensor_scalar(pring[:, m % 6, :, c:NB], pring[:, m % 6, :, c:NB], 1.0 / top, top,
                                      ALU.max, ALU.min).then_inc(a_clip, 1)
                if n - 3 in done:
                    out_block(done[n - 3])
                if n - 6 in done:
                    norm_block(done[n - 6])
            out_block(len(BLOCKS) - 1)
            norm_block(len(BLOCKS) - 1)
            for g in range(G):
                dve.wait_ge(a_wo, g + 1)
                dve.tensor_tensor(x[:, 4 * g:4 * g + 4, :], bank[g][:, :].rearrange("p (t n) -> p t n", t=4),
                                  x[:, 4 * g:4 * g + 4, :], ALU.add).then_inc(x_ready, 1)

        def mla_tensor(pe):
            pe.wait_ge(a_w, 80)
            pe.matmul(bank[0][:, 0:2 * HR], m_dqT[0:DL, :], m_qr2[0:DL, :]).then_inc(a_fold, 1)
            pe.matmul(bank[1][:, 0:2 * CP], m_dkvT[0:DL, :], m_uk[0:DL, :]).then_inc(a_fold, 1)
            pe.matmul(bank[2][:, 0:P], m_dkvT[0:DL, :], m_uv[0:DL, :]).then_inc(a_fold, 1)
            pe.wait_ge(a_folded, 3)
            for b in range(G):
                pe.wait_ge(ln_xnT, b + 1)
                if b >= 2:
                    pe.wait_ge(a_rope, b - 1)
                    pe.wait_ge(a_cq, b - 1)
                pe.matmul(bank[2 * (b % 2)][:, :], m_wab[:, 0, :], xnT[:, xcol(b)])
                pe.matmul(bank[2 * (b % 2) + 1][:, :], m_wab[:, 1, :], xnT[:, xcol(b)]).then_inc(a_ab, 1)
            for g in range(G):
                if g >= 2:
                    pe.wait_ge(a_vcopied, g - 1)
                for i in range(4):
                    ins = pe.matmul(bank[4 + g % 2][:, P * i:P * (i + 1)], xnT[:, xtile(4 * g + i)], m_wv)
                ins.then_inc(a_v, 1)
            for n in range(len(QK)):
                a, side, b = QK[n]
                if n < 4:
                    pe.wait_ge(a_z, b + 1)
                    pe.wait_ge(a_cq, b + 1)
                if n == 0:
                    pe.wait_ge(a_rope, G)
                    pe.wait_ge(a_cq, G)
                if n >= 4:
                    pe.wait_ge(a_res, n - 3)
                cols = slice(CP * a, CP * (a + 1))
                if side == 0:
                    pe.matmul(bank[n % 4][0:CP, :], m_wq[:, cols], zq[:, NB * b:NB * (b + 1)]).then_inc(a_qk, 1)
                else:
                    pe.matmul(bank[n % 4][0:CP, :], m_wkc[:, cols], xnT[:, xcol(b)], start=True, stop=False)
                    pe.matmul(bank[n % 4][0:CP, :], m_wkr[:, cols], zq[:, NB * b:NB * (b + 1)],
                              start=False, stop=True).then_inc(a_qk, 1)

            def scores(n):
                g, qb, kt = UNITS[n]
                c = first_col(qb, kt)
                if kt == 0 and qb == 0:
                    pe.wait_ge(a_stack[g % 2], 192 * (g // 2 + 1))
                for h in range(2):
                    m = 2 * n + h
                    if m >= 3:
                        pe.wait_ge(a_exp, m - 2)
                    for i in range(2):
                        head = 2 * h + i
                        ins = pe.matmul(pair[m % 3][:, i, c:NB], stack[g % 2][1][:, head, P * kt:P * (kt + 1)],
                                        stack[g % 2][0][:, head, NB * qb + c:NB * (qb + 1)])
                    ins.then_inc(a_scores, 1)

            def values(n):
                g, qb, kt = UNITS[n]
                c = first_col(qb, kt)
                j = BLOCKS.index((g, qb))
                if kt == 0 and j >= 2:
                    pe.wait_ge(a_norm, j - 1)
                pe.wait_ge(a_clip, 2 * n + 2)
                if masked[n]:
                    pe.wait_ge(a_mask, masks_to[n])
                for head in range(4):
                    m = 2 * n + head // 2
                    ins = pe.matmul(bank[6 + j % 2][32 * head:32 * head + 32, c:NB], vpad[:, kt, 4 * g + head, :],
                                    pring[:, m % 6, head % 2, c:NB], start=(kt == 0), stop=(kt == 4 * qb + 3),
                                    tile_position=(0, 32 * head))
                ins.then_inc(a_pv, 1)

            def turn(j):
                pe.wait_ge(a_oT, j + 1)
                for i in range(4):
                    ins = pe.transpose(bank[6 + j % 2][:, P * i:P * (i + 1)], oT[:, j % 2, P * i:P * (i + 1)], ident[:, :])
                ins.then_inc(a_turned, 1)

            done = {last_unit[b]: j for j, b in enumerate(BLOCKS)}
            pe.wait_ge(a_res, len(QK))
            pe.wait_ge(a_vcopied, G)
            for n in range(len(UNITS)):
                scores(n)
                if n >= 2:
                    values(n - 2)
                if n - 5 in done:
                    turn(done[n - 5])
            values(len(UNITS) - 2)
            values(len(UNITS) - 1)
            turn(len(BLOCKS) - 1)
            pe.wait_ge(a_norm, len(BLOCKS))
            for g in range(G):
                if g >= 2:
                    pe.wait_ge(a_atc, g - 1)
                for i in range(4):
                    ins = pe.transpose(bank[6 + g % 2][:, P * i:P * (i + 1)], attn[:, 4 * g + i, :], ident[:, :])
                ins.then_inc(a_at, 1)
                pe.wait_ge(a_atc, g + 1)
                for i in range(4):
                    ins = pe.matmul(bank[g][:, P * i:P * (i + 1)], oT[:, g % 2, P * i:P * (i + 1)], m_wo)
                ins.then_inc(a_wo, 1)


        a_words = arena.at

        f_w12 = arena.take(2, NE + 1, FH)
        f_b12 = arena.take(2, NE + 1, FH)
        f_w3raw = arena.take(5, P)
        f_w3 = arena.take(5, P)
        f_bsel = arena.take(5, NE + 1)
        f_gcol = arena.take(5)
        f_wg = arena.take(NE + 1)
        f_bg = arena.take(NE + 1)
        f_bx = arena.take(NE)
        f_pref = arena.take(NE)
        f_idx = arena.take(2, M + 2, dtype=I32)
        f_notin = arena.take(T)
        f_rcnt = arena.take(2)
        f_scol = arena.take(T)
        f_row = arena.take(M + 2)
        f_scoli = arena.take(T, dtype=I32)
        later_words = arena.at
        arena.at = resid_words
        f_i1, f_i2 = arena.take(2, M + 2), arena.take(M + 2)
        arena.at = resid_words + 2 * NB
        f_srow = arena.take(S)
        f_srowi = f_srow.bitcast(I32)
        rounded.reset()
        f_gtr = rounded.take(T, M)
        f_gmr = rounded.take(2, S)
        f_gt, f_gm = f_gtr.bitcast(F32), f_gmr.bitcast(F32)
        arena.reset()
        keep_words = arena.at
        f_hb = arena.take(T, 2, FH)
        f_sg = arena.take(T, FH)
        f_u = arena.take(T, FH)
        f_st = arena.take(T, 6)
        f_mv = arena.take(T, 2)
        f_rs = arena.take(T)
        f_rv = arena.take(T)
        f_sh = arena.take(T, FH + 1)
        f_shT = arena.take(S)
        f_xm = arena.take(M)
        f_sc = arena.take(24, 2, NE + 1)
        f_hm = arena.take(2, 2, NE + 1, FH)
        f_sm = arena.take(2, NE + 1, FH)
        f_um = arena.take(2, NE + 1, FH)
        f_stm = arena.take(2 * (NE + 1), 6)
        f_mvm = arena.take(2 * (NE + 1), 2)
        f_rsm = arena.take(2, NE + 1)
        f_z = arena.take(2, (NE + 1) * FH + NE + 1)
        f_zT = arena.take(5, M)
        f_moe = arena.take(2, P)
        f_same = arena.take(M)

        f_w = sem("f_w")
        f_c = sem("f_c")
        f_pc = sem("f_pc")
        f_onehot = sem("f_onehot")
        f_prep = sem("f_prep")
        f_fold = sem("f_fold")
        f_hs = sem("f_hs")
        f_hsb = sem("f_hsb")
        f_silu = sem("f_silu")
        f_stat = sem("f_stat")
        f_rstd = sem("f_rstd")
        f_shn = sem("f_shn")
        f_sturn = sem("f_sturn")
        f_sT = sem("f_sT")
        f_gath = sem("f_gath")
        f_xmc = sem("f_xmc")
        f_gate = sem("f_gate")
        f_lg = sem("f_lg")
        f_ex = sem("f_ex")
        f_hid = sem("f_hid")
        f_hmb = sem("f_hmb")
        f_zd = sem("f_zd")
        f_zturn = sem("f_zturn")
        f_zc = sem("f_zc")
        f_mo = sem("f_mo")
        f_moc = sem("f_moc")
        f_out = sem("f_out")
        count = {"f_c": 0, "f_pc": 0, "f_ex": 0, "f_lg": 0}

        def link(eng, s, name, ins):
            count[name] += 1
            ins.then_inc(s, 1)
            eng.wait_ge(s, count[name])

        def ffn_load(sp):
            bc = lambda ap: ap.partition_broadcast(P)
            sp.dma_start(f_w12, I["F_w12"]).then_inc(f_w, 16)
            sp.dma_start(f_b12.rearrange("p a e h -> p (a e h)"), bc(I["F_b12"])).then_inc(f_w, 16)
            sp.dma_start(f_w3raw, I["F_w3"]).then_inc(f_w, 16)
            sp.dma_start(f_bsel, I["F_bsel"]).then_inc(f_w, 16)
            sp.dma_start(f_gcol, I["F_gcol"]).then_inc(f_w, 16)
            sp.dma_start(f_wg, I["F_wg"]).then_inc(f_w, 16)
            sp.dma_start(f_bg, bc(I["F_bg"])).then_inc(f_w, 16)
            sp.dma_start(f_bx, bc(I["F_bx"])).then_inc(f_w, 16)
            sp.dma_start(f_pref, bc(I["F_pref"])).then_inc(f_w, 16)
            for i, name in enumerate(("F_ib", "F_it")):
                sp.dma_start(f_idx[:, i, 0:M], bc(I[name])).then_inc(f_w, 16)
                sp.dma_start(f_idx[:, i, M:M + 2], I[name + "c"]).then_inc(f_w, 16)

        def ffn_rows_gpsimd(pool):
            c = lambda ins: link(pool, f_pc, "f_pc", ins)
            pool.wait_ge(f_w, 13 * 16)
            pool.wait_ge(a_res, len(QK))
            pool.wait_ge(a_z, G)
            c(pool.iota(f_scoli, [[P, T]], base=0, channel_multiplier=1))
            pool.tensor_copy(f_scol, f_scoli)
            c(pool.tensor_copy(f_i1, f_idx))
            pool.tensor_scalar(f_i2, f_i1[:, 1], 0.0, float(S), ALU.is_lt, ALU.mult)
            c(pool.tensor_scalar(f_row, f_i1[:, 0], -1.0, None, ALU.is_equal))
            c(pool.tensor_tensor(f_i2, f_i2, f_i1[:, 1], ALU.add))
            c(pool.tensor_scalar(f_i1[:, 0], f_i1[:, 0], 0.0, None, ALU.is_equal))
            c(pool.tensor_tensor(f_row, f_row, f_i1[:, 0], ALU.add))
            c(pool.tensor_scalar(f_i2, f_i2, 1.0, None, ALU.add))
            c(pool.tensor_tensor(f_i2, f_i2, f_row, ALU.mult))
            c(pool.tensor_scalar(f_row, f_i2, -1.0, None, ALU.add))

        def ffn_tokens_gpsimd(pool):
            c = lambda ins: link(pool, f_pc, "f_pc", ins)
            c(pool.iota(f_srowi, [[1, S]], base=0, channel_multiplier=0))
            c(pool.tensor_copy(f_srow, f_srowi))

        def ffn_onehots_gpsimd(pool, part):
            if part < 2:
                for t in range(8 * part, 8 * part + 8):
                    pool.tensor_scalar(f_gtr[:, t, :], f_row[:, 0:M], f_scol[:, t:t + 1], None, ALU.is_equal)
            else:
                for m in range(2):
                    ins = pool.tensor_scalar(f_gmr[:, m, :], f_srow, f_row[:, M + m:M + m + 1], None, ALU.is_equal)
                ins.then_inc(f_onehot, 1)

        def ffn_prepare_vector(dve):
            c = lambda ins: link(dve, f_c, "f_c", ins)
            dve.wait_ge(f_onehot, 1)
            for kt in range(5):
                ins = dve.tensor_scalar(f_w3[:, kt, :], f_w3raw[:, kt, :], f_gcol[:, kt:kt + 1], None, ALU.mult)
            c(ins)
            dve.wait_ge(f_fold, 1)
            dve.tensor_tensor(f_w3[64:64 + NE + 1, 4, :], bank[5][64:64 + NE + 1, 0:P],
                              f_w3raw[64:64 + NE + 1, 4, :], ALU.add).then_inc(f_prep, 1)

        def ffn_counts_vector(dve):
            c = lambda ins: link(dve, f_c, "f_c", ins)
            for m in range(2):
                c(dve.tensor_scalar(f_same, f_row[:, 0:M], f_row[:, M + m:M + m + 1], None, ALU.is_equal))
                c(dve.tensor_reduce(f_rcnt[:, m:m + 1], f_same, AX.X, ALU.add))
            c(dve.reciprocal(f_rcnt, f_rcnt))
            c(dve.tensor_reduce(f_notin, f_gt, AX.X, ALU.max))
            dve.tensor_scalar(f_notin, f_notin, -1.0, 1.0, ALU.mult, ALU.add).then_inc(f_prep, 1)

        def ffn_gpsimd(pool, rep):
            k = 2 * rep + 1
            if rep == 0:
                pool.wait_ge(f_prep, 2)
            c = lambda ins: link(pool, f_pc, "f_pc", ins)
            pool.wait_ge(f_stat, 2 * rep + 1)
            c(pool.tensor_scalar(f_rv, f_mv[:, :, 1], EPS, None, ALU.add))
            c(pool.tensor_tensor(f_rs, f_rv, mhalf[:, 0:T], ALU.pow))
            pool.tensor_tensor(f_rs, f_rs, f_notin, ALU.mult).then_inc(f_rstd, 1)
            pool.wait_ge(f_stat, 2 * rep + 2)
            mvm = f_mvm[:, :, 1]
            flat = f_rsm.rearrange("p m e -> p (m e)")
            c(pool.tensor_scalar(flat, mvm, EPS, None, ALU.add))
            c(pool.tensor_tensor(flat, flat, mhalf[:, 0:2 * (NE + 1)], ALU.pow))
            pool.tensor_tensor(f_rsm, f_rsm, f_sc[:, FAC], ALU.mult).then_inc(f_rstd, 1)

        def ffn_scalar(act, rep):
            act.wait_ge(f_gath, rep + 1)
            act.activation(f_xm, bank[4][:, 0:M], ACT.Copy).then_inc(f_xmc, 1)
            act.wait_ge(f_lg, 2 * rep + 1)
            act.activation(f_sc[:, 1], f_sc[:, 0], ACT.Exp, scale=-1.0).then_inc(f_ex, 1)
            act.wait_ge(f_lg, 2 * rep + 2)
            act.activation(f_sc[:, 12, :, 0:2], f_sc[:, 11, :, 0:2], ACT.Exp).then_inc(f_ex, 1)
            for g in range(G):
                act.wait_ge(f_hsb, 4 * rep + g + 1)
                act.activation(f_sg[:, 4 * g:4 * g + 4, :], f_hb[:, 4 * g:4 * g + 4, 0, :], ACT.Silu
                               ).then_inc(f_silu, 1)
            for m in range(2):
                act.wait_ge(f_hmb, 2 * rep + m + 1)
                act.activation(f_sm[:, m], f_hm[:, m, 0], ACT.Silu).then_inc(f_silu, 1)
            for g in range(G):
                act.wait_ge(f_sturn, 4 * rep + g + 1)
                act.activation(f_shT[0:FH + 1, NB * g:NB * (g + 1)], bank[6 + g % 2][0:FH + 1, :], ACT.Copy
                               ).then_inc(f_sT, 1)
            act.wait_ge(f_zturn, rep + 1)
            for kt in range(4):
                act.activation(f_zT[:, kt, :], bank[kt // 2][:, M * (kt % 2):M * (kt % 2 + 1)], ACT.Copy)
            act.activation(f_zT[0:FH + NE + 1, 4, :], bank[4][0:FH + NE + 1, 0:M], ACT.Copy).then_inc(f_zc, 1)
            act.wait_ge(f_mo, rep + 1)
            act.activation(f_moe, bank[5][:, 0:2 * P].rearrange("p (m n) -> p m n", m=2), ACT.Copy
                           ).then_inc(f_moc, 1)

        LOG, SIG, BIA, FAC = 0, 3, 4, 20

        def ffn_vector(dve, rep):
            c = lambda ins: link(dve, f_c, "f_c", ins)
            if rep == 0:
                ffn_prepare_vector(dve)
            for g in range(G):
                dve.wait_ge(f_hs, 4 * rep + g + 1)
                dve.tensor_tensor(f_hb[:, 4 * g:4 * g + 4], bank[g][:, :].rearrange("p (t a h) -> p t a h", t=4, a=2),
                                  f_b12[:, :, NE, :].unsqueeze(1).broadcast_to([P, 4, 2, FH]), ALU.add
                                  ).then_inc(f_hsb, 1)
            if rep == 0:
                ffn_counts_vector(dve)
            sc = f_sc
            dve.wait_ge(f_gate, rep + 1)
            dve.tensor_tensor(sc[:, LOG], bank[5][:, 0:2 * (NE + 1)].rearrange("p (m e) -> p m e", m=2),
                              f_bg.unsqueeze(1).broadcast_to([P, 2, NE + 1]), ALU.add).then_inc(f_lg, 1)
            dve.wait_ge(f_ex, 2 * rep + 1)
            c(dve.tensor_scalar(sc[:, 2], sc[:, 1], 1.0, None, ALU.add))
            c(dve.reciprocal(sc[:, SIG], sc[:, 2]))
            c(dve.tensor_tensor(sc[:, BIA, :, 0:NE], sc[:, SIG, :, 0:NE], f_bx.unsqueeze(1).broadcast_to([P, 2, NE]), ALU.add))
            c(dve.tensor_reduce(sc[:, 5, :, 0], sc[:, BIA, :, 0:NE], AX.X, ALU.max))
            c(dve.tensor_tensor(sc[:, 6, :, 0:NE], sc[:, BIA, :, 0:NE], sc[:, 5, :, 0:1].broadcast_to([P, 2, NE]), ALU.is_equal))
            c(dve.tensor_tensor(sc[:, 7, :, 0:NE], sc[:, 6, :, 0:NE], f_pref.unsqueeze(1).broadcast_to([P, 2, NE]), ALU.mult))
            c(dve.tensor_reduce(sc[:, 8, :, 0], sc[:, 7, :, 0:NE], AX.X, ALU.max))
            c(dve.tensor_tensor(sc[:, 9, :, 0:NE], sc[:, 7, :, 0:NE], sc[:, 8, :, 0:1].broadcast_to([P, 2, NE]), ALU.is_equal))
            c(dve.tensor_tensor(sc[:, 10, :, 0:NE], sc[:, 9, :, 0:NE], sc[:, SIG, :, 0:NE], ALU.mult))
            dve.tensor_copy(sc[:, 11, :, 0:1], sc[:, SIG, :, NE:NE + 1])
            c(dve.tensor_reduce(sc[:, 11, :, 1], sc[:, 10, :, 0:NE], AX.X, ALU.add))
            dve.tensor_copy(sc[:, 13, :, 0:1], sc[:, 11, :, 0:1]).then_inc(f_lg, 1)
            dve.wait_ge(f_ex, 2 * rep + 2)
            c(dve.tensor_reduce(sc[:, 14, :, 0], sc[:, 12, :, 0:2], AX.X, ALU.add))
            c(dve.reciprocal(sc[:, 15, :, 0], sc[:, 14, :, 0]))
            c(dve.tensor_tensor(sc[:, 16, :, 0], sc[:, 15, :, 0], f_rcnt, ALU.mult))
            c(dve.tensor_tensor(sc[:, 17, :, 0:2], sc[:, 12, :, 0:2], sc[:, 16, :, 0:1].broadcast_to([P, 2, 2]), ALU.mult))
            dve.tensor_copy(sc[:, FAC, :, NE:NE + 1], sc[:, 17, :, 0:1])
            c(dve.tensor_tensor(sc[:, FAC, :, 0:NE], sc[:, 9, :, 0:NE], sc[:, 17, :, 1:2].broadcast_to([P, 2, NE]), ALU.mult))
            for m in range(2):
                for a in range(2):
                    dve.wait_ge(f_hid, 4 * rep + 2 * m + a + 1)
                    dve.tensor_tensor(f_hm[:, m, a, 0:NE, :], bank[2 * m + a][:, :].rearrange("p (e h) -> p e h", e=NE),
                                      f_b12[:, a, 0:NE, :], ALU.add)
                dve.tensor_tensor(f_hm[:, m, :, NE, :], bank[5][:, 256 + 128 * m:384 + 128 * m].rearrange("p (a h) -> p a h", a=2),
                                  f_b12[:, :, NE, :], ALU.add).then_inc(f_hmb, 1)
            for g in range(G):
                dve.wait_ge(f_silu, 6 * rep + g + 1)
                ins = dve.tensor_tensor(f_u[:, 4 * g:4 * g + 4, :], f_sg[:, 4 * g:4 * g + 4, :],
                                        f_hb[:, 4 * g:4 * g + 4, 1, :], ALU.mult)
            c(ins)
            for t in range(T):
                ins = dve.bn_stats(f_st[:, t, :], f_u[:, t, :])
            c(ins)
            for t in range(T):
                ins = dve.bn_aggr(f_mv[:, t, :], f_st[:, t, :])
            ins.then_inc(f_stat, 1)
            for m in range(2):
                dve.wait_ge(f_silu, 6 * rep + 4 + m + 1)
                ins = dve.tensor_tensor(f_um[:, m], f_sm[:, m], f_hm[:, m, 1], ALU.mult)
            c(ins)
            for n in range(2 * (NE + 1)):
                ins = dve.bn_stats(f_stm[:, n, :], f_um[:, n // (NE + 1), n % (NE + 1), :])
            c(ins)
            for n in range(2 * (NE + 1)):
                ins = dve.bn_aggr(f_mvm[:, n, :], f_stm[:, n, :])
            ins.then_inc(f_stat, 1)
            dve.wait_ge(f_rstd, 2 * rep + 1)
            dve.tensor_copy(f_sh[:, :, FH:FH + 1], f_notin.unsqueeze(2))
            for t in range(T):
                ins = dve.tensor_scalar(f_sh[:, t, 0:FH], f_u[:, t, :], f_mv[:, t, 0:1], f_rs[:, t:t + 1],
                                        ALU.subtract, ALU.mult)
                if t % 4 == 3:
                    ins.then_inc(f_shn, 1)
            dve.wait_ge(f_rstd, 2 * rep + 2)
            for m in range(2):
                for e in range(NE + 1):
                    n = m * (NE + 1) + e
                    dve.tensor_scalar(f_z[:, m, FH * e:FH * (e + 1)], f_um[:, m, e, :], f_mvm[:, n, 0:1],
                                      f_rsm[:, m, e:e + 1], ALU.subtract, ALU.mult)
                dve.tensor_copy(f_z[:, m, FH * (NE + 1):FH * (NE + 1) + 1], sc[:, FAC, m, NE:NE + 1])
                ins = dve.tensor_copy(f_z[:, m, FH * (NE + 1) + 1:], sc[:, FAC, m, 0:NE])
            ins.then_inc(f_zd, 1)
            for g in range(G):
                dve.wait_ge(f_out, 4 * rep + g + 1)
                dve.tensor_tensor(x[:, 4 * g:4 * g + 4, :], bank[g][:, :].rearrange("p (t n) -> p t n", t=4),
                                  x[:, 4 * g:4 * g + 4, :], ALU.add).then_inc(x_ready, 1)

        def ffn_tensor(pe, rep):
            k = 2 * rep + 1
            if rep == 0:
                pe.wait_ge(f_w, 13 * 16)
                for kt in range(5):
                    rows = P if kt < 4 else FH
                    ins = pe.matmul(bank[5][64:64 + NE + 1, 0:P], f_bsel[0:rows, kt, :], f_w3raw[0:rows, kt, :],
                                    start=(kt == 0), stop=(kt == 4), tile_position=(0, 64))
                ins.then_inc(f_fold, 1)
            for g in range(G):
                pe.wait_ge(ln_xnT, 4 * k + g + 1)
                for i in range(4):
                    ins = pe.matmul(bank[g][:, P * i:P * (i + 1)], xnT[:, xtile(4 * g + i)], f_w12[:, :, NE, :])
                ins.then_inc(f_hs, 1)
            if rep == 0:
                pe.wait_ge(f_onehot, 1)
            for t in range(T):
                ins = pe.matmul(bank[4][:, 0:M], xn[:, t, :], f_gt[:, t, :], start=(t == 0), stop=(t == T - 1))
            ins.then_inc(f_gath, 1)
            pe.wait_ge(f_xmc, rep + 1)
            if rep == 0:
                pe.wait_ge(f_prep, 1)
            for m in range(2):
                pe.matmul(bank[5][:, (NE + 1) * m:(NE + 1) * (m + 1)], f_xm[:, P * m:P * (m + 1)], f_wg)
                ins = pe.matmul(bank[5][:, 256 + 128 * m:384 + 128 * m], f_xm[:, P * m:P * (m + 1)], f_w12[:, :, NE, :])
            ins.then_inc(f_gate, 1)
            for m in range(2):
                for a in range(2):
                    pe.wait_ge(f_hsb, 4 * rep + 2 * m + a + 1)
                    pe.matmul(bank[2 * m + a][:, :], f_xm[:, P * m:P * (m + 1)],
                              f_w12[:, a, 0:NE, :]).then_inc(f_hid, 1)
            for g in range(G):
                pe.wait_ge(f_shn, 4 * rep + g + 1)
                if g >= 2:
                    pe.wait_ge(f_sT, 4 * rep + g - 1)
                for i in range(4):
                    ins = pe.transpose(bank[6 + g % 2][0:FH + 1, P * i:P * (i + 1)], f_sh[:, 4 * g + i, :], ident[:, :])
                ins.then_inc(f_sturn, 1)
            pe.wait_ge(f_zd, rep + 1)
            for m in range(2):
                for kt in range(4):
                    pe.transpose(bank[kt // 2][:, M * (kt % 2) + P * m:M * (kt % 2) + P * (m + 1)],
                                 f_z[:, m, P * kt:P * (kt + 1)], ident[:, :])
                ins = pe.transpose(bank[4][0:FH + NE + 1, P * m:P * (m + 1)], f_z[:, m, 4 * P:], ident[:, :])
            ins.then_inc(f_zturn, 1)
            pe.wait_ge(f_zc, rep + 1)
            for m in range(2):
                for kt in range(5):
                    rows = P if kt < 4 else FH + NE + 1
                    ins = pe.matmul(bank[5][:, P * m:P * (m + 1)], f_zT[0:rows, kt, P * m:P * (m + 1)],
                                    f_w3[0:rows, kt, :], start=(kt == 0), stop=(kt == 4))
            ins.then_inc(f_mo, 1)
            pe.wait_ge(f_moc, rep + 1)
            for g in range(G):
                pe.wait_ge(f_sT, 4 * rep + g + 1)
                for i in range(4):
                    t = 4 * g + i
                    o = bank[g][:, P * i:P * (i + 1)]
                    pe.matmul(o, f_shT[0:FH + 1, P * t:P * (t + 1)], f_w3[0:FH + 1, 4, :], start=True, stop=False)
                    pe.matmul(o, f_gm[:, 0, P * t:P * (t + 1)], f_moe[:, 0, :], start=False, stop=False)
                    ins = pe.matmul(o, f_gm[:, 1, P * t:P * (t + 1)], f_moe[:, 1, :], start=False, stop=True)
                ins.then_inc(f_out, 1)


        arena.at = later_words
        b_ww, b_wr = arena.take(P), arena.take(P)
        b_in = arena.take(2)
        b_sm = arena.take(8)
        later_words2 = arena.at
        arena.at = keep_words
        b_expo = arena.take(2 * P + 2)
        b_expoi = arena.take(2 * P + 2, dtype=I32)
        b_pow = arena.take(2 * P + 2)
        b_wv = arena.take(P)
        b_v = arena.take(T, P)
        b_wtok = arena.take(T, P)
        b_sm2 = arena.take(T, P)
        b_xdec = arena.take(T, P)
        b_state = arena.take(T, P)

        b_w = sem("b_w")
        b_iota = sem("b_iota")
        b_c = sem("b_c")
        b_s = sem("b_s")
        b_powd = sem("b_powd")
        b_mask = sem("b_mask")
        b_fold = sem("b_fold")
        b_wvd = sem("b_wvd")
        b_vm = sem("b_vm")
        b_vc = sem("b_vc")
        b_wt = sem("b_wt")
        b_wtc = sem("b_wtc")
        b_scm = sem("b_scm")
        b_smd = sem("b_smd")
        b_um = sem("b_um")
        b_st = sem("b_st")
        b_xd = sem("b_xd")
        b_xz = sem("b_xz")
        b_out = sem("b_out")
        count["b_c"] = 0

        def shifted(t):
            return slice(XO - 1 + P * t, XO - 1 + P * (t + 1))

        def dla_load(sp):
            sp.dma_start(b_ww, I["B_ww"]).then_inc(b_w, 16)
            sp.dma_start(b_wr, I["B_wrT"]).then_inc(b_w, 16)
            sp.dma_start(b_in[:, 0:1], I["B_decay"].partition_broadcast(P)).then_inc(b_w, 16)
            sp.dma_start(b_in[:, 1:2], I["B_la"].partition_broadcast(P)).then_inc(b_w, 16)

        def dla_gpsimd(pool):
            pool.wait_ge(x_ready, 8)
            pool.iota(b_expoi[:, 0:P], [[1, P]], base=-1, channel_multiplier=-1)
            pool.iota(b_expoi[:, P:2 * P], [[1, P]], base=0, channel_multiplier=0)
            pool.iota(b_expoi[:, 2 * P:2 * P + 1], [[1, 1]], base=P - 1, channel_multiplier=-1)
            pool.iota(b_expoi[:, 2 * P + 1:2 * P + 2], [[1, 1]], base=P, channel_multiplier=0).then_inc(b_iota, 1)
            pool.wait_ge(b_powd, 1)
            pool.affine_select(out=b_pow[:, 0:P], in_=b_pow[:, 0:P], compare_op=ALU.is_ge, fill=0.0, base=-1,
                               pattern=[[1, P]], channel_multiplier=-1).then_inc(b_mask, 1)
            for g in range(G):
                pool.wait_ge(ln_xnT, 8 + g + 1)
                pool.tensor_tensor(b_xdec[:, 4 * g:4 * g + 4, :], xnT[:, xcol(g)].rearrange("p (t n) -> p t n", t=4),
                                   b_pow[:, P:2 * P].unsqueeze(1).broadcast_to([P, 4, P]), ALU.mult).then_inc(b_xd, 1)

        def dla_scalar(act):
            act.wait_ge(b_st, 1)
            act.activation(b_sm[:, 2:3], b_sm[:, 1:2], ACT.Exp, scale=-1.0).then_inc(b_s, 1)
            act.activation(b_sm[:, 6:7], b_in[:, 1:2], ACT.Exp).then_inc(b_s, 1)
            act.wait_ge(b_s, 2)
            act.activation(b_sm[:, 3:4], b_sm[:, 2:3], ACT.Ln, bias=1.0).then_inc(b_s, 1)
            act.wait_ge(b_st, 2)
            act.activation(b_pow, b_expo, ACT.Exp, scale=b_sm[:, 4:5]).then_inc(b_powd, 1)
            for g in range(G):
                act.wait_ge(b_vm, g + 1)
                act.activation(b_v[:, 4 * g:4 * g + 4, :], bank[g][:, :].rearrange("p (t n) -> p t n", t=4), ACT.Copy
                               ).then_inc(b_vc, 1)

        def dla_vector(dve):
            c = lambda ins: link(dve, b_c, "b_c", ins)
            dve.wait_ge(b_w, 64)
            c(dve.tensor_scalar(b_sm[:, 0:1], b_in[:, 0:1], -1.0, None, ALU.mult))
            dve.tensor_tensor(b_sm[:, 1:2], b_sm[:, 0:1], b_in[:, 0:1], ALU.max).then_inc(b_st, 1)
            dve.wait_ge(b_iota, 1)
            c(dve.tensor_scalar(b_expo, b_expoi, 0.0, None, ALU.max))
            dve.wait_ge(b_s, 3)
            dve.scalar_tensor_tensor(b_sm[:, 4:5], b_in[:, 0:1], 0.0, b_sm[:, 3:4], ALU.min, ALU.subtract
                                     ).then_inc(b_st, 1)
            dve.wait_ge(b_fold, 1)
            dve.tensor_scalar(b_wv, bank[0][:, 0:P], b_sm[:, 6:7], None, ALU.mult).then_inc(b_wvd, 1)
            dve.memset(b_state[:, 0, :], 0.0)
            dve.wait_ge(b_powd, 1)
            for g in range(G):
                dve.wait_ge(b_wt, g + 1)
                dve.tensor_scalar(b_wtok[:, 4 * g:4 * g + 4, :], bank[4 + g % 2][:, :].rearrange("p (t n) -> p t n", t=4),
                                  b_pow[:, 2 * P:2 * P + 1], None, ALU.mult).then_inc(b_wtc, 1)
            dve.wait_ge(b_mask, 1)
            for g in range(G):
                dve.wait_ge(b_scm, g + 1)
                dve.tensor_tensor(b_sm2[:, 4 * g:4 * g + 4, :], bank[g][:, :].rearrange("p (t n) -> p t n", t=4),
                                  b_pow[:, 0:P].unsqueeze(1).broadcast_to([P, 4, P]), ALU.mult).then_inc(b_smd, 1)
            for t in range(T - 1):
                dve.wait_ge(b_um, t // 4 + 1)
                ins = dve.scalar_tensor_tensor(b_state[:, t + 1, :], b_state[:, t, :], b_pow[:, 2 * P + 1:2 * P + 2],
                                               bank[4 + t // 4][:, P * (t % 4):P * (t % 4 + 1)], ALU.mult, ALU.add)
                ins.then_inc(b_st, 1)
                dve.wait_ge(b_st, 2 + t + 1)
            for g in range(G):
                xg = x[:, 4 * g:4 * g + 4, :]
                c(dve.tensor_tensor(xg, xg, xn[:, 4 * g:4 * g + 4, :], ALU.add))
            for g in range(G):
                xg = x[:, 4 * g:4 * g + 4, :]
                dve.wait_ge(b_out, g + 1)
                dve.tensor_tensor(xg, bank[g][:, :].rearrange("p (t n) -> p t n", t=4), xg, ALU.add
                                  ).then_inc(x_ready, 1)

        def dla_tensor(pe):
            pe.wait_ge(b_w, 64)
            pe.matmul(bank[0][:, 0:P], b_ww, b_wr).then_inc(b_fold, 1)
            pe.wait_ge(b_wvd, 1)
            for g in range(G):
                pe.wait_ge(ln_xnT, 8 + g + 1)
                for i in range(4):
                    ins = pe.matmul(bank[g][:, P * i:P * (i + 1)], xnT[:, xtile(4 * g + i)], b_wv)
                ins.then_inc(b_vm, 1)
                if g >= 2:
                    pe.wait_ge(b_wtc, g - 1)
                for i in range(4):
                    ins = pe.transpose(bank[4 + g % 2][:, P * i:P * (i + 1)], xnT[:, shifted(4 * g + i)], ident[:, :])
                ins.then_inc(b_wt, 1)
            for g in range(G):
                pe.wait_ge(b_vc, g + 1)
                for i in range(4):
                    t = 4 * g + i
                    ins = pe.matmul(bank[g][:, P * i:P * (i + 1)], xnT[:, shifted(t)], xnT[:, xtile(t)])
                ins.then_inc(b_scm, 1)
            pe.wait_ge(b_wtc, G)
            for g in range(G):
                for i in range(4):
                    t = 4 * g + i
                    ins = pe.matmul(bank[4 + g][:, P * i:P * (i + 1)], b_wtok[:, t, :], b_v[:, t, :])
                ins.then_inc(b_um, 1)
            for g in range(G):
                pe.wait_ge(b_smd, g + 1)
                pe.wait_ge(b_xd, g + 1)
                pe.wait_ge(b_st, 2 + min(4 * g + 3, T - 1))
                for i in range(4):
                    t = 4 * g + i
                    o = bank[g][:, P * i:P * (i + 1)]
                    pe.matmul(o, b_sm2[:, t, :], b_v[:, t, :], start=True, stop=(t == 0))
                    if t:
                        ins = pe.matmul(o, b_xdec[:, t, :], b_state[:, t, :], start=False, stop=True)
                ins.then_inc(b_out, 1)


        arena.at = later_words2
        c_wnat = arena.take(2, NH // 2, P)
        d_w = arena.take(4, P)
        arena.at = LATER_AT
        g_w13 = arena.take(2, NX, GI)
        g_w2 = arena.take(NX, 2, P)
        g_gw = arena.take(NE)
        g_gb = arena.take(NE)
        g_pref = arena.take(NE)
        c_wvT = arena.take(NH, CE)
        c_woT = arena.take(NH // 2, P)
        c_bo = arena.take(P)
        assert arena.at <= a_words, (arena.at, a_words)
        later_load = sem("later_load")
        qk_load = sem("qk_load")

        def later_weights(sp):
            sp.wait_ge(x_ready, 4)
            sp.dma_start(c_wnat, I["C_wnat"]).then_inc(later_load, 16)
            sp.dma_start(c_wvT, I["C_wvT"]).then_inc(later_load, 16)
            sp.dma_start(c_woT, I["C_woT"]).then_inc(later_load, 16)
            sp.dma_start(c_bo, I["C_bo"].partition_broadcast(P)).then_inc(later_load, 16)
            sp.dma_start(g_w13, I["G_w13"]).then_inc(later_load, 16)
            sp.dma_start(g_w2, I["G_w2"]).then_inc(later_load, 16)
            sp.dma_start(g_gw, I["G_gw"]).then_inc(later_load, 16)
            sp.dma_start(g_gb, I["G_gb"].partition_broadcast(P)).then_inc(later_load, 16)
            sp.dma_start(g_pref, I["F_pref"].partition_broadcast(P)).then_inc(later_load, 16)
            sp.dma_start(d_w, I["D_w"]).then_inc(later_load, 16)
            sp.wait_ge(x_ready, 16)
            sp.dma_start(c_wqkT, I["C_wqkT"]).then_inc(qk_load, 16)
        LATER = 160

        arena.reset()
        c_wqkT = arena.take(2, NH * CD)
        c_as = arena.take(NH, P)
        c_sq = arena.take(2, NH * CD)
        c_n2 = arena.take(T, 2 * NH)
        c_mx = arena.take(2 * NH)
        c_r = arena.take(4)
        c_diag = arena.take(2 * NH)
        c_rr = arena.take(2 * NH)
        c_ch = arena.take(NH)
        c_ones = arena.take(P)
        c_mask = arena.take(P)
        c_cnt = arena.take(T)
        c_cnti = arena.take(T, dtype=I32)
        c_cum = arena.take(S)
        c_zero = arena.take(S)
        c_v = arena.take(2, NH, CE)
        c_a = arena.take(NH, P)
        c_s = arena.take(NH, P)
        c_kv = arena.take(NH, CE)
        c_vh = arena.take(NH, CD)
        c_vhT = arena.take(NH // 2, P)
        c_den = arena.take(NH)
        c_rden = arena.take(NH)
        assert arena.at <= LATER_AT, arena.at

        c_c = sem("c_c")
        c_pc = sem("c_pc")
        c_consts = sem("c_consts")
        c_qk = sem("c_qk")
        c_sqd = sem("c_sqd")
        c_n2d = sem("c_n2d")
        c_mxd = sem("c_mxd")
        c_mxt = sem("c_mxt")
        c_mxr = sem("c_mxr")
        c_rd = sem("c_rd")
        c_dg = sem("c_dg")
        c_bc = sem("c_bc")
        c_am = sem("c_am")
        c_asd = sem("c_asd")
        c_apm = sem("c_apm")
        c_apc = sem("c_apc")
        c_vm = sem("c_vm")
        c_vc = sem("c_vc")
        c_scm = sem("c_scm")
        c_scd = sem("c_scd")
        c_num = sem("c_num")
        c_vhd = sem("c_vhd")
        c_kvm = sem("c_kvm")
        c_kvd = sem("c_kvd")
        c_tr = sem("c_tr")
        c_trc = sem("c_trc")
        c_out = sem("c_out")
        c_xadd = sem("c_xadd")
        count["c_c"] = 0

        def cla_gpsimd(pool):
            pool.wait_ge(x_ready, 16)
            pool.memset(c_ones, 1.0)
            pool.memset(c_zero, 0.0)
            pool.memset(c_mask, 1.0)
            pool.iota(c_cnti, [[P, T]], base=1, channel_multiplier=1)
            pool.memset(c_v, 1.0).then_inc(c_consts, 1)
            pool.wait_ge(c_consts, 1)
            pool.affine_select(out=c_mask, in_=c_mask, compare_op=ALU.is_ge, fill=0.0, base=0,
                               pattern=[[1, P]], channel_multiplier=-1).then_inc(c_consts, 1)
            pool.wait_ge(c_mxr, 1)
            pool.tensor_tensor(c_r[0:2 * NH, 1:2], c_r[0:2 * NH, 0:1], mhalf[0:2 * NH, 0:1], ALU.pow).then_inc(c_rd, 1)

        def cla_scalar(act):
            for n in range(2 * T):
                act.wait_ge(c_qk, n + 1)
                if n >= 2:
                    act.wait_ge(c_n2d, n - 1)
                act.activation(c_sq[:, n % 2, :].rearrange("p (a n) -> p a n", a=2), pair[n % 4][:, :, :], ACT.Square
                               ).then_inc(c_sqd, 1)
            for t in range(T):
                for i in range(4):
                    act.wait_ge(c_apm, 4 * t + i + 1)
                    if t:
                        act.wait_ge(c_num, 4 * t)
                    act.activation(c_a[:, 4 * i:4 * i + 4, :], bank[i].rearrange("p (h n) -> p h n", h=4), ACT.Copy
                                   ).then_inc(c_apc, 1)
                act.wait_ge(c_vm, t + 1)
                if t >= 2:
                    act.wait_ge(c_kvm, 4 * (t - 1))
                act.activation(c_v[:, t % 2, :, 0:CD], pair[2][:, :, :].rearrange("p a (h d) -> p (a h) d", d=CD),
                               ACT.Copy).then_inc(c_vc, 1)
                act.wait_ge(c_tr, t + 1)
                if t:
                    act.wait_ge(c_out, t)
                act.activation(c_vhT.rearrange("p (a h) n -> p a (h n)", a=2), pair[2][:, :, :], ACT.Copy
                               ).then_inc(c_trc, 1)

        def cla_vector(dve):
            c = lambda ins: link(dve, c_c, "c_c", ins)
            dve.wait_ge(later_load, LATER)
            dve.wait_ge(c_consts, 2)
            dve.wait_ge(ln_xn, 20)
            for g in range(G):
                xg = x[:, 4 * g:4 * g + 4, :]
                dve.tensor_tensor(xg, xg, c_bo.unsqueeze(1).broadcast_to([P, 4, P]), ALU.add)
            dve.tensor_copy(c_cnt, c_cnti)
            dve.memset(c_kv, 0.0)
            dve.wait_ge(ln_xnT, 20)
            c(dve.tensor_tensor_scan(c_cum, xnT[:, XO:XO + S], c_zero, 0.0, ALU.add, ALU.add))
            for n in range(2 * T):
                dve.wait_ge(c_sqd, n + 1)
                t, side = divmod(n, 2)
                dve.tensor_reduce(c_n2[:, t, NH * side:NH * (side + 1)],
                                  c_sq[:, n % 2, :].rearrange("p (h d) -> p h d", d=CD), AX.X, ALU.add
                                  ).then_inc(c_n2d, 1)
            dve.wait_ge(c_n2d, 2 * T)
            dve.tensor_reduce(c_mx, c_n2.rearrange("p t h -> p h t"), AX.X, ALU.max).then_inc(c_mxd, 1)
            dve.wait_ge(c_mxt, 1)
            dve.tensor_reduce(c_r[0:2 * NH, 0:1], bank[4][0:2 * NH, 0:P], AX.X, ALU.max).then_inc(c_mxr, 1)
            dve.wait_ge(c_rd, 1)
            dve.tensor_scalar(c_diag[0:2 * NH, :], ident[0:2 * NH, 0:2 * NH], c_r[0:2 * NH, 1:2], None, ALU.mult
                              ).then_inc(c_dg, 1)
            dve.wait_ge(c_bc, 1)
            c(dve.tensor_copy(c_rr, bank[4][:, 128:128 + 2 * NH]))
            c(dve.tensor_tensor(c_ch, c_rr[:, 0:NH], c_rr[:, NH:2 * NH], ALU.mult))
            for i in range(4):
                dve.wait_ge(c_am, i + 1)
                hs = c_as.rearrange("p (a j o) n -> p a j o n", a=2, o=2)[:, i % 2, :, i // 2, :]
                ch = c_ch.rearrange("p (a j o) -> p a j o", a=2, o=2)[:, i % 2, :, i // 2]
                dve.tensor_tensor(hs, bank[i].rearrange("p (h n) -> p h n", h=4),
                                  ch.unsqueeze(2).broadcast_to([P, 4, P]), ALU.mult).then_inc(c_asd, 1)
            for t in range(T):
                for i in range(4):
                    dve.wait_ge(c_scm, 4 * t + i + 1)
                    if t:
                        dve.wait_ge(c_num, 4 * t)
                    dve.tensor_tensor(c_s[:, 4 * i:4 * i + 4, :], bank[i].rearrange("p (h n) -> p h n", h=4),
                                      c_mask.unsqueeze(1).broadcast_to([P, 4, P]), ALU.mult).then_inc(c_scd, 1)
                for i in range(4):
                    hs = slice(4 * i, 4 * i + 4)
                    o = bank[NUMBANK[i]][:, 0:4 * CE].rearrange("p (h d) -> p h d", h=4)
                    dve.wait_ge(c_num, 4 * t + i + 1)
                    if t:
                        dve.wait_ge(c_tr, t)
                    c(dve.tensor_scalar(c_den[:, hs], o[:, :, CD], c_cnt[:, t:t + 1], None, ALU.add))
                    c(dve.reciprocal(c_rden[:, hs], c_den[:, hs]))
                    dve.tensor_tensor(c_vh[:, hs, :], o[:, :, 0:CD], c_rden[:, hs].unsqueeze(2).broadcast_to([P, 4, CD]),
                                      ALU.mult).then_inc(c_vhd, 1)
                if t < T - 1:
                    for i in range(4):
                        hs = slice(4 * i, 4 * i + 4)
                        dve.wait_ge(c_kvm, 4 * t + i + 1)
                        if t:
                            dve.wait_ge(c_kvd, 4 * t)
                        dve.tensor_tensor(c_kv[:, hs, :], bank[i][:, 0:4 * CE].rearrange("p (h d) -> p h d", h=4),
                                          c_kv[:, hs, :], ALU.add).then_inc(c_kvd, 1)
                dve.wait_ge(c_out, t + 1)
                ins = dve.tensor_tensor(x[:, t, :], bank[6][:, 0:P], x[:, t, :], ALU.add)
                ins.then_inc(x_ready if t % 4 == 3 else c_xadd, 1)
                if t % 4 == 3:
                    ln_follow(dve, 5, t // 4)

        def cla_added(engine, t):
            if t % 4 == 3:
                engine.wait_ge(x_ready, 16 + t // 4 + 1)
            else:
                engine.wait_ge(c_xadd, 3 * (t // 4) + t % 4 + 1)

        NUMBANK = [6, 7, 4, 5]

        def cla_tensor(pe):
            pe.wait_ge(later_load, LATER)
            pe.wait_ge(qk_load, 16)
            pe.wait_ge(ln_xnT, 20)
            for n in range(2 * T):
                t, side = divmod(n, 2)
                if n >= 4:
                    pe.wait_ge(c_sqd, n - 3)
                for a in range(2):
                    ins = pe.matmul(pair[n % 4][:, a, :], xnT[:, xtile(t)], c_wqkT[:, side, NB * a:NB * (a + 1)])
                ins.then_inc(c_qk, 1)
            pe.wait_ge(c_sqd, 2 * T)
            for i in range(4):
                rows = slice(CD * (i // 2), CD * (i // 2 + 1))
                for j in range(4):
                    ins = pe.matmul(bank[i][:, P * j:P * (j + 1)], c_wnat[rows, 0, 4 * (i % 2) + j, :],
                                    c_wnat[rows, 1, 4 * (i % 2) + j, :])
                ins.then_inc(c_am, 1)
            pe.wait_ge(c_mxd, 1)
            pe.transpose(bank[4][0:2 * NH, 0:P], c_mx, ident[:, :]).then_inc(c_mxt, 1)
            pe.wait_ge(c_dg, 1)
            pe.matmul(bank[4][:, 128:128 + 2 * NH], c_ones[0:2 * NH, :], c_diag[0:2 * NH, :]).then_inc(c_bc, 1)

            def project(t):
                for i in range(4):
                    if t == 0:
                        pe.wait_ge(c_asd, 4)
                    elif t < T:
                        pe.wait_ge(c_kvd, 4 * (t - 1) + i + 1)
                    for j in range(4):
                        ins = pe.matmul(bank[i][:, P * j:P * (j + 1)], c_as[:, 4 * i + j, :], xnT[:, xtile(t)])
                    ins.then_inc(c_apm, 1)

            def finish(t):
                pe.wait_ge(c_trc, t + 1)
                for j in range(NH // 2):
                    ins = pe.matmul(bank[6][:, 0:P], c_vhT[:, j, :], c_woT[:, j, :], start=(j == 0), stop=(j == NH // 2 - 1))
                ins.then_inc(c_out, 1)

            for t in range(T):
                project(t)
                if t:
                    finish(t - 1)
                for a in range(2):
                    ins = pe.matmul(pair[2][:, a, :].rearrange("p (h d) -> p h d", d=CD), xnT[:, xtile(t)],
                                    c_wvT[:, 8 * a:8 * (a + 1), 0:CD])
                ins.then_inc(c_vm, 1)
                for i in range(4):
                    pe.wait_ge(c_apc, 4 * t + i + 1)
                    pe.matmul(bank[i], xnT[:, xtile(t)], c_a[:, 4 * i:4 * i + 4, :]).then_inc(c_scm, 1)
                pe.wait_ge(c_vc, t + 1)
                for i in range(4):
                    o = bank[NUMBANK[i]][:, 0:4 * CE]
                    if i == 0 and t:
                        cla_added(pe, t - 1)
                    pe.matmul(o, c_cumtile(t), c_wvT[:, 4 * i:4 * i + 4, :], start=True, stop=False, skip_group_check=True)
                    for j in range(4):
                        h = 4 * i + j
                        if t:
                            if j == 0:
                                pe.wait_ge(c_kvd, 4 * (t - 1) + i + 1)
                            pe.matmul(o[:, CE * j:CE * (j + 1)], c_a[:, h, :], c_kv[:, h, :], start=False, stop=False,
                                      skip_group_check=True)
                    pe.wait_ge(c_scd, 4 * t + i + 1)
                    for j in range(4):
                        h = 4 * i + j
                        ins = pe.matmul(o[:, CE * j:CE * (j + 1)], c_s[:, h, :], c_v[:, t % 2, h, :], start=False,
                                        stop=(j == 3), skip_group_check=True)
                    ins.then_inc(c_num, 1)
                if t < T - 1:
                    for i in range(4):
                        pe.matmul(bank[i][:, 0:4 * CE], xn[:, t, :], c_v[:, t % 2, 4 * i:4 * i + 4, :]).then_inc(c_kvm, 1)
                pe.wait_ge(c_vhd, 4 * t + 4)
                for j in range(NH // 2):
                    ins = pe.transpose(bank[4 + j // 4][:, P * (j % 4):P * (j % 4 + 1)],
                                       c_vh[:, 2 * j:2 * j + 2, :].rearrange("p h d -> p (h d)"), ident[:, :])
                ins.then_inc(c_tr, 1)
            finish(T - 1)
            cla_added(pe, T - 1)

        c_cumtile = lambda t: c_cum[:, P * t:P * (t + 1)]

        arena.reset()
        g_lg = arena.take(20, T, NE)
        g_red = arena.take(8, T)
        g_s = arena.take(3, NB)
        g_h = arena.take(3, 2, NB)
        assert arena.at <= LATER_AT

        rounded.at = XR_WORDS
        g_wr = rounded.take(2, 2, 2, GI)
        g_whi = sem("g_whi")
        g_wlo = sem("g_wlo")
        g_c = sem("g_c")
        g_gate = sem("g_gate")
        g_gd = sem("g_gd")
        g_ge = sem("g_ge")
        g_hm = sem("g_hm")
        g_silu = sem("g_silu")
        g_mul = sem("g_mul")
        g_y = sem("g_y")
        g_add = sem("g_add")
        count["g_c"] = 0
        MIDDLE = 4 * (NX - 1)
        STEPS = 4 * NX

        def moe_high(act, rep, e):
            if rep == 0 and e == 0:
                act.wait_ge(later_load, LATER)
                act.wait_ge(x_ready, 16)
            elif e == 0:
                act.wait_ge(x_ready, 28)
            elif e >= 2:
                act.wait_ge(g_hm, 2 * STEPS * rep + 8 * (e - 1))
            act.activation(g_wr[:, e % 2, 0], g_w13[:, :, e, :], ACT.Copy).then_inc(g_whi, 1)

        def moe_low(pool, rep, e):
            pool.wait_ge(g_whi, NX * rep + e + 1)
            pool.tensor_tensor(g_wr[:, e % 2, 1], g_w13[:, :, e, :], g_wr[:, e % 2, 0].bitcast(F32), ALU.subtract
                               ).then_inc(g_wlo, 1)

        def moe_gpsimd(pool, rep):
            for e in range(1, NX):
                moe_low(pool, rep, e)

        def moe_scalar(act, rep):
            for n in range(STEPS):
                if n % 4 == 1 and n // 4 + 1 < NX:
                    moe_high(act, rep, n // 4 + 1)
                if n == 2:
                    act.wait_ge(g_gd, rep + 1)
                    act.activation(g_lg[:, 2], g_lg[:, 1], ACT.Exp).then_inc(g_ge, 1)
                for i in range(2):
                    m = 2 * STEPS * rep + 2 * n + i
                    act.wait_ge(g_hm, m + 1)
                    if m >= 3:
                        act.wait_ge(g_mul, m - 2)
                    act.activation(g_s[:, m % 3, :], pair[m % 3][:, 0, :], ACT.Silu).then_inc(g_silu, 1)

        def moe_vector(dve, rep):
            c = lambda ins: link(dve, g_c, "g_c", ins)
            L = g_lg
            over = lambda col: col.unsqueeze(2).broadcast_to([P, T, NE])
            along = lambda row: row.unsqueeze(1).broadcast_to([P, T, NE])
            k = 5 + 2 * rep
            lg = bank[7][:, 0:T * NE].rearrange("p (t e) -> p t e", e=NE)

            def gate_logits():
                dve.wait_ge(g_gate, rep + 1)
                c(dve.tensor_reduce(g_red[:, 0], lg, AX.X, ALU.max))
                dve.tensor_tensor(L[:, 1], lg, over(g_red[:, 0]), ALU.subtract).then_inc(g_gd, 1)

            def gate_softmax():
                dve.wait_ge(g_ge, rep + 1)
                c(dve.tensor_reduce(g_red[:, 1], L[:, 2], AX.X, ALU.add))
                c(dve.reciprocal(g_red[:, 2], g_red[:, 1]))
                c(dve.tensor_tensor(L[:, 3], L[:, 2], over(g_red[:, 2]), ALU.mult))
                c(dve.tensor_tensor(L[:, 4], L[:, 3], along(g_gb), ALU.add))

            def best(src, at, red):
                c(dve.tensor_reduce(g_red[:, red], L[:, src], AX.X, ALU.max))
                c(dve.tensor_tensor(L[:, at], L[:, src], over(g_red[:, red]), ALU.is_equal))
                c(dve.tensor_tensor(L[:, at + 1], L[:, at], along(g_pref), ALU.mult))
                c(dve.tensor_reduce(g_red[:, red + 1], L[:, at + 1], AX.X, ALU.max))
                c(dve.tensor_tensor(L[:, at + 2], L[:, at + 1], over(g_red[:, red + 1]), ALU.is_equal))

            def gate_second():
                c(dve.scalar_tensor_tensor(L[:, 8], L[:, 7], -1e30, L[:, 4], ALU.mult, ALU.add))
                best(8, 9, 5)

            def gate_weights():
                c(dve.tensor_tensor(L[:, 12], L[:, 7], L[:, 11], ALU.add))
                c(dve.tensor_tensor(L[:, 13], L[:, 3], L[:, 12], ALU.mult))

            def add(n):
                e, b = divmod(n, 4)
                dve.wait_ge(g_y, STEPS * rep + n + 1)
                if e:
                    dve.wait_ge(g_add, MIDDLE * rep + n - 3)
                y = bank[6 + n % 2]
                for i in range(4):
                    t = 4 * b + i
                    w = L[:, 13, t, e - 1:e] if e else 1.0
                    ins = dve.scalar_tensor_tensor(x[:, t, :], y[:, P * i:P * (i + 1)], w, x[:, t, :], ALU.mult, ALU.add)
                ins.then_inc(x_ready if n >= MIDDLE else g_add, 1)
                if n >= MIDDLE:
                    ln_follow(dve, k + 1, b)

            if rep == 0:
                dve.wait_ge(later_load, LATER)
            dve.wait_ge(ln_xn, 4 * k + 4)
            for n in range(STEPS):
                for i in range(2):
                    m = 2 * STEPS * rep + 2 * n + i
                    nn = STEPS * rep + n
                    dve.wait_ge(g_silu, m + 1)
                    if nn >= 3:
                        dve.wait_ge(g_y, nn - 2)
                    dve.tensor_tensor(g_h[:, nn % 3, i, :], pair[m % 3][:, 1, :], g_s[:, m % 3, :], ALU.mult
                                      ).then_inc(g_mul, 1)
                if n == 1:
                    gate_logits()
                if n:
                    add(n - 1)
                if n == 2:
                    gate_softmax()
                    best(4, 5, 3)
                if n == 3:
                    gate_second()
                    gate_weights()
            add(STEPS - 1)

        def moe_tensor(pe, rep):
            k = 5 + 2 * rep
            pe.wait_ge(later_load, LATER)

            def up(n):
                e, b = divmod(n, 4)
                if e == 0:
                    pe.wait_ge(ln_lo, 4 * (k - SPLIT) + b + 1)
                if b == 0:
                    pe.wait_ge(g_wlo, NX * rep + e + 1)
                for i in range(2):
                    m = 2 * STEPS * rep + 2 * n + i
                    if m >= 3:
                        pe.wait_ge(g_mul, m - 2)
                    for a in range(2):
                        for q, (w, v) in enumerate(PARTS):
                            ins = pe.matmul(pair[m % 3][:, a, :], g_wr[:, e % 2, w, a, P * i:P * (i + 1)],
                                            xr[:, v, NB * b:NB * (b + 1)], start=(q == 0), stop=(q == 2))
                    ins.then_inc(g_hm, 1)

            def gate():
                pe.wait_ge(ln_xnT, 4 * k + 4)
                for t in range(T):
                    ins = pe.matmul(bank[7][:, NE * t:NE * (t + 1)], xnT[:, xtile(t)], g_gw)
                ins.then_inc(g_gate, 1)

            def down(n):
                e, b = divmod(n, 4)
                nn = STEPS * rep + n
                pe.wait_ge(g_mul, 2 * nn + 2)
                if n == 1:
                    pe.wait_ge(g_gd, rep + 1)
                if n >= MIDDLE + 2:
                    pe.wait_ge(x_ready, 4 * k + n - MIDDLE - 1)
                elif n >= 2:
                    pe.wait_ge(g_add, MIDDLE * rep + n - 1)
                for i in range(4):
                    for j in range(2):
                        ins = pe.matmul(bank[6 + n % 2][:, P * i:P * (i + 1)], g_h[:, nn % 3, j, P * i:P * (i + 1)],
                                        g_w2[:, e, j, :], start=(j == 0), stop=(j == 1))
                ins.then_inc(g_y, 1)

            for n in range(STEPS):
                up(n)
                if n == 1:
                    gate()
                if n:
                    down(n - 1)
            down(STEPS - 1)
            pe.wait_ge(x_ready, 4 * (k + 1))

        arena.reset()
        d_a = arena.take(P)
        d_b = arena.take(P)
        rounded.at = XR_WORDS
        d_aT = rounded.take(2, S)
        d_v = arena.take(T, P)
        d_p = arena.take(2, S)
        d_pT = arena.take(4, NB)
        d_m = arena.take(T, 8)
        assert arena.at <= LATER_AT
        d_c = sem("d_c")
        d_fold = sem("d_fold")
        d_foldc = sem("d_foldc")
        d_pre = sem("d_pre")
        d_prec = sem("d_prec")
        d_low = sem("d_low")
        d_s = sem("d_s")
        d_max = sem("d_max")
        d_bias = sem("d_bias")
        d_exp = sem("d_exp")
        d_tr = sem("d_tr")
        d_trA = sem("d_trA")
        d_trB = sem("d_trB")
        d_pv = sem("d_pv")
        d_x = sem("d_x")
        count["d_c"] = 0
        SC7 = float(np.float32(1.0) / np.sqrt(np.float32(P)))

        def soft_scalar(act):
            act.wait_ge(d_fold, 1)
            act.activation(d_a, bank[0][:, 0:P], ACT.Copy)
            act.activation(d_b, bank[0][:, P:2 * P], ACT.Copy).then_inc(d_foldc, 1)
            for n in range(8):
                act.wait_ge(d_pre, n + 1)
                dst = d_aT[:, 0, NB * n:NB * (n + 1)] if n < 4 else d_v[:, 4 * (n - 4):4 * (n - 3), :].rearrange("p t n -> p (t n)")
                act.activation(dst, bank[n % 4], ACT.Copy).then_inc(d_prec, 1)

            def turned(t):
                for i in range(2):
                    j = 4 * t + i
                    act.wait_ge(d_tr, j + 1)
                    if t:
                        act.wait_ge(d_pv, j - 3)
                    act.activation(d_pT[:, i, :], bank[4 + i], ACT.Copy).then_inc(d_trA, 1)

            for t in range(T):
                if t:
                    turned(t - 1)
                act.wait_ge(d_bias, t + 1)
                if t >= 2:
                    act.wait_ge(d_tr, 4 * (t - 1))
                for a in range(2):
                    act.activation(d_p[:, t % 2, 2 * NB * a:2 * NB * (a + 1)].rearrange("p (a n) -> p a n", a=2),
                                   pair[a][:, :, :], ACT.Exp, bias=d_m[:, t, 3:4], scale=SC7,
                                   accum_out=d_m[:, t, 4 + a:5 + a]).then_inc(d_exp, 1)
            turned(T - 1)

        def soft_vector(dve):
            c = lambda ins: link(dve, d_c, "d_c", ins)

            def turned(t):
                for i in range(2, 4):
                    j = 4 * t + i
                    dve.wait_ge(d_tr, j + 1)
                    if t:
                        dve.wait_ge(d_pv, j - 3)
                    dve.tensor_copy(d_pT[:, i, :], bank[4 + i % 2]).then_inc(d_trB, 1)

            def finish(t):
                dve.wait_ge(d_exp, 2 * t + 2)
                c(dve.tensor_reduce(d_m[:, t, 6:7], d_m[:, t, 4:6], AX.X, ALU.add))
                c(dve.reciprocal(d_m[:, t, 7:8], d_m[:, t, 6:7]))
                dve.wait_ge(d_pv, 4 * t + 4)
                ins = dve.scalar_tensor_tensor(x[:, t, :], bank[6 + t % 2][:, 0:P], d_m[:, t, 7:8], x[:, t, :],
                                               ALU.mult, ALU.add)
                ins.then_inc(x_ready if t % 4 == 3 else d_x, 1)
                if t % 4 == 3:
                    ln_follow(dve, 7, t // 4)

            dve.wait_ge(ln_xn, 28)
            for n in range(4):
                dve.wait_ge(d_prec, n + 1)
                dve.tensor_tensor(d_aT[:, 1, NB * n:NB * (n + 1)], bank[n],
                                  d_aT[:, 0, NB * n:NB * (n + 1)].bitcast(F32), ALU.subtract).then_inc(d_low, 1)
            for t in range(T):
                for a in range(2):
                    dve.wait_ge(d_s, 2 * t + a + 1)
                    dve.tensor_reduce(d_m[:, t, a:a + 1], pair[a][:, :, :], AX.XY, ALU.max).then_inc(d_max, 1)
                dve.wait_ge(d_max, 2 * t + 2)
                c(dve.tensor_reduce(d_m[:, t, 2:3], d_m[:, t, 0:2], AX.X, ALU.max))
                dve.tensor_scalar(d_m[:, t, 3:4], d_m[:, t, 2:3], -SC7, None, ALU.mult).then_inc(d_bias, 1)
                if t:
                    turned(t - 1)
                if t >= 1:
                    finish(t - 1)
            turned(T - 1)
            finish(T - 1)

        def soft_added(engine, t):
            if t % 4 == 3:
                engine.wait_ge(x_ready, 24 + t // 4 + 1)
            else:
                engine.wait_ge(d_x, 3 * (t // 4) + t % 4 + 1)

        def soft_tensor(pe):
            pe.wait_ge(ln_xnT, 25)
            pe.matmul(bank[0][:, 0:P], d_w[:, 0, :], d_w[:, 1, :])
            pe.matmul(bank[0][:, P:2 * P], d_w[:, 2, :], d_w[:, 3, :]).then_inc(d_fold, 1)
            pe.wait_ge(d_foldc, 1)
            for n in range(8):
                pe.wait_ge(ln_xnT, 24 + n % 4 + 1)
                if n >= 4:
                    pe.wait_ge(d_low, n - 3)
                if n < 4:
                    ins = pe.matmul(bank[n % 4], d_a, xnT[:, xcol(n)])
                else:
                    for i in range(4):
                        ins = pe.matmul(bank[n % 4][:, P * i:P * (i + 1)], xnT[:, xtile(4 * (n - 4) + i)], d_b)
                ins.then_inc(d_pre, 1)
            pe.wait_ge(d_prec, 8)
            pe.wait_ge(ln_lo, 8)

            def scores(t, a):
                if t:
                    pe.wait_ge(d_exp, 2 * (t - 1) + a + 1)
                for b in range(2):
                    for q, (w, v) in enumerate(PARTS):
                        ins = pe.matmul(pair[a][:, b, :], d_aT[:, w, P * t:P * (t + 1)],
                                        xr[:, v, NB * (2 * a + b):NB * (2 * a + b + 1)], start=(q == 0), stop=(q == 2))
                ins.then_inc(d_s, 1)

            def turn(t, i):
                if i % 2 == 0:
                    pe.wait_ge(d_exp, 2 * t + i // 2 + 1)
                if i >= 2:
                    pe.wait_ge(d_trA, 2 * t + i - 1)
                elif t:
                    pe.wait_ge(d_trB, 2 * (t - 1) + i + 1)
                for q in range(4):
                    ins = pe.transpose(bank[4 + i % 2][:, P * q:P * (q + 1)],
                                       d_p[:, t % 2, NB * i + P * q:NB * i + P * (q + 1)], ident[:, :])
                ins.then_inc(d_tr, 1)

            def values(t, i):
                pe.wait_ge(d_trA if i < 2 else d_trB, 2 * t + i % 2 + 1)
                if i == 0 and t >= 2:
                    soft_added(pe, t - 2)
                for q in range(4):
                    ins = pe.matmul(bank[6 + t % 2][:, 0:P], d_pT[:, i, P * q:P * (q + 1)], d_v[:, 4 * i + q, :],
                                    start=(i == 0 and q == 0), stop=(i == 3 and q == 3))
                ins.then_inc(d_pv, 1)

            scores(0, 0)
            scores(0, 1)
            for t in range(T):
                if t + 1 < T:
                    scores(t + 1, 0)
                turn(t, 0)
                turn(t, 1)
                if t + 1 < T:
                    scores(t + 1, 1)
                for i in range(4):
                    values(t, i)
                    if i < 2:
                        turn(t, i + 2)
            soft_added(pe, T - 2)
            soft_added(pe, T - 1)

        def later_stages(n):
            ffn = lambda rep: {"pool": lambda e: ffn_gpsimd(e, rep), "act": lambda e: ffn_scalar(e, rep),
                               "dve": lambda e: ffn_vector(e, rep), "pe": lambda e: ffn_tensor(e, rep)}
            dla = {"pool": dla_gpsimd, "act": dla_scalar, "dve": dla_vector, "pe": dla_tensor}
            moe = lambda rep: {"act": lambda e: moe_scalar(e, rep), "pool": lambda e: moe_gpsimd(e, rep),
                               "dve": lambda e: moe_vector(e, rep), "pe": lambda e: moe_tensor(e, rep)}
            cla = {"pool": cla_gpsimd, "act": cla_scalar, "dve": cla_vector, "pe": cla_tensor}
            soft = {"pool": lambda e: None, "act": soft_scalar, "dve": soft_vector, "pe": soft_tensor}
            return [ffn(0), dla, ffn(1), cla, moe(0), soft, moe(1)][:n - 1]

        block = ctx.enter_context(nc.Block())

        @block.sync
        def _(sp):
            for g in range(G):
                sp.dma_start(x[:, 4 * g:4 * g + 4, :], I["x"][NB * g:NB * (g + 1), :].rearrange("(t p) d -> p t d", p=P)
                             ).then_inc(x_in[g], 16)
            mla_load(sp)
            ffn_load(sp)
            dla_load(sp)
            mla_sync(sp)
            if STAGES > 4:
                later_weights(sp)
            for g in range(G):
                sp.wait_ge(x_ready, 4 * (STAGES - 1) + g + 1)
                sp.dma_start(out[NB * g:NB * (g + 1), :].rearrange("(t p) d -> p t d", p=P),
                             x[:, 4 * g:4 * g + 4, :]).then_inc(stored, 16)
            sp.wait_ge(stored, 64)

        @block.gpsimd
        def _(pool):
            pool.memset(ident[:, :], 0.0).then_inc(ident_done, 1)
            pool.memset(mhalf[:, :], -0.5).then_inc(ident_done, 1)
            pool.wait_ge(ident_done, 2)
            pool.affine_select(out=ident[:, :], in_=ident[:, :], compare_op=ALU.not_equal, fill=1.0, base=0,
                               pattern=[[-1, P]], channel_multiplier=1).then_inc(ident_done, 1)
            pool.memset(stack[0][0].bitcast(F32), 0.0)
            pool.memset(stack[0][1].bitcast(F32), 0.0).then_inc(a_zero, 1)
            ln_gpsimd(pool, 0)

            def prepare(n):
                g, qb, kt = UNITS[n]
                if (g, qb, kt) == (0, 1, 7):
                    ffn_rows_gpsimd(pool)
                if (g, qb, kt) == (0, 2, 11):
                    ffn_tokens_gpsimd(pool)
                if g == 3 and qb < 3 and kt == 4 * qb + 3:
                    if qb == 0:
                        pool.wait_ge(a_pv, last_unit[(2, G - 1)] + 1)
                    ffn_onehots_gpsimd(pool, qb)

            mla_gpsimd(pool, prepare)
            for k, stage in enumerate(later_stages(STAGES)):
                ln_gpsimd(pool, k + 1)
                if k + 1 in (5, 7):
                    moe_low(pool, (k + 1) // 7, 0)
                if k + 1 >= SPLIT:
                    ln_low(pool, k + 1)
                stage["pool"](pool)

        @block.scalar
        def _(act):
            ln_scalar(act, 0)
            mla_scalar(act)
            for k, stage in enumerate(later_stages(STAGES)):
                if k + 1 in (5, 7):
                    moe_high(act, (k + 1) // 7, 0)
                ln_scalar(act, k + 1)
                stage["act"](act)

        @block.vector
        def _(dve):
            dve.memset(xnT[:, 0:XO], 0.0)
            dve.memset(vpad, 0.0).then_inc(a_vzero, 1)
            dve.wait_ge(a_vzero, 1)
            dve.memset(vpad[:, :, :, DH:DH + 1], 1.0).then_inc(a_vzero, 1)
            ln_vector(dve, 0)
            mla_vector(dve)
            for k, stage in enumerate(later_stages(STAGES)):
                if k < 4:
                    ln_vector(dve, k + 1)
                stage["dve"](dve)

        @block.tensor
        def _(pe):
            pe.wait_ge(ident_done, 3)
            ln_tensor(pe, 0)
            mla_tensor(pe)
            for k, stage in enumerate(later_stages(STAGES)):
                ln_tensor(pe, k + 1)
                stage["pe"](pe)


def host_layout(inputs):
    f = lambda name: np.asarray(inputs[name])
    z = lambda *shape: np.zeros(shape, np.float32)
    A = {}
    A["x"] = f("L0_attn_a_x").reshape(S, P)
    wdq, wdkv = f("L0_attn_a_W_DQ"), f("L0_attn_a_W_DKV")
    wqr, wkr = f("L0_attn_a_W_QR"), f("L0_attn_a_W_KR")
    A["WDQT"], A["WDKVT"] = wdq.T, wdkv.T
    swap = np.arange(HR).reshape(-1, 2)[:, ::-1].reshape(-1)
    A["WQR2"] = np.concatenate([wqr, wqr[:, swap]], axis=1)
    ab = z(2, P, P - HR)
    ab[0, :, 0:DR] = wkr
    ab[1, :, 0:DR] = wkr[:, swap[:DR]]
    ab[0, :, 32:64] = wdq
    A["WABr"] = ab
    A["WUV"] = f("L0_attn_a_W_UV")
    uk = z(DL, NH, DQK)
    uk[:, :, 0:DH] = f("L0_attn_a_W_UK").reshape(DL, NH, DH)
    A["WUKc"] = uk.reshape(DL, NH * DQK)
    wq, wks = z(P, NH, DQK), z(P, NH, DQK)
    wq[96:P, :, 0:DH] = f("L0_attn_a_W_UQ").reshape(DL, NH, DH)
    for h in range(NH):
        for i in range(DR):
            wq[DR * h + i, h, DH + i] = 1.0
            wks[HR + i, h, DH + i] = 1.0
    A["WQc"], A["WKsel"] = wq.reshape(P, -1), wks.reshape(P, -1)
    A["WO"] = f("L0_attn_a_W_O")
    inv = np.float32(10000.0) ** (-np.arange(0, DR, 2, dtype=np.float32) / np.float32(DR))
    angle = np.arange(S, dtype=np.float32)[:, None] * inv
    cos, sin = z(96, S), z(96, S)
    for r in range(HR + DR):
        cos[r] = np.cos(angle[:, (r % DR) // 2])
        sin[r] = np.sin(angle[:, (r % DR) // 2]) * (1.0 if r % 2 else -1.0)
    A["cosT"], A["sinT"] = cos, sin
    e1, e2, e3 = f("L0_ffn_ew1"), f("L0_ffn_ew2"), f("L0_ffn_ew3")
    w12 = z(P, 2, NE + 1, FH)
    b12 = z(2, NE + 1, FH)
    for a, (w, b, sw, sb) in enumerate(((e1, "L0_ffn_eb1", "L0_ffn_sw1", "L0_ffn_sb1"),
                                        (e2, "L0_ffn_eb2", "L0_ffn_sw2", "L0_ffn_sb2"))):
        w12[:, a, 0:NE] = w.transpose(2, 0, 1)
        w12[:, a, NE] = f(sw).T
        b12[a, 0:NE], b12[a, NE] = f(b), f(sb)
    A["F_w12"], A["F_b12"] = w12, b12.reshape(-1)
    w3 = z(P, 5, P)
    w3[:, 0:4] = e3.transpose(0, 2, 1).reshape(4, P, P).transpose(1, 0, 2)
    w3[0:FH, 4] = f("L0_ffn_sw3").T
    w3[FH, 4] = f("L0_ffn_sb3")
    w3[FH + 1:FH + 1 + NE, 4] = f("L0_ffn_eb3")
    A["F_w3"] = w3
    bsel, gcol = z(P, 5, NE + 1), z(P, 5)
    for kt in range(4):
        for half in range(2):
            rows = slice(FH * half, FH * (half + 1))
            bsel[rows, kt, 1 + 2 * kt + half] = f("L0_ffn_sel_ln_b")
            gcol[rows, kt] = f("L0_ffn_sel_ln_g")
    bsel[0:FH, 4, 0] = f("L0_ffn_s_ln_b")
    gcol[0:FH, 4] = f("L0_ffn_s_ln_g")
    A["F_bsel"], A["F_gcol"] = bsel, gcol
    A["F_wg"] = np.concatenate([f("L0_ffn_eg_w").T, f("L0_ffn_sg_w").T], axis=1)
    A["F_bg"] = np.concatenate([f("L0_ffn_eg_b"), f("L0_ffn_sg_b")])
    A["F_bx"] = f("L0_ffn_exp_bias")
    A["F_pref"] = np.arange(NE, 0, -1).astype(np.float32)
    for name, rows in (("F_ib", f("L0_ffn_index_b")), ("F_it", f("L0_ffn_index_t"))):
        A[name], A[name + "c"] = rows, rows.reshape(2, P).T
    A["B_ww"], A["B_wrT"] = f("L0_attn_b_W_write"), f("L0_attn_b_W_read").T
    A["B_decay"], A["B_la"] = f("L0_attn_b_decay").reshape(1), f("L0_attn_b_log_alpha").reshape(1)
    wq, wk, wv, wo = (f("L1_attn_a_" + n) for n in ("Wq", "Wk", "Wv", "Wo"))
    A["C_wnat"] = np.stack([w.reshape(NH // 2, P, P).transpose(1, 0, 2) for w in (wq, wk)], axis=1)
    A["C_wqkT"] = np.stack([wq.T, wk.T], axis=1)
    wvT = z(P, NH, CE)
    wvT[:, :, 0:CD] = wv.T.reshape(P, NH, CD)
    A["C_wvT"] = wvT
    A["C_woT"] = wo.T.reshape(NH // 2, P, P).transpose(1, 0, 2)
    A["C_bo"] = f("L1_attn_a_bo")
    w13, w2 = z(P, 2, NX, GI), z(P, NX, 2, P)
    for a, n in enumerate(("1", "3")):
        w13[:, a, 1:NX] = f("L1_ffn_w" + n).transpose(2, 0, 1)
        w13[:, a, 0] = f("L1_ffn_sw" + n).T
    w2[:, 1:NX] = f("L1_ffn_w2").transpose(0, 2, 1).reshape(NE, 2, P, P).transpose(2, 0, 1, 3)
    w2[:, 0] = f("L1_ffn_sw2").T.reshape(2, P, P).transpose(1, 0, 2)
    A["G_w13"], A["G_w2"] = w13, w2
    A["G_gw"], A["G_gb"] = f("L1_ffn_gate_w").T, f("L1_ffn_gate_bias")
    qkv = f("L1_attn_b_W_qkv")
    A["D_w"] = np.stack([qkv[0::3], qkv[1::3], qkv[2::3], f("L1_attn_b_W_out").T], axis=1)
    return {k: np.ascontiguousarray(v) for k, v in A.items()}


def kernel(**inputs):
    import concourse.bacc as _bacc
    from concourse.bass_utils import run_bass_kernel_spmd as _run

    nc = _bacc.Bacc("TRN2", target_bir_lowering=False, num_devices=1)
    arrays = host_layout(inputs)
    aps = {name: nc.dram_tensor(f"in_{name}", a.shape, mybir.dt.from_np(a.dtype), kind="ExternalInput").ap()
           for name, a in arrays.items()}
    out = nc.dram_tensor("out", (S, P), F32, kind="ExternalOutput").ap()
    program(nc, aps, out)
    r = _run(nc, [{f"in_{name}": a for name, a in arrays.items()}], core_ids=[0])
    return r.results[0]["out"].reshape(1, S, P)
```

```python
from contextlib import ExitStack

import numpy as np

import concourse.bass as bass
from concourse import mybir

ACT = mybir.ActivationFunctionType
ALU = mybir.AluOpType
F32 = mybir.dt.float32
BF16 = mybir.dt.bfloat16
I32 = mybir.dt.int32
F32R = mybir.dt.float32r
AX = mybir.AxisListType

P = 128
S = 2048
T = S // P
G = 4
NB = 512
SPLIT = 4
XO = 4
EPS = 1e-5
STAGES = 8

NH, DH, DR, DL = 16, 8, 4, 32
DQK = DH + DR
HR = NH * DR
CP = NH * DQK // 2
CLIP = 80.0
NE, FH, M = 8, 64, 256
CD = 64
NX, GI = 9, 256
PARTS = [(0, 0), (0, 1), (1, 0)]
COMBOS = [(0, 0), (0, 1), (1, 0), (0, 2), (2, 0), (1, 1)]


class Arena:

    def __init__(self, tensor, words, native=F32):
        self.tensor, self.words, self.native, self.at = tensor, words, native, 0

    def reset(self):
        self.at = 0

    def take(self, *shape, dtype=None):
        n = int(np.prod(shape))
        words = n if dtype is not BF16 else n // 2
        view = self.tensor[:, self.at:self.at + words]
        self.at += words
        assert self.at <= self.words, (self.at, self.words)
        if dtype not in (None, self.native):
            view = view.bitcast(dtype)
        if len(shape) > 1:
            names = "abcde"[:len(shape)]
            view = view.rearrange(f"p ({' '.join(names)}) -> p {' '.join(names)}",
                                  **{c: n for c, n in zip(names, shape)})
        return view


def program(nc, I, out):
    ctx = ExitStack()
    with ctx:
        def sb(name, shape, dt=F32):
            return ctx.enter_context(nc.sbuf_tensor(name, shape, dt))

        def sem(name):
            return ctx.enter_context(nc.semaphore(name))

        pair = [ctx.enter_context(nc.psum_tensor(f"pair{i}", [P, 2, NB], F32)) for i in range(4)]
        bank = [pair[i // 2][:, i % 2, :] for i in range(8)]

        x = sb("x", [P, T, P])
        xn = sb("xn", [P, T, P])
        xnT = sb("xnT", [P, XO + S])
        ident = sb("ident", [P, P])
        stats = sb("stats", [P, T, 6])
        mv = sb("mv", [P, T, 2])
        ve = sb("ve", [P, T])
        rstd = sb("rstd", [P, T])
        mhalf = sb("mhalf", [P, 64])
        ROUND = 4 * S
        ARENA = 46500 - ROUND
        LATER_AT = 21344
        arena = Arena(sb("arena", [P, ARENA]), ARENA)
        rounded = Arena(sb("rounded", [P, ROUND], F32R), ROUND, F32R)
        xr = rounded.take(2, S)
        XR_WORDS = rounded.at
        rounded.reset()

        x_in = [sem(f"x_in{g}") for g in range(G)]
        x_ready = sem("x_ready")
        ident_done = sem("ident_done")
        ln_stats = sem("ln_stats")
        ln_moments = sem("ln_moments")
        ln_ve = sem("ln_ve")
        ln_rstd = sem("ln_rstd")
        ln_xn = sem("ln_xn")
        ln_turned = sem("ln_turned")
        ln_xnT = sem("ln_xnT")
        ln_lo = sem("ln_lo")
        stored = sem("stored")

        def xcol(g):
            return slice(XO + NB * g, XO + NB * (g + 1))

        def xtile(t):
            return slice(XO + P * t, XO + P * (t + 1))

        def ln_moment(dve, k, g):
            if k == 0:
                dve.wait_ge(x_in[g], 16)
            else:
                dve.wait_ge(x_ready, 4 * (k - 1) + g + 1)
            for t in range(4 * g, 4 * g + 4):
                ins = dve.bn_stats(stats[:, t, :], x[:, t, :])
            ins.then_inc(ln_stats, 1)
            dve.wait_ge(ln_stats, 4 * k + g + 1)
            for t in range(4 * g, 4 * g + 4):
                ins = dve.bn_aggr(mv[:, t, :], stats[:, t, :])
            ins.then_inc(ln_moments, 1)

        def ln_normalise(dve, k, g):
            dve.wait_ge(ln_rstd, 4 * k + g + 1)
            for t in range(4 * g, 4 * g + 4):
                ins = dve.tensor_scalar(xn[:, t, :], x[:, t, :], mv[:, t, 0:1], rstd[:, t:t + 1],
                                        ALU.subtract, ALU.mult)
            ins.then_inc(ln_xn, 1)

        def ln_follow(dve, k, g):
            if k < STAGES:
                ln_moment(dve, k, g)
                if g:
                    ln_normalise(dve, k, g - 1)
                if g == G - 1:
                    ln_normalise(dve, k, g)

        def ln_rstd_group(pool, k, g):
            pool.wait_ge(ln_moments, 4 * k + g + 1)
            pool.tensor_scalar(ve[:, 4 * g:4 * g + 4], mv[:, 4 * g:4 * g + 4, 1], EPS, None,
                               ALU.add).then_inc(ln_ve, 1)
            pool.wait_ge(ln_ve, 4 * k + g + 1)
            pool.tensor_tensor(rstd[:, 4 * g:4 * g + 4], ve[:, 4 * g:4 * g + 4], mhalf[:, 0:4],
                               ALU.pow).then_inc(ln_rstd, 1)

        def ln_gpsimd(pool, k):
            for g in range(G - 1 if k == 5 else 0, G):
                ln_rstd_group(pool, k, g)

        def ln_low(pool, k):
            for g in range(G):
                pool.wait_ge(ln_xnT, 4 * k + g + 1)
                pool.tensor_tensor(xr[:, 1, NB * g:NB * (g + 1)], xnT[:, xcol(g)],
                                   xr[:, 0, NB * g:NB * (g + 1)].bitcast(F32), ALU.subtract).then_inc(ln_lo, 1)

        def ln_tensor(pe, k, after_group=lambda g: None):
            for g in range(G):
                pe.wait_ge(ln_xn, 4 * k + g + 1)
                if 4 * k + g >= 2:
                    pe.wait_ge(ln_xnT, 4 * k + g - 1)
                for i in range(4):
                    ins = pe.transpose(bank[6 + g % 2][:, P * i:P * (i + 1)], xn[:, 4 * g + i, :], ident[:, :])
                ins.then_inc(ln_turned, 1)
                after_group(g)

        def ln_scalar(act, k):
            for g in range(G):
                act.wait_ge(ln_turned, 4 * k + g + 1)
                if k >= SPLIT:
                    act.activation(xr[:, 0, NB * g:NB * (g + 1)], bank[6 + g % 2][:, :], ACT.Copy)
                act.activation(xnT[:, xcol(g)], bank[6 + g % 2][:, :], ACT.Copy).then_inc(ln_xnT, 1)

        arena.reset()
        vpad = arena.take(T, NH, 32)
        stack = [[a.take(4, S, dtype=BF16) for _ in range(2)] for a in (rounded, arena)]
        arena.at -= 2 * 2 * S
        parts = arena.take(2, 3, S, dtype=BF16)
        arena.at += 2 * 2 * S - 3 * S
        pring = arena.take(6, 2, NB)
        arena.at -= 6 * 2 * NB
        cosT, sinT, zq = arena.take(S), arena.take(S), arena.take(S)
        resid_words = arena.at
        resid = arena.take(2, NB)
        rope1, rope2 = arena.take(2, NB), arena.take(2, NB)
        oT = arena.take(2, NB)
        attn = arena.take(T, P)
        m_wab = arena.take(2, P)
        m_wq = arena.take(2 * CP)
        m_wkc, m_wkr = arena.take(2 * CP), arena.take(2 * CP)
        m_wv = arena.take(P)
        m_wo = arena.take(P)
        m_dqT = arena.take(P)
        m_dkvT = arena.take(P)
        m_qr2 = arena.take(2 * HR)
        m_uk = arena.take(2 * CP)
        m_uv = arena.take(P)
        rdenA = arena.take(16)
        scratch = nc.dram_tensor("split_parts", [2, 2, 3, CP, S], BF16, kind="Internal").ap()

        a_zero = sem("a_zero")
        a_vzero = sem("a_vzero")
        a_w = sem("a_w")
        a_w2 = sem("a_w2")
        a_fold = sem("a_fold")
        a_folded = sem("a_folded")
        a_ab = sem("a_ab")
        a_rope = sem("a_rope")
        a_cq = sem("a_cq")
        a_z = sem("a_z")
        a_v = sem("a_v")
        a_vcopied = sem("a_vcopied")
        a_qk = sem("a_qk")
        a_hi = sem("a_hi")
        a_res = sem("a_res")
        a_mid = sem("a_mid")
        a_lo = sem("a_lo")
        a_parts = [sem(f"a_parts{i}") for i in range(4)]
        a_stack = [sem(f"a_stack{i}") for i in range(2)]
        a_scores = sem("a_scores")
        a_exp = sem("a_exp")
        a_clip = sem("a_clip")
        a_mask = sem("a_mask")
        a_pv = sem("a_pv")
        a_oT = sem("a_oT")
        a_turned = sem("a_turned")
        a_rden = sem("a_rden")
        a_norm = sem("a_norm")
        a_at = sem("a_at")
        a_atc = sem("a_atc")
        a_wo = sem("a_wo")

        UNITS = [(g, qb, kt) for g in range(4) for qb in range(G) for kt in range(4 * qb + 4)]
        BLOCKS = [(g, qb) for g in range(4) for qb in range(G)]
        first_col = lambda qb, kt: max(0, kt * P - qb * NB)
        last_unit = {}
        for n, (g, qb, kt) in enumerate(UNITS):
            last_unit[(g, qb)] = n
        masked = [kt >= 4 * qb for _, qb, kt in UNITS]
        masks_to = [2 * sum(masked[:n + 1]) for n in range(len(UNITS))]
        QK = [(a, side, b) for a in range(2) for side in range(2) for b in range(G)]

        def mla_load(sp):
            sp.dma_start(m_dqT[0:DL, :], I["WDQT"]).then_inc(a_w, 16)
            sp.dma_start(m_dkvT[0:DL, :], I["WDKVT"]).then_inc(a_w, 16)
            sp.dma_start(m_qr2[0:DL, :], I["WQR2"]).then_inc(a_w, 16)
            sp.dma_start(m_uk[0:DL, :], I["WUKc"]).then_inc(a_w, 16)
            sp.dma_start(m_uv[0:DL, :], I["WUV"]).then_inc(a_w, 16)
            sp.dma_start(m_wab[:, :, HR:P], I["WABr"].rearrange("a p n -> p a n")).then_inc(a_w2, 16)
            sp.dma_start(m_wq, I["WQc"]).then_inc(a_w2, 16)
            sp.dma_start(m_wkr, I["WKsel"]).then_inc(a_w2, 16)
            sp.dma_start(m_wo, I["WO"]).then_inc(a_w2, 16)
            sp.dma_start(cosT[0:96, :], I["cosT"]).then_inc(a_w2, 16)
            sp.dma_start(sinT[0:96, :], I["sinT"]).then_inc(a_w2, 16)

        def mla_sync(sp):
            def out(n):
                for b in range(G):
                    cols = slice(NB * b, NB * (b + 1))
                    sp.wait_ge(a_lo, 4 * n + b + 1)
                    sp.dma_start(scratch[n % 2, n // 2, :, :, cols].rearrange("c p n -> p c n"),
                                 parts[0:CP, n % 2, :, cols]).then_inc(a_parts[n], 16)

            def back(g):
                sp.wait_ge(a_parts[2 * (g // 2)], 16 * G)
                sp.wait_ge(a_parts[2 * (g // 2) + 1], 16 * G)
                if g < 2:
                    sp.wait_ge(a_zero, g + 2)
                if g >= 2:
                    sp.wait_ge(a_pv, last_unit[(g - 2, G - 1)] + 1)
                for side in range(2):
                    for c, combo in enumerate(COMBOS):
                        src = scratch[side, g // 2, combo[side], (g % 2) * 48:(g % 2) * 48 + 48, :]
                        sp.dma_start(stack[g % 2][side][c * DQK:(c + 1) * DQK],
                                     src.rearrange("(h d) n -> d h n", h=4)).then_inc(a_stack[g % 2], 16)

            out(0)
            out(1)
            back(0)
            out(2)
            out(3)
            for g in range(1, 4):
                back(g)

        def mla_gpsimd(pool, loop_hook):
            for b in range(G):
                pool.wait_ge(a_rope, b + 1)
                pool.tensor_tensor(zq[0:96, NB * b:NB * (b + 1)], rope1[0:96, b % 2], rope2[0:96, b % 2],
                                   ALU.add).then_inc(a_z, 1)
            pool.memset(stack[0][0].bitcast(F32), 0.0).then_inc(a_zero, 1)
            for n in range(len(QK)):
                a, side, b = QK[n]
                pool.wait_ge(a_mid, n + 1)
                pool.tensor_tensor(parts[0:CP, (n // 4) % 2, 2, NB * b:NB * (b + 1)], resid[0:CP, n % 2],
                                   parts[0:CP, (n // 4) % 2, 1, NB * b:NB * (b + 1)],
                                   ALU.subtract).then_inc(a_lo, 1)
            for n, (g, qb, kt) in enumerate(UNITS):
                if masked[n]:
                    c = first_col(qb, kt)
                    for h in range(2):
                        r = (2 * n + h) % 6
                        pool.wait_ge(a_clip, 2 * n + h + 1)
                        pool.affine_select(out=pring[:, r, :, c:c + P], in_=pring[:, r, :, c:c + P],
                                           compare_op=ALU.is_ge, fill=0.0, base=0,
                                           pattern=[[0, 2], [1, P]], channel_multiplier=-1).then_inc(a_mask, 1)
                loop_hook(n)

        def mla_fold_scalar(act):
            act.wait_ge(a_fold, 3)
            act.activation(m_wab[:, :, 0:HR], bank[0][:, 0:2 * HR].rearrange("p (a n) -> p a n", a=2),
                           ACT.Copy).then_inc(a_folded, 1)
            act.activation(m_wkc, bank[1][:, 0:2 * CP], ACT.Copy).then_inc(a_folded, 1)
            act.activation(m_wv, bank[2][:, 0:P], ACT.Copy).then_inc(a_folded, 1)

        def mla_scalar(act):
            for b in range(G):
                act.wait_ge(a_ab, b + 1)
                act.activation(zq[96:P, NB * b:NB * (b + 1)], bank[2 * (b % 2)][96:P, :], ACT.Copy).then_inc(a_cq, 1)
            for g in range(G):
                act.wait_ge(a_v, g + 1)
                if g == 0:
                    act.wait_ge(a_vzero, 2)
                act.activation(vpad[:, 4 * g:4 * g + 4, :, 0:DH],
                               bank[4 + g % 2][:, :].rearrange("p (t h d) -> p t h d", t=4, h=NH),
                               ACT.Copy).then_inc(a_vcopied, 1)

            def middle(n):
                a, side, b = QK[n]
                act.wait_ge(a_res, n + 1)
                act.activation(parts[0:CP, (n // 4) % 2, 1, NB * b:NB * (b + 1)], resid[0:CP, n % 2],
                               ACT.Copy).then_inc(a_mid, 1)

            for n in range(len(QK)):
                a, side, b = QK[n]
                half = n // 4
                act.wait_ge(a_qk, n + 1)
                if n >= 8 and n % 4 == 0:
                    act.wait_ge(a_parts[half - 2], 16 * G)
                act.activation(parts[0:CP, half % 2, 0, NB * b:NB * (b + 1)], bank[n % 4][0:CP, :],
                               ACT.Copy).then_inc(a_hi, 1)
                if n:
                    middle(n - 1)
            middle(len(QK) - 1)
            dla_decay_scalar(act)
            for n, (g, qb, kt) in enumerate(UNITS):
                c = first_col(qb, kt)
                for h in range(2):
                    m = 2 * n + h
                    act.wait_ge(a_scores, m + 1)
                    if m >= 6:
                        act.wait_ge(a_pv, (m - 6) // 2 + 1)
                    act.activation(pring[:, m % 6, :, c:NB], pair[m % 3][:, :, c:NB], ACT.Exp,
                                   scale=float(1.0 / np.sqrt(np.float32(DQK)))).then_inc(a_exp, 1)
            for g in range(G):
                act.wait_ge(a_at, g + 1)
                act.activation(oT[:, g % 2], bank[6 + g % 2][:, :], ACT.Copy).then_inc(a_atc, 1)

        def mla_vector(dve):
            dve.wait_ge(a_w2, 96)
            for b in range(G):
                dve.wait_ge(a_ab, b + 1)
                if b >= 2:
                    dve.wait_ge(a_z, b - 1)
                dve.tensor_tensor(rope1[0:96, b % 2], bank[2 * (b % 2)][0:96, :], cosT[0:96, NB * b:NB * (b + 1)],
                                  ALU.mult)
                dve.tensor_tensor(rope2[0:96, b % 2], bank[2 * (b % 2) + 1][0:96, :],
                                  sinT[0:96, NB * b:NB * (b + 1)], ALU.mult).then_inc(a_rope, 1)
            dve.memset(stack[0][1].bitcast(F32), 0.0).then_inc(a_zero, 1)
            for n in range(len(QK)):
                a, side, b = QK[n]
                dve.wait_ge(a_hi, n + 1)
                if n >= 2:
                    dve.wait_ge(a_lo, n - 1)
                dve.tensor_tensor(resid[0:CP, n % 2], bank[n % 4][0:CP, :],
                                  parts[0:CP, (n // 4) % 2, 0, NB * b:NB * (b + 1)], ALU.subtract).then_inc(a_res, 1)
            dla_decay_vector(dve, 1)
            top = float(np.exp(np.float32(CLIP) / np.sqrt(np.float32(DQK))))

            def out_block(j):
                dve.wait_ge(a_pv, last_unit[BLOCKS[j]] + 1)
                if j >= 2:
                    dve.wait_ge(a_turned, j - 1)
                dve.tensor_copy(oT[:, j % 2], bank[6 + j % 2][:, :]).then_inc(a_oT, 1)

            def norm_block(j):
                g, qb = BLOCKS[j]
                o = bank[6 + j % 2][:, :].rearrange("p (i h d) -> p i h d", i=4, h=4)
                dve.wait_ge(a_turned, j + 1)
                dve.reciprocal(rdenA[:, :].rearrange("p (i h) -> p i h", i=4), o[:, :, :, DH]).then_inc(a_rden, 1)
                dve.wait_ge(a_rden, j + 1)
                for i in range(4):
                    ins = dve.tensor_tensor(
                        attn[:, 4 * qb + i, 32 * g:32 * g + 32].rearrange("p (h d) -> p h d", h=4), o[:, i, :, 0:DH],
                        rdenA[:, 4 * i:4 * i + 4].unsqueeze(2).broadcast_to([P, 4, DH]), ALU.mult)
                ins.then_inc(a_norm, 1)

            done = {last_unit[b]: j for j, b in enumerate(BLOCKS)}
            for n, (g, qb, kt) in enumerate(UNITS):
                c = first_col(qb, kt)
                for h in range(2):
                    m = 2 * n + h
                    dve.wait_ge(a_exp, m + 1)
                    dve.tensor_scalar(pring[:, m % 6, :, c:NB], pring[:, m % 6, :, c:NB], 1.0 / top, top,
                                      ALU.max, ALU.min).then_inc(a_clip, 1)
                if n - 2 in done:
                    out_block(done[n - 2])
                if n - 4 in done:
                    norm_block(done[n - 4])
            out_block(len(BLOCKS) - 1)
            norm_block(len(BLOCKS) - 1)
            for g in range(G):
                dve.wait_ge(a_wo, g + 1)
                dve.tensor_tensor(x[:, 4 * g:4 * g + 4, :], bank[g][:, :].rearrange("p (t n) -> p t n", t=4),
                                  x[:, 4 * g:4 * g + 4, :], ALU.add).then_inc(x_ready, 1)
                ln_follow(dve, 1, g)

        def mla_fold_tensor(pe):
            pe.wait_ge(a_w, 80)
            pe.matmul(bank[0][:, 0:2 * HR], m_dqT[0:DL, :], m_qr2[0:DL, :]).then_inc(a_fold, 1)
            pe.matmul(bank[1][:, 0:2 * CP], m_dkvT[0:DL, :], m_uk[0:DL, :]).then_inc(a_fold, 1)
            pe.matmul(bank[2][:, 0:P], m_dkvT[0:DL, :], m_uv[0:DL, :]).then_inc(a_fold, 1)

        def mla_tensor(pe):
            pe.wait_ge(a_folded, 3)
            pe.wait_ge(a_w2, 96)
            for b in range(G):
                pe.wait_ge(ln_xnT, b + 1)
                if b >= 2:
                    pe.wait_ge(a_rope, b - 1)
                    pe.wait_ge(a_cq, b - 1)
                pe.matmul(bank[2 * (b % 2)][:, :], m_wab[:, 0, :], xnT[:, xcol(b)])
                pe.matmul(bank[2 * (b % 2) + 1][:, :], m_wab[:, 1, :], xnT[:, xcol(b)]).then_inc(a_ab, 1)
            for g in range(G):
                if g >= 2:
                    pe.wait_ge(a_vcopied, g - 1)
                for i in range(4):
                    ins = pe.matmul(bank[4 + g % 2][:, P * i:P * (i + 1)], xnT[:, xtile(4 * g + i)], m_wv)
                ins.then_inc(a_v, 1)
            for n in range(len(QK)):
                a, side, b = QK[n]
                if n < 4:
                    pe.wait_ge(a_z, b + 1)
                    pe.wait_ge(a_cq, b + 1)
                if n == 0:
                    pe.wait_ge(a_rope, G)
                    pe.wait_ge(a_cq, G)
                if n >= 4:
                    pe.wait_ge(a_res, n - 3)
                cols = slice(CP * a, CP * (a + 1))
                if side == 0:
                    pe.matmul(bank[n % 4][0:CP, :], m_wq[:, cols], zq[:, NB * b:NB * (b + 1)]).then_inc(a_qk, 1)
                else:
                    pe.matmul(bank[n % 4][0:CP, :], m_wkc[:, cols], xnT[:, xcol(b)], start=True, stop=False)
                    pe.matmul(bank[n % 4][0:CP, :], m_wkr[:, cols], zq[:, NB * b:NB * (b + 1)],
                              start=False, stop=True).then_inc(a_qk, 1)

            def scores(n):
                g, qb, kt = UNITS[n]
                c = first_col(qb, kt)
                if kt == 0 and qb == 0:
                    pe.wait_ge(a_stack[g % 2], 192 * (g // 2 + 1))
                for h in range(2):
                    m = 2 * n + h
                    if m >= 3:
                        pe.wait_ge(a_exp, m - 2)
                    for i in range(2):
                        head = 2 * h + i
                        ins = pe.matmul(pair[m % 3][:, i, c:NB], stack[g % 2][1][:, head, P * kt:P * (kt + 1)],
                                        stack[g % 2][0][:, head, NB * qb + c:NB * (qb + 1)])
                    ins.then_inc(a_scores, 1)

            def values(n):
                g, qb, kt = UNITS[n]
                c = first_col(qb, kt)
                j = BLOCKS.index((g, qb))
                if kt == 0 and j >= 2:
                    pe.wait_ge(a_norm, j - 1)
                pe.wait_ge(a_clip, 2 * n + 2)
                if masked[n]:
                    pe.wait_ge(a_mask, masks_to[n])
                for head in range(4):
                    m = 2 * n + head // 2
                    ins = pe.matmul(bank[6 + j % 2][32 * head:32 * head + 32, c:NB], vpad[:, kt, 4 * g + head, :],
                                    pring[:, m % 6, head % 2, c:NB], start=(kt == 0), stop=(kt == 4 * qb + 3),
                                    tile_position=(0, 32 * head))
                ins.then_inc(a_pv, 1)

            def turn(j):
                pe.wait_ge(a_oT, j + 1)
                for i in range(4):
                    ins = pe.transpose(bank[6 + j % 2][:, P * i:P * (i + 1)], oT[:, j % 2, P * i:P * (i + 1)], ident[:, :])
                ins.then_inc(a_turned, 1)

            done = {last_unit[b]: j for j, b in enumerate(BLOCKS)}
            pe.wait_ge(a_res, len(QK))
            pe.wait_ge(a_vcopied, G)
            for n in range(len(UNITS)):
                scores(n)
                if n >= 2:
                    values(n - 2)
                if n - 4 in done:
                    turn(done[n - 4])
            values(len(UNITS) - 2)
            values(len(UNITS) - 1)
            turn(len(BLOCKS) - 1)
            pe.wait_ge(a_norm, len(BLOCKS))
            for g in range(G):
                if g >= 2:
                    pe.wait_ge(a_atc, g - 1)
                for i in range(4):
                    ins = pe.transpose(bank[6 + g % 2][:, P * i:P * (i + 1)], attn[:, 4 * g + i, :], ident[:, :])
                ins.then_inc(a_at, 1)
                pe.wait_ge(a_atc, g + 1)
                for i in range(4):
                    ins = pe.matmul(bank[g][:, P * i:P * (i + 1)], oT[:, g % 2, P * i:P * (i + 1)], m_wo)
                ins.then_inc(a_wo, 1)


        a_words = arena.at

        f_w12 = arena.take(2, NE + 1, FH)
        f_b12 = arena.take(2, NE + 1, FH)
        f_w3raw = arena.take(5, P)
        f_w3 = arena.take(5, P)
        f_bsel = arena.take(5, NE + 1)
        f_gcol = arena.take(5)
        f_wg = arena.take(NE + 1)
        f_bg = arena.take(NE + 1)
        f_bx = arena.take(NE)
        f_pref = arena.take(NE)
        f_idx = arena.take(2, M + 2, dtype=I32)
        f_notin = arena.take(T)
        f_rcnt = arena.take(2)
        f_scol = arena.take(T)
        f_row = arena.take(M + 2)
        f_scoli = arena.take(T, dtype=I32)
        later_words = arena.at
        arena.at = resid_words
        f_i1, f_i2 = arena.take(2, M + 2), arena.take(M + 2)
        arena.at = resid_words + 2 * NB
        f_srow = arena.take(S)
        f_srowi = f_srow.bitcast(I32)
        rounded.reset()
        f_gtr = rounded.take(T, M)
        f_gmr = rounded.take(2, S)
        f_gt, f_gm = f_gtr.bitcast(F32), f_gmr.bitcast(F32)
        arena.reset()
        keep_words = arena.at
        f_hb = arena.take(T, 2, FH)
        f_sg = arena.take(T, FH)
        f_u = arena.take(T, FH)
        f_st = arena.take(T, 6)
        f_mv = arena.take(T, 2)
        f_rs = arena.take(T)
        f_rv = arena.take(T)
        f_sh = arena.take(T, FH + 1)
        f_shT = arena.take(S)
        f_xm = arena.take(M)
        f_sc = arena.take(24, 2, NE + 1)
        f_hm = arena.take(2, 2, NE + 1, FH)
        f_sm = arena.take(2, NE + 1, FH)
        f_um = arena.take(2, NE + 1, FH)
        f_stm = arena.take(2 * (NE + 1), 6)
        f_mvm = arena.take(2 * (NE + 1), 2)
        f_rsm = arena.take(2, NE + 1)
        f_sums = arena.take(T, M // 2)
        arena.at -= T * M // 2
        f_z = arena.take(2, (NE + 1) * FH + NE + 1)
        f_zT = arena.take(5, M)
        f_moe = arena.take(2, P)
        f_same = arena.take(M)
        ffn_words = arena.at

        f_w = sem("f_w")
        f_c = sem("f_c")
        f_pc = sem("f_pc")
        f_onehot = sem("f_onehot")
        f_prep = sem("f_prep")
        f_fold = sem("f_fold")
        f_hs = sem("f_hs")
        f_hsb = sem("f_hsb")
        f_silu = sem("f_silu")
        f_stat = sem("f_stat")
        f_rstd = sem("f_rstd")
        f_shn = sem("f_shn")
        f_sturn = sem("f_sturn")
        f_sT = sem("f_sT")
        f_gath = sem("f_gath")
        f_xmc = sem("f_xmc")
        f_gate = sem("f_gate")
        f_lg = sem("f_lg")
        f_ex = sem("f_ex")
        f_hid = sem("f_hid")
        f_hmb = sem("f_hmb")
        f_zd = sem("f_zd")
        f_zturn = sem("f_zturn")
        f_zc = sem("f_zc")
        f_mo = sem("f_mo")
        f_moc = sem("f_moc")
        f_out = sem("f_out")
        count = {"f_c": 0, "f_pc": 0, "f_ex": 0, "f_lg": 0}

        def link(eng, s, name, ins):
            count[name] += 1
            ins.then_inc(s, 1)
            eng.wait_ge(s, count[name])

        def ffn_load(sp):
            bc = lambda ap: ap.partition_broadcast(P)
            sp.dma_start(f_w12, I["F_w12"]).then_inc(f_w, 16)
            sp.dma_start(f_b12.rearrange("p a e h -> p (a e h)"), bc(I["F_b12"])).then_inc(f_w, 16)
            sp.dma_start(f_w3raw, I["F_w3"]).then_inc(f_w, 16)
            sp.dma_start(f_bsel, I["F_bsel"]).then_inc(f_w, 16)
            sp.dma_start(f_gcol, I["F_gcol"]).then_inc(f_w, 16)
            sp.dma_start(f_wg, I["F_wg"]).then_inc(f_w, 16)
            sp.dma_start(f_bg, bc(I["F_bg"])).then_inc(f_w, 16)
            sp.dma_start(f_bx, bc(I["F_bx"])).then_inc(f_w, 16)
            sp.dma_start(f_pref, bc(I["F_pref"])).then_inc(f_w, 16)
            for i, name in enumerate(("F_ib", "F_it")):
                sp.dma_start(f_idx[:, i, 0:M], bc(I[name])).then_inc(f_w, 16)
                sp.dma_start(f_idx[:, i, M:M + 2], I[name + "c"]).then_inc(f_w, 16)

        def ffn_rows_gpsimd(pool):
            c = lambda ins: link(pool, f_pc, "f_pc", ins)
            pool.wait_ge(f_w, 13 * 16)
            pool.wait_ge(a_res, len(QK))
            pool.wait_ge(a_z, G)
            c(pool.iota(f_scoli, [[P, T]], base=0, channel_multiplier=1))
            pool.tensor_copy(f_scol, f_scoli)
            c(pool.tensor_copy(f_i1, f_idx))
            pool.tensor_scalar(f_i2, f_i1[:, 1], 0.0, float(S), ALU.is_lt, ALU.mult)
            c(pool.tensor_scalar(f_row, f_i1[:, 0], -1.0, None, ALU.is_equal))
            c(pool.tensor_tensor(f_i2, f_i2, f_i1[:, 1], ALU.add))
            c(pool.tensor_scalar(f_i1[:, 0], f_i1[:, 0], 0.0, None, ALU.is_equal))
            c(pool.tensor_tensor(f_row, f_row, f_i1[:, 0], ALU.add))
            c(pool.tensor_scalar(f_i2, f_i2, 1.0, None, ALU.add))
            c(pool.tensor_tensor(f_i2, f_i2, f_row, ALU.mult))
            c(pool.tensor_scalar(f_row, f_i2, -1.0, None, ALU.add))

        def ffn_tokens_gpsimd(pool):
            c = lambda ins: link(pool, f_pc, "f_pc", ins)
            c(pool.iota(f_srowi, [[1, S]], base=0, channel_multiplier=0))
            c(pool.tensor_copy(f_srow, f_srowi))

        def ffn_onehots_gpsimd(pool, part):
            if part < 2:
                for t in range(8 * part, 8 * part + 8):
                    pool.tensor_scalar(f_gtr[:, t, :], f_row[:, 0:M], f_scol[:, t:t + 1], None, ALU.is_equal)
            else:
                for m in range(2):
                    ins = pool.tensor_scalar(f_gmr[:, m, :], f_srow, f_row[:, M + m:M + m + 1], None, ALU.is_equal)
                ins.then_inc(f_onehot, 1)

        def ffn_notin_gpsimd(pool):
            c = lambda ins: link(pool, f_pc, "f_pc", ins)
            pool.wait_ge(f_onehot, 1)
            step = M // 2
            c(pool.tensor_tensor(f_sums[:, :, 0:step], f_gt[:, :, 0:step], f_gt[:, :, step:], ALU.add))
            while step > 1:
                step //= 2
                c(pool.tensor_tensor(f_sums[:, :, 0:step], f_sums[:, :, 0:step],
                                     f_sums[:, :, step:2 * step], ALU.add))
            c(pool.tensor_scalar(f_notin, f_sums[:, :, 0], 0.0, None, ALU.is_equal))

        def ffn_prepare_vector(dve):
            c = lambda ins: link(dve, f_c, "f_c", ins)
            dve.wait_ge(f_onehot, 1)
            for kt in range(5):
                ins = dve.tensor_scalar(f_w3[:, kt, :], f_w3raw[:, kt, :], f_gcol[:, kt:kt + 1], None, ALU.mult)
            c(ins)
            dve.wait_ge(f_fold, 1)
            dve.tensor_tensor(f_w3[64:64 + NE + 1, 4, :], bank[5][64:64 + NE + 1, 0:P],
                              f_w3raw[64:64 + NE + 1, 4, :], ALU.add).then_inc(f_prep, 1)

        def ffn_counts_vector(dve):
            c = lambda ins: link(dve, f_c, "f_c", ins)
            for m in range(2):
                c(dve.tensor_scalar(f_same, f_row[:, 0:M], f_row[:, M + m:M + m + 1], None, ALU.is_equal))
                c(dve.tensor_reduce(f_rcnt[:, m:m + 1], f_same, AX.X, ALU.add))
            c(dve.reciprocal(f_rcnt, f_rcnt))

        def ffn_gpsimd(pool, rep):
            k = 2 * rep + 1
            if rep == 0:
                ffn_notin_gpsimd(pool)
            c = lambda ins: link(pool, f_pc, "f_pc", ins)
            pool.wait_ge(f_stat, 3 * rep + 1)
            c(pool.tensor_scalar(f_rv, f_mv[:, :, 1], EPS, None, ALU.add))
            c(pool.tensor_tensor(f_rs, f_rv, mhalf[:, 0:T], ALU.pow))
            pool.tensor_tensor(f_rs, f_rs, f_notin, ALU.mult).then_inc(f_rstd, 1)
            for m in range(2):
                pool.wait_ge(f_stat, 3 * rep + 2 + m)
                c(pool.tensor_scalar(f_rsm[:, m], f_mvm[:, (NE + 1) * m:(NE + 1) * (m + 1), 1], EPS, None, ALU.add))
                c(pool.tensor_tensor(f_rsm[:, m], f_rsm[:, m], mhalf[:, 0:NE + 1], ALU.pow))
                pool.tensor_tensor(f_rsm[:, m], f_rsm[:, m], f_sc[:, FAC, m], ALU.mult).then_inc(f_rstd, 1)

        def ffn_scalar(act, rep):
            act.wait_ge(f_gath, rep + 1)
            act.activation(f_xm, bank[4][:, 0:M], ACT.Copy).then_inc(f_xmc, 1)
            for g in range(G):
                act.wait_ge(f_hsb, 4 * rep + g + 1)
                act.activation(f_sg[:, 4 * g:4 * g + 4, :], f_hb[:, 4 * g:4 * g + 4, 0, :], ACT.Silu
                               ).then_inc(f_silu, 1)
            act.wait_ge(f_lg, 2 * rep + 1)
            act.activation(f_sc[:, 1], f_sc[:, 0], ACT.Exp, scale=-1.0).then_inc(f_ex, 1)
            act.wait_ge(f_lg, 2 * rep + 2)
            act.activation(f_sc[:, 12, :, 0:2], f_sc[:, 11, :, 0:2], ACT.Exp).then_inc(f_ex, 1)
            for m in range(2):
                act.wait_ge(f_hmb, 2 * rep + m + 1)
                act.activation(f_sm[:, m], f_hm[:, m, 0], ACT.Silu).then_inc(f_silu, 1)

            def shared_turned(g):
                act.wait_ge(f_sturn, 4 * rep + g + 1)
                act.activation(f_shT[0:FH + 1, NB * g:NB * (g + 1)], bank[6 + g % 2][0:FH + 1, :], ACT.Copy
                               ).then_inc(f_sT, 1)

            act.wait_ge(f_zturn, rep + 1)
            for kt in range(4):
                act.activation(f_zT[:, kt, :], bank[kt // 2][:, M * (kt % 2):M * (kt % 2 + 1)], ACT.Copy)
            act.activation(f_zT[0:FH + NE + 1, 4, :], bank[4][0:FH + NE + 1, 0:M], ACT.Copy).then_inc(f_zc, 1)
            shared_turned(0)
            shared_turned(1)
            act.wait_ge(f_mo, rep + 1)
            act.activation(f_moe, bank[5][:, 0:2 * P].rearrange("p (m n) -> p m n", m=2), ACT.Copy
                           ).then_inc(f_moc, 1)
            shared_turned(2)
            shared_turned(3)

        LOG, SIG, BIA, FAC = 0, 3, 4, 20

        def ffn_vector(dve, rep):
            c = lambda ins: link(dve, f_c, "f_c", ins)
            k = 2 * rep + 1
            if rep == 0:
                ffn_prepare_vector(dve)
            for g in range(G):
                dve.wait_ge(f_hs, 4 * rep + g + 1)
                dve.tensor_tensor(f_hb[:, 4 * g:4 * g + 4], bank[g][:, :].rearrange("p (t a h) -> p t a h", t=4, a=2),
                                  f_b12[:, :, NE, :].unsqueeze(1).broadcast_to([P, 4, 2, FH]), ALU.add
                                  ).then_inc(f_hsb, 1)
            if rep == 0:
                ffn_counts_vector(dve)

            def shared_sums(t0, t1):
                for t in range(t0, t1):
                    dve.bn_stats(f_st[:, t, :], f_u[:, t, :])

            def shared_moments(t0, t1):
                for t in range(t0, t1):
                    ins = dve.bn_aggr(f_mv[:, t, :], f_st[:, t, :])
                return ins

            def r(ins, work, t0, t1):
                count["f_c"] += 1
                ins.then_inc(f_c, 1)
                work(t0, t1)
                dve.wait_ge(f_c, count["f_c"])

            sc = f_sc
            dve.wait_ge(f_gate, rep + 1)
            dve.tensor_tensor(sc[:, LOG], bank[5][:, 0:2 * (NE + 1)].rearrange("p (m e) -> p m e", m=2),
                              f_bg.unsqueeze(1).broadcast_to([P, 2, NE + 1]), ALU.add).then_inc(f_lg, 1)
            for g in range(G):
                dve.wait_ge(f_silu, 6 * rep + g + 1)
                ins = dve.tensor_tensor(f_u[:, 4 * g:4 * g + 4, :], f_sg[:, 4 * g:4 * g + 4, :],
                                        f_hb[:, 4 * g:4 * g + 4, 1, :], ALU.mult)
            c(ins)
            shared_sums(0, 2)
            dve.wait_ge(f_ex, 2 * rep + 1)
            r(dve.tensor_scalar(sc[:, 2], sc[:, 1], 1.0, None, ALU.add), shared_sums, 2, 3)
            r(dve.reciprocal(sc[:, SIG], sc[:, 2]), shared_sums, 3, 4)
            r(dve.tensor_tensor(sc[:, BIA, :, 0:NE], sc[:, SIG, :, 0:NE], f_bx.unsqueeze(1).broadcast_to([P, 2, NE]), ALU.add),
              shared_sums, 4, 5)
            r(dve.tensor_reduce(sc[:, 5, :, 0], sc[:, BIA, :, 0:NE], AX.X, ALU.max), shared_sums, 5, 6)
            r(dve.tensor_tensor(sc[:, 6, :, 0:NE], sc[:, BIA, :, 0:NE], sc[:, 5, :, 0:1].broadcast_to([P, 2, NE]), ALU.is_equal),
              shared_sums, 6, 7)
            r(dve.tensor_tensor(sc[:, 7, :, 0:NE], sc[:, 6, :, 0:NE], f_pref.unsqueeze(1).broadcast_to([P, 2, NE]), ALU.mult),
              shared_sums, 7, 8)
            r(dve.tensor_reduce(sc[:, 8, :, 0], sc[:, 7, :, 0:NE], AX.X, ALU.max), shared_sums, 8, 9)
            r(dve.tensor_tensor(sc[:, 9, :, 0:NE], sc[:, 7, :, 0:NE], sc[:, 8, :, 0:1].broadcast_to([P, 2, NE]), ALU.is_equal),
              shared_sums, 9, 10)
            r(dve.tensor_tensor(sc[:, 10, :, 0:NE], sc[:, 9, :, 0:NE], sc[:, SIG, :, 0:NE], ALU.mult), shared_sums, 10, 11)
            dve.tensor_copy(sc[:, 11, :, 0:1], sc[:, SIG, :, NE:NE + 1])
            r(dve.tensor_reduce(sc[:, 11, :, 1], sc[:, 10, :, 0:NE], AX.X, ALU.add), shared_sums, 11, 12)
            dve.tensor_copy(sc[:, 13, :, 0:1], sc[:, 11, :, 0:1]).then_inc(f_lg, 1)
            shared_sums(12, T)
            dve.wait_ge(f_ex, 2 * rep + 2)
            r(dve.tensor_reduce(sc[:, 14, :, 0], sc[:, 12, :, 0:2], AX.X, ALU.add), shared_moments, 0, 2)
            r(dve.reciprocal(sc[:, 15, :, 0], sc[:, 14, :, 0]), shared_moments, 2, 4)
            r(dve.tensor_tensor(sc[:, 16, :, 0], sc[:, 15, :, 0], f_rcnt, ALU.mult), shared_moments, 4, 6)
            r(dve.tensor_tensor(sc[:, 17, :, 0:2], sc[:, 12, :, 0:2], sc[:, 16, :, 0:1].broadcast_to([P, 2, 2]), ALU.mult),
              shared_moments, 6, 8)
            dve.tensor_copy(sc[:, FAC, :, NE:NE + 1], sc[:, 17, :, 0:1])
            r(dve.tensor_tensor(sc[:, FAC, :, 0:NE], sc[:, 9, :, 0:NE], sc[:, 17, :, 1:2].broadcast_to([P, 2, NE]), ALU.mult),
              shared_moments, 8, 10)
            shared_moments(10, T).then_inc(f_stat, 1)
            for m in range(2):
                for a in range(2):
                    dve.wait_ge(f_hid, 4 * rep + 2 * m + a + 1)
                    dve.tensor_tensor(f_hm[:, m, a, 0:NE, :], bank[2 * m + a][:, :].rearrange("p (e h) -> p e h", e=NE),
                                      f_b12[:, a, 0:NE, :], ALU.add)
                dve.tensor_tensor(f_hm[:, m, :, NE, :], bank[5][:, 256 + 128 * m:384 + 128 * m].rearrange("p (a h) -> p a h", a=2),
                                  f_b12[:, :, NE, :], ALU.add).then_inc(f_hmb, 1)
            for m in range(2):
                dve.wait_ge(f_silu, 6 * rep + 4 + m + 1)
                c(dve.tensor_tensor(f_um[:, m], f_sm[:, m], f_hm[:, m, 1], ALU.mult))
                for e in range(NE + 1):
                    ins = dve.bn_stats(f_stm[:, (NE + 1) * m + e, :], f_um[:, m, e, :])
                c(ins)
                for e in range(NE + 1):
                    n = (NE + 1) * m + e
                    ins = dve.bn_aggr(f_mvm[:, n, :], f_stm[:, n, :])
                ins.then_inc(f_stat, 1)
            dve.wait_ge(f_stat, 3 * rep + 3)
            for m in range(2):
                means = f_mvm[:, (NE + 1) * m:(NE + 1) * (m + 1), 0:1].broadcast_to([P, NE + 1, FH])
                ins = dve.tensor_tensor(f_um[:, m], f_um[:, m], means, ALU.subtract)
            c(ins)
            for m in range(2):
                dve.wait_ge(f_rstd, 3 * rep + 2 + m)
                dve.tensor_tensor(f_z[:, m, 0:FH * (NE + 1)].rearrange("p (e h) -> p e h", h=FH), f_um[:, m],
                                  f_rsm[:, m].unsqueeze(2).broadcast_to([P, NE + 1, FH]), ALU.mult)
                dve.tensor_copy(f_z[:, m, FH * (NE + 1):FH * (NE + 1) + 1], sc[:, FAC, m, NE:NE + 1])
                dve.tensor_copy(f_z[:, m, FH * (NE + 1) + 1:], sc[:, FAC, m, 0:NE]).then_inc(f_zd, 1)
            for g in range(G):
                ts = slice(4 * g, 4 * g + 4)
                ins = dve.tensor_tensor(f_u[:, ts, :], f_u[:, ts, :], f_mv[:, ts, 0:1].broadcast_to([P, 4, FH]),
                                        ALU.subtract)
            c(ins)
            dve.wait_ge(f_rstd, 3 * rep + 1)
            dve.tensor_copy(f_sh[:, :, FH:FH + 1], f_notin.unsqueeze(2))
            for g in range(G):
                ts = slice(4 * g, 4 * g + 4)
                dve.tensor_tensor(f_sh[:, ts, 0:FH], f_u[:, ts, :], f_rs[:, ts].unsqueeze(2).broadcast_to([P, 4, FH]),
                                  ALU.mult).then_inc(f_shn, 1)
            for g in range(G):
                dve.wait_ge(f_out, 4 * rep + g + 1)
                dve.tensor_tensor(x[:, 4 * g:4 * g + 4, :], bank[g][:, :].rearrange("p (t n) -> p t n", t=4),
                                  x[:, 4 * g:4 * g + 4, :], ALU.add).then_inc(x_ready, 1)
                ln_follow(dve, k + 1, g)

        def ffn_gather(pe, rep, g):
            if rep == 0 and g == 0:
                pe.wait_ge(f_w, 13 * 16)
                for kt in range(5):
                    rows = P if kt < 4 else FH
                    ins = pe.matmul(bank[5][64:64 + NE + 1, 0:P], f_bsel[0:rows, kt, :], f_w3raw[0:rows, kt, :],
                                    start=(kt == 0), stop=(kt == 4), tile_position=(0, 64))
                ins.then_inc(f_fold, 1)
                pe.wait_ge(f_onehot, 1)
            for t in range(4 * g, 4 * g + 4):
                ins = pe.matmul(bank[4][:, 0:M], xn[:, t, :], f_gt[:, t, :], start=(t == 0), stop=(t == T - 1))
            if g == G - 1:
                ins.then_inc(f_gath, 1)

        def ffn_tensor(pe, rep):
            k = 2 * rep + 1
            for g in range(G):
                pe.wait_ge(ln_xnT, 4 * k + g + 1)
                for i in range(4):
                    ins = pe.matmul(bank[g][:, P * i:P * (i + 1)], xnT[:, xtile(4 * g + i)], f_w12[:, :, NE, :])
                ins.then_inc(f_hs, 1)
            pe.wait_ge(f_xmc, rep + 1)
            if rep == 0:
                pe.wait_ge(f_prep, 1)
            for m in range(2):
                pe.matmul(bank[5][:, (NE + 1) * m:(NE + 1) * (m + 1)], f_xm[:, P * m:P * (m + 1)], f_wg)
                ins = pe.matmul(bank[5][:, 256 + 128 * m:384 + 128 * m], f_xm[:, P * m:P * (m + 1)], f_w12[:, :, NE, :])
            ins.then_inc(f_gate, 1)
            for m in range(2):
                for a in range(2):
                    pe.wait_ge(f_hsb, 4 * rep + 2 * m + a + 1)
                    pe.matmul(bank[2 * m + a][:, :], f_xm[:, P * m:P * (m + 1)],
                              f_w12[:, a, 0:NE, :]).then_inc(f_hid, 1)
            def turn_shared(g):
                pe.wait_ge(f_shn, 4 * rep + g + 1)
                if g >= 2:
                    pe.wait_ge(f_sT, 4 * rep + g - 1)
                for i in range(4):
                    ins = pe.transpose(bank[6 + g % 2][0:FH + 1, P * i:P * (i + 1)], f_sh[:, 4 * g + i, :], ident[:, :])
                ins.then_inc(f_sturn, 1)

            for m in range(2):
                pe.wait_ge(f_zd, 2 * rep + m + 1)
                for kt in range(4):
                    pe.transpose(bank[kt // 2][:, M * (kt % 2) + P * m:M * (kt % 2) + P * (m + 1)],
                                 f_z[:, m, P * kt:P * (kt + 1)], ident[:, :])
                ins = pe.transpose(bank[4][0:FH + NE + 1, P * m:P * (m + 1)], f_z[:, m, 4 * P:], ident[:, :])
            ins.then_inc(f_zturn, 1)
            turn_shared(0)
            turn_shared(1)
            pe.wait_ge(f_zc, rep + 1)
            for m in range(2):
                for kt in range(5):
                    rows = P if kt < 4 else FH + NE + 1
                    ins = pe.matmul(bank[5][:, P * m:P * (m + 1)], f_zT[0:rows, kt, P * m:P * (m + 1)],
                                    f_w3[0:rows, kt, :], start=(kt == 0), stop=(kt == 4))
            ins.then_inc(f_mo, 1)
            turn_shared(2)
            turn_shared(3)
            pe.wait_ge(f_moc, rep + 1)
            for g in range(G):
                pe.wait_ge(f_sT, 4 * rep + g + 1)
                for i in range(4):
                    t = 4 * g + i
                    o = bank[g][:, P * i:P * (i + 1)]
                    pe.matmul(o, f_shT[0:FH + 1, P * t:P * (t + 1)], f_w3[0:FH + 1, 4, :], start=True, stop=False)
                    pe.matmul(o, f_gm[:, 0, P * t:P * (t + 1)], f_moe[:, 0, :], start=False, stop=False)
                    ins = pe.matmul(o, f_gm[:, 1, P * t:P * (t + 1)], f_moe[:, 1, :], start=False, stop=True)
                ins.then_inc(f_out, 1)


        arena.at = later_words
        b_ww, b_wr = arena.take(P), arena.take(P)
        b_in = arena.take(2)
        b_sm = arena.take(8)
        later_words2 = arena.at
        arena.at = keep_words
        b_expo = arena.take(2 * P + 2)
        b_expoi = arena.take(2 * P + 2, dtype=I32)
        b_pow = arena.take(2 * P + 2)
        b_wv = arena.take(P)
        b_v = arena.take(T, P)
        b_wtok = arena.take(T, P)
        b_sm2 = arena.take(T, P)
        b_xdec = arena.take(T, P)
        b_state = arena.take(T, P)

        b_w = sem("b_w")
        b_iota = sem("b_iota")
        b_c = sem("b_c")
        b_s = sem("b_s")
        b_powd = sem("b_powd")
        b_mask = sem("b_mask")
        b_fold = sem("b_fold")
        b_wvd = sem("b_wvd")
        b_vm = sem("b_vm")
        b_vc = sem("b_vc")
        b_wt = sem("b_wt")
        b_wtc = sem("b_wtc")
        b_scm = sem("b_scm")
        b_smd = sem("b_smd")
        b_um = sem("b_um")
        b_st = sem("b_st")
        b_xd = sem("b_xd")
        b_out = sem("b_out")
        count["b_c"] = 0

        def shifted(t):
            return slice(XO - 1 + P * t, XO - 1 + P * (t + 1))

        def dla_load(sp):
            sp.dma_start(b_ww, I["B_ww"]).then_inc(b_w, 16)
            sp.dma_start(b_wr, I["B_wrT"]).then_inc(b_w, 16)
            sp.dma_start(b_in[:, 0:1], I["B_decay"].partition_broadcast(P)).then_inc(b_w, 16)
            sp.dma_start(b_in[:, 1:2], I["B_la"].partition_broadcast(P)).then_inc(b_w, 16)

        def dla_gpsimd(pool):
            pool.wait_ge(x_ready, 8)
            pool.iota(b_expoi[:, 0:P], [[1, P]], base=-1, channel_multiplier=-1)
            pool.iota(b_expoi[:, P:2 * P], [[1, P]], base=0, channel_multiplier=0)
            pool.iota(b_expoi[:, 2 * P:2 * P + 1], [[1, 1]], base=P - 1, channel_multiplier=-1)
            pool.iota(b_expoi[:, 2 * P + 1:2 * P + 2], [[1, 1]], base=P, channel_multiplier=0).then_inc(b_iota, 1)
            pool.wait_ge(b_powd, 1)
            pool.affine_select(out=b_pow[:, 0:P], in_=b_pow[:, 0:P], compare_op=ALU.is_ge, fill=0.0, base=-1,
                               pattern=[[1, P]], channel_multiplier=-1).then_inc(b_mask, 1)
            for g in range(G):
                pool.wait_ge(ln_xnT, 8 + g + 1)
                pool.tensor_tensor(b_xdec[:, 4 * g:4 * g + 4, :], xnT[:, xcol(g)].rearrange("p (t n) -> p t n", t=4),
                                   b_pow[:, P:2 * P].unsqueeze(1).broadcast_to([P, 4, P]), ALU.mult).then_inc(b_xd, 1)
            pool.wait_ge(ln_xn, 12)
            for g in range(G):
                xg = x[:, 4 * g:4 * g + 4, :]
                pool.tensor_tensor(xg, xg, xn[:, 4 * g:4 * g + 4, :], ALU.add).then_inc(b_xd, 1)

        def dla_decay_scalar(act):
            act.wait_ge(b_st, 1)
            act.activation(b_sm[:, 2:3], b_sm[:, 1:2], ACT.Exp, scale=-1.0).then_inc(b_s, 1)
            act.activation(b_sm[:, 6:7], b_in[:, 1:2], ACT.Exp).then_inc(b_s, 1)
            act.wait_ge(b_s, 2)
            act.activation(b_sm[:, 3:4], b_sm[:, 2:3], ACT.Ln, bias=1.0).then_inc(b_s, 1)

        def dla_scalar(act):
            act.wait_ge(b_iota, 2)
            act.activation(b_pow, b_expo, ACT.Exp, scale=b_sm[:, 4:5]).then_inc(b_powd, 1)
            for g in range(G):
                act.wait_ge(b_vm, g + 1)
                act.activation(b_v[:, 4 * g:4 * g + 4, :], bank[g][:, :].rearrange("p (t n) -> p t n", t=4), ACT.Copy
                               ).then_inc(b_vc, 1)

        def dla_decay_vector(dve, part):
            c = lambda ins: link(dve, b_c, "b_c", ins)
            if part == 1:
                dve.wait_ge(b_s, 3)
                dve.scalar_tensor_tensor(b_sm[:, 4:5], b_in[:, 0:1], 0.0, b_sm[:, 3:4], ALU.min, ALU.subtract
                                         ).then_inc(b_st, 1)
                return
            dve.wait_ge(b_w, 64)
            c(dve.tensor_scalar(b_sm[:, 0:1], b_in[:, 0:1], -1.0, None, ALU.mult))
            dve.tensor_tensor(b_sm[:, 1:2], b_sm[:, 0:1], b_in[:, 0:1], ALU.max).then_inc(b_st, 1)

        def dla_vector(dve):
            dve.wait_ge(b_iota, 1)
            dve.tensor_scalar(b_expo, b_expoi, 0.0, None, ALU.max).then_inc(b_iota, 1)
            dve.wait_ge(b_fold, 1)
            dve.tensor_scalar(b_wv, bank[0][:, 0:P], b_sm[:, 6:7], None, ALU.mult).then_inc(b_wvd, 1)
            dve.memset(b_state[:, 0, :], 0.0)
            dve.wait_ge(b_powd, 1)
            for g in range(G):
                dve.wait_ge(b_wt, g + 1)
                dve.tensor_scalar(b_wtok[:, 4 * g:4 * g + 4, :], bank[4 + g % 2][:, :].rearrange("p (t n) -> p t n", t=4),
                                  b_pow[:, 2 * P:2 * P + 1], None, ALU.mult).then_inc(b_wtc, 1)
            dve.wait_ge(b_mask, 1)
            for g in range(G):
                dve.wait_ge(b_scm, g + 1)
                dve.tensor_tensor(b_sm2[:, 4 * g:4 * g + 4, :], bank[g][:, :].rearrange("p (t n) -> p t n", t=4),
                                  b_pow[:, 0:P].unsqueeze(1).broadcast_to([P, 4, P]), ALU.mult).then_inc(b_smd, 1)
            for t in range(T - 1):
                dve.wait_ge(b_um, t // 4 + 1)
                ins = dve.scalar_tensor_tensor(b_state[:, t + 1, :], b_state[:, t, :], b_pow[:, 2 * P + 1:2 * P + 2],
                                               bank[4 + t // 4][:, P * (t % 4):P * (t % 4 + 1)], ALU.mult, ALU.add)
                ins.then_inc(b_st, 1)
                dve.wait_ge(b_st, 2 + t + 1)
            for g in range(G):
                xg = x[:, 4 * g:4 * g + 4, :]
                dve.wait_ge(b_xd, G + g + 1)
                dve.wait_ge(b_out, g + 1)
                dve.tensor_tensor(xg, bank[g][:, :].rearrange("p (t n) -> p t n", t=4), xg, ALU.add
                                  ).then_inc(x_ready, 1)
                ln_follow(dve, 3, g)

        def dla_tensor(pe):
            pe.wait_ge(b_w, 64)
            pe.matmul(bank[0][:, 0:P], b_ww, b_wr).then_inc(b_fold, 1)
            pe.wait_ge(b_wvd, 1)
            for g in range(G):
                pe.wait_ge(ln_xnT, 8 + g + 1)
                for i in range(4):
                    ins = pe.matmul(bank[g][:, P * i:P * (i + 1)], xnT[:, xtile(4 * g + i)], b_wv)
                ins.then_inc(b_vm, 1)
                if g >= 2:
                    pe.wait_ge(b_wtc, g - 1)
                for i in range(4):
                    ins = pe.transpose(bank[4 + g % 2][:, P * i:P * (i + 1)], xnT[:, shifted(4 * g + i)], ident[:, :])
                ins.then_inc(b_wt, 1)
            for g in range(G):
                pe.wait_ge(b_vc, g + 1)
                for i in range(4):
                    t = 4 * g + i
                    ins = pe.matmul(bank[g][:, P * i:P * (i + 1)], xnT[:, shifted(t)], xnT[:, xtile(t)])
                ins.then_inc(b_scm, 1)
            pe.wait_ge(b_wtc, G)
            for g in range(G):
                for i in range(4):
                    t = 4 * g + i
                    ins = pe.matmul(bank[4 + g][:, P * i:P * (i + 1)], b_wtok[:, t, :], b_v[:, t, :])
                ins.then_inc(b_um, 1)
            for g in range(G):
                pe.wait_ge(b_smd, g + 1)
                pe.wait_ge(b_xd, g + 1)
                pe.wait_ge(b_st, 2 + min(4 * g + 3, T - 1))
                for i in range(4):
                    t = 4 * g + i
                    o = bank[g][:, P * i:P * (i + 1)]
                    pe.matmul(o, b_sm2[:, t, :], b_v[:, t, :], start=True, stop=(t == 0))
                    if t:
                        ins = pe.matmul(o, b_xdec[:, t, :], b_state[:, t, :], start=False, stop=True)
                ins.then_inc(b_out, 1)


        arena.at = later_words2
        c_wnat = arena.take(2, NH // 2, P)
        d_w = arena.take(4, P)
        arena.at = LATER_AT
        g_w13 = arena.take(2, NX, GI)
        g_w2 = arena.take(NX, 2, P)
        g_gw = arena.take(NE)
        g_gb = arena.take(NE)
        g_pref = arena.take(NE)
        c_wvT = arena.take(NH, CD)
        c_woT = arena.take(NH // 2, P)
        c_bo = arena.take(P)
        assert arena.at <= a_words, (arena.at, a_words)
        later_load = sem("later_load")
        qk_load = sem("qk_load")

        def later_weights(sp):
            sp.wait_ge(x_ready, 4)
            sp.dma_start(c_wnat, I["C_wnat"]).then_inc(later_load, 16)
            sp.dma_start(c_wvT, I["C_wvT"]).then_inc(later_load, 16)
            sp.dma_start(c_woT, I["C_woT"]).then_inc(later_load, 16)
            sp.dma_start(c_bo, I["C_bo"].partition_broadcast(P)).then_inc(later_load, 16)
            sp.dma_start(g_w13, I["G_w13"]).then_inc(later_load, 16)
            sp.dma_start(g_w2, I["G_w2"]).then_inc(later_load, 16)
            sp.dma_start(g_gw, I["G_gw"]).then_inc(later_load, 16)
            sp.dma_start(g_gb, I["G_gb"].partition_broadcast(P)).then_inc(later_load, 16)
            sp.dma_start(g_pref, I["F_pref"].partition_broadcast(P)).then_inc(later_load, 16)
            sp.dma_start(d_w, I["D_w"]).then_inc(later_load, 16)
            sp.dma_start(c_wqkT, I["C_wqkT"]).then_inc(qk_load, 16)
        LATER = 160

        arena.reset()
        c_as = arena.take(NH, P)
        c_sq = arena.take(2, NH * CD)
        arena.at -= 2 * NH * CD
        c_z = arena.take(NH, P)
        c_n2 = arena.take(T, 2 * NH)
        c_mx = arena.take(2 * NH)
        c_r = arena.take(4)
        c_diag = arena.take(2 * NH)
        c_rr = arena.take(2 * NH)
        c_ch = arena.take(NH)
        c_ones = arena.take(P)
        c_mask = arena.take(P)
        c_cnt = arena.take(P)
        c_cnti = arena.take(P, dtype=I32)
        c_cum = arena.take(S)
        c_zero = arena.take(S)
        arena.at -= S
        c_rep = arena.take(NH // 2, P)
        c_den = arena.take(2, P)
        arena.at += S - (NH // 2 + 2) * P
        c_unit = arena.take(4, 32)
        c_sel = arena.take(NH // 2, P)
        c_vs = arena.take(NH // 2, T)
        c_v = arena.take(2, NH, CD)
        c_a = arena.take(NH, P)
        c_kv = arena.take(NH, CD)
        c_vhT = arena.take(NH // 2, P)
        assert arena.at >= ffn_words
        c_wqkT = arena.take(2, NH * CD)
        arena.at -= 2 * NH * CD
        c_s = arena.take(NH, P)
        rounded.at = XR_WORDS
        c_wr = rounded.take(2, 2, NH * CD)
        rounded.at = XR_WORDS
        c_ar = rounded.take(2, NH, P)
        assert arena.at <= LATER_AT, arena.at

        c_c = sem("c_c")
        c_consts = sem("c_consts")
        c_qk = sem("c_qk")
        c_sqd = sem("c_sqd")
        c_n2d = sem("c_n2d")
        c_mxd = sem("c_mxd")
        c_mxt = sem("c_mxt")
        c_mxr = sem("c_mxr")
        c_rd = sem("c_rd")
        c_dg = sem("c_dg")
        c_bc = sem("c_bc")
        c_am = sem("c_am")
        c_asd = sem("c_asd")
        c_apm = sem("c_apm")
        c_apc = sem("c_apc")
        c_whi = sem("c_whi")
        c_wlo = sem("c_wlo")
        c_alo = sem("c_alo")
        c_vm = sem("c_vm")
        c_vc = sem("c_vc")
        c_scm = sem("c_scm")
        c_scd = sem("c_scd")
        c_num = sem("c_num")
        c_vhd = sem("c_vhd")
        c_kvm = sem("c_kvm")
        c_kvd = sem("c_kvd")
        c_zd = sem("c_zd")
        c_dm = sem("c_dm")
        c_vsm = sem("c_vsm")
        c_rdd = sem("c_rdd")
        c_rpm = sem("c_rpm")
        c_rpc = sem("c_rpc")
        c_out = sem("c_out")
        c_xadd = sem("c_xadd")
        count["c_c"] = 0

        def cla_gpsimd(pool):
            pool.wait_ge(x_ready, 16)
            pool.memset(c_ones, 1.0)
            pool.memset(c_zero, 0.0)
            pool.memset(c_mask, 1.0)
            pool.memset(c_unit, 0.0)
            for j in range(NH // 2):
                row = 32 * (j // 2) + 2 * (j % 2)
                pool.tensor_copy(c_sel[:, j].rearrange("p (h n) -> p h n", h=2),
                                 ident[:, row:row + 2].unsqueeze(2).broadcast_to([P, 2, CD]))
            pool.iota(c_cnti, [[1, P]], base=1, channel_multiplier=0).then_inc(c_consts, 1)
            pool.wait_ge(c_consts, 1)
            pool.affine_select(out=c_mask, in_=c_mask, compare_op=ALU.is_ge, fill=0.0, base=0,
                               pattern=[[1, P]], channel_multiplier=-1)
            for j in range(4):
                ins = pool.memset(c_unit[:, j, j:j + 1], 1.0)
            ins.then_inc(c_consts, 1)
            pool.wait_ge(later_load, LATER)
            pool.wait_ge(ln_xn, 20)
            for g in range(G):
                xg = x[:, 4 * g:4 * g + 4, :]
                ins = pool.tensor_tensor(xg, xg, c_bo.unsqueeze(1).broadcast_to([P, 4, P]), ALU.add)
            ins.then_inc(c_consts, 1)
            pool.wait_ge(c_mxr, 1)
            pool.tensor_tensor(c_r[0:2 * NH, 1:2], c_r[0:2 * NH, 0:1], mhalf[0:2 * NH, 0:1], ALU.pow).then_inc(c_rd, 1)
            for t in range(T):
                for i in range(4):
                    hs = slice(4 * i, 4 * i + 4)
                    pool.wait_ge(c_apc, 4 * t + i + 1)
                    if t:
                        pool.wait_ge(c_dm, t)
                    pool.tensor_tensor(c_z[:, hs, :], c_a[:, hs, :],
                                       c_cum[:, P * t:P * (t + 1)].unsqueeze(1).broadcast_to([P, 4, P]), ALU.mult
                                       ).then_inc(c_zd, 1)
                if t and t % 4 == 0 and STAGES > 5:
                    ln_rstd_group(pool, 5, t // 4 - 1)

        def cla_high(act):
            act.wait_ge(qk_load, 16)
            act.wait_ge(x_ready, 16)
            for side in range(2):
                act.activation(c_wr[:, side, 0], c_wqkT[:, side], ACT.Copy).then_inc(c_whi, 1)

        def cla_scalar(act):
            for n in range(2 * T):
                act.wait_ge(c_qk, n + 1)
                if n >= 2:
                    act.wait_ge(c_n2d, n - 1)
                act.activation(c_sq[:, n % 2, :].rearrange("p (a n) -> p a n", a=2), pair[n % 4][:, :, :], ACT.Square
                               ).then_inc(c_sqd, 1)
            for t in range(T):
                for i in range(4):
                    act.wait_ge(c_apm, 4 * t + i + 1)
                    if t:
                        act.wait_ge(c_num, 4 * t)
                        act.wait_ge(c_zd, 4 * t)
                    src = bank[i].rearrange("p (h n) -> p h n", h=4)
                    act.activation(c_a[:, 4 * i:4 * i + 4, :], src, ACT.Copy)
                    act.activation(c_ar[:, 0, 4 * i:4 * i + 4, :], src, ACT.Copy).then_inc(c_apc, 1)
                if t:
                    act.wait_ge(c_rpm, t)
                    act.activation(c_rep.rearrange("p (a j) n -> p a (j n)", a=2), pair[2][:, :, :], ACT.Copy
                                   ).then_inc(c_rpc, 1)
                act.wait_ge(c_vm, t + 1)
                if t >= 2:
                    act.wait_ge(c_kvm, 4 * (t - 1))
                act.activation(c_v[:, t % 2].rearrange("p (a h) d -> p a (h d)", a=2), pair[2][:, :, :],
                               ACT.Copy).then_inc(c_vc, 1)
            act.wait_ge(c_rpm, T)
            act.activation(c_rep.rearrange("p (a j) n -> p a (j n)", a=2), pair[2][:, :, :], ACT.Copy).then_inc(c_rpc, 1)

        def cla_vector(dve):
            c = lambda ins: link(dve, c_c, "c_c", ins)
            dve.wait_ge(later_load, LATER)
            for side in range(2):
                dve.wait_ge(c_whi, side + 1)
                dve.tensor_tensor(c_wr[:, side, 1], c_wqkT[:, side], c_wr[:, side, 0].bitcast(F32), ALU.subtract
                                  ).then_inc(c_wlo, 1)
            dve.wait_ge(c_consts, 2)
            dve.tensor_copy(c_cnt, c_cnti)
            dve.memset(c_kv, 0.0)
            for n in range(2 * T):
                dve.wait_ge(c_sqd, n + 1)
                t, side = divmod(n, 2)
                dve.tensor_reduce(c_n2[:, t, NH * side:NH * (side + 1)],
                                  c_sq[:, n % 2, :].rearrange("p (h d) -> p h d", d=CD), AX.X, ALU.add
                                  ).then_inc(c_n2d, 1)
            dve.wait_ge(c_n2d, 2 * T)
            dve.tensor_reduce(c_mx, c_n2.rearrange("p t h -> p h t"), AX.X, ALU.max).then_inc(c_mxd, 1)
            dve.wait_ge(ln_xnT, 20)
            c(dve.tensor_tensor_scan(c_cum, xnT[:, XO:XO + S], c_zero, 0.0, ALU.add, ALU.add))
            dve.wait_ge(c_mxt, 1)
            dve.tensor_reduce(c_r[0:2 * NH, 0:1], bank[4][0:2 * NH, 0:P], AX.X, ALU.max).then_inc(c_mxr, 1)
            dve.wait_ge(c_rd, 1)
            dve.tensor_scalar(c_diag[0:2 * NH, :], ident[0:2 * NH, 0:2 * NH], c_r[0:2 * NH, 1:2], None, ALU.mult
                              ).then_inc(c_dg, 1)
            dve.wait_ge(c_bc, 1)
            c(dve.tensor_copy(c_rr, bank[4][:, 128:128 + 2 * NH]))
            c(dve.tensor_tensor(c_ch, c_rr[:, 0:NH], c_rr[:, NH:2 * NH], ALU.mult))
            for i in range(4):
                dve.wait_ge(c_am, i + 1)
                hs = c_as.rearrange("p (a j o) n -> p a j o n", a=2, o=2)[:, i % 2, :, i // 2, :]
                ch = c_ch.rearrange("p (a j o) -> p a j o", a=2, o=2)[:, i % 2, :, i // 2]
                dve.tensor_tensor(hs, bank[i].rearrange("p (h n) -> p h n", h=4),
                                  ch.unsqueeze(2).broadcast_to([P, 4, P]), ALU.mult).then_inc(c_asd, 1)
            dve.memset(c_vs[:, :, 0:1], 0.0)
            dve.wait_ge(c_vsm, 1)
            dve.tensor_copy(c_vs[:, :, 1:T], bank[5][:, 0:T * NH // 2].rearrange("p (j t) -> p j t", t=T)[:, :, 1:T])

            def outputs(t):
                dve.wait_ge(c_num, 4 * t + 4)
                dve.wait_ge(c_rpc, t + 1)
                for j in range(NH // 2):
                    ins = dve.scalar_tensor_tensor(c_vhT[:, j, :], bank[6 + j // 4][:, P * (j % 4):P * (j % 4 + 1)],
                                                   c_vs[:, j, t:t + 1], c_rep[:, j, :], ALU.add, ALU.mult)
                ins.then_inc(c_vhd, 1)

            def update(t):
                if t == 0:
                    dve.wait_ge(c_consts, 3)
                dve.wait_ge(c_out, t + 1)
                ins = dve.tensor_tensor(x[:, t, :], bank[7][:, 0:P], x[:, t, :], ALU.add)
                ins.then_inc(x_ready if t % 4 == 3 else c_xadd, 1)

            for t in range(T):
                for i in range(4):
                    hs = slice(4 * i, 4 * i + 4)
                    dve.wait_ge(c_apc, 4 * t + i + 1)
                    if t:
                        dve.wait_ge(c_scm, 4 * t)
                    dve.tensor_tensor(c_ar[:, 1, hs, :], c_a[:, hs, :], c_ar[:, 0, hs, :].bitcast(F32), ALU.subtract
                                      ).then_inc(c_alo, 1)
                if t:
                    outputs(t - 1)
                for i in range(4):
                    hs = slice(4 * i, 4 * i + 4)
                    dve.wait_ge(c_scm, 4 * t + i + 1)
                    dve.scalar_tensor_tensor(c_s[:, hs, :], bank[i].rearrange("p (h n) -> p h n", h=4), 1.0,
                                             c_mask.unsqueeze(1).broadcast_to([P, 4, P]), ALU.add, ALU.mult
                                             ).then_inc(c_scd, 1)
                if t:
                    update(t - 1)
                    if t % 4 == 0:
                        ln_follow(dve, 5, t // 4 - 1)
                dve.wait_ge(c_dm, t + 1)
                c(dve.scalar_tensor_tensor(c_den[:, 0], bank[4][:, 0:P], float(P * t), c_cnt, ALU.add, ALU.add))
                dve.reciprocal(c_den[:, 1], c_den[:, 0]).then_inc(c_rdd, 1)
                if t < T - 1:
                    for i in range(4):
                        hs = slice(4 * i, 4 * i + 4)
                        dve.wait_ge(c_kvm, 4 * t + i + 1)
                        if t:
                            dve.wait_ge(c_kvd, 4 * t)
                        dve.tensor_tensor(c_kv[:, hs, :], bank[i][:, 0:4 * CD].rearrange("p (h d) -> p h d", h=4),
                                          c_kv[:, hs, :], ALU.add).then_inc(c_kvd, 1)
            outputs(T - 1)
            update(T - 1)
            ln_follow(dve, 5, G - 1)

        def cla_added(engine, t):
            if t % 4 == 3:
                engine.wait_ge(x_ready, 16 + t // 4 + 1)
            else:
                engine.wait_ge(c_xadd, 3 * (t // 4) + t % 4 + 1)

        def cla_tensor(pe):
            pe.wait_ge(later_load, LATER)
            pe.wait_ge(c_wlo, 2)
            pe.wait_ge(ln_xnT, 20)
            pe.wait_ge(ln_lo, 4)
            for n in range(2 * T):
                t, side = divmod(n, 2)
                if n >= 4:
                    pe.wait_ge(c_sqd, n - 3)
                for a in range(2):
                    for q, (v, w) in enumerate(PARTS):
                        ins = pe.matmul(pair[n % 4][:, a, :], xr[:, v, P * t:P * (t + 1)],
                                        c_wr[:, side, w, NB * a:NB * (a + 1)], start=(q == 0), stop=(q == 2))
                ins.then_inc(c_qk, 1)
            pe.wait_ge(c_sqd, 2 * T)
            for i in range(4):
                rows = slice(CD * (i // 2), CD * (i // 2 + 1))
                for j in range(4):
                    ins = pe.matmul(bank[i][:, P * j:P * (j + 1)], c_wnat[rows, 0, 4 * (i % 2) + j, :],
                                    c_wnat[rows, 1, 4 * (i % 2) + j, :])
                ins.then_inc(c_am, 1)
                if i == 1:
                    pe.wait_ge(c_mxd, 1)
                    pe.transpose(bank[4][0:2 * NH, 0:P], c_mx, ident[:, :]).then_inc(c_mxt, 1)
            pe.wait_ge(c_dg, 1)
            pe.matmul(bank[4][:, 128:128 + 2 * NH], c_ones[0:2 * NH, :], c_diag[0:2 * NH, :]).then_inc(c_bc, 1)
            ends = c_cum.rearrange("p (t n) -> p t n", n=P)[:, 0:T - 1, P - 1]
            for j in range(NH // 2):
                ins = pe.matmul(bank[5][:, T * j + 1:T * (j + 1)], c_wvT[:, 2 * j:2 * j + 2, :], ends)
            ins.then_inc(c_vsm, 1)

            def project(t):
                for i in range(4):
                    if t == 0:
                        pe.wait_ge(c_asd, 4)
                    elif t < T:
                        pe.wait_ge(c_kvd, 4 * (t - 1) + i + 1)
                    for j in range(4):
                        ins = pe.matmul(bank[i][:, P * j:P * (j + 1)], c_as[:, 4 * i + j, :], xnT[:, xtile(t)])
                    ins.then_inc(c_apm, 1)

            def repeat(t):
                pe.wait_ge(c_rdd, t + 1)
                for j in range(NH // 2):
                    ins = pe.matmul(bank[4 + j // 4][:, P * (j % 4):P * (j % 4 + 1)], c_sel[:, j], c_den[:, 1])
                ins.then_inc(c_rpm, 1)

            def finish(t):
                pe.wait_ge(c_vhd, t + 1)
                for j in range(NH // 2):
                    ins = pe.matmul(bank[7][:, 0:P], c_vhT[:, j, :], c_woT[:, j, :], start=(j == 0), stop=(j == NH // 2 - 1))
                ins.then_inc(c_out, 1)

            for t in range(T):
                project(t)
                if t:
                    repeat(t - 1)
                for i in range(4):
                    pe.wait_ge(c_alo, 4 * t + i + 1)
                    for q, (v, w) in enumerate(PARTS):
                        ins = pe.matmul(bank[i], xr[:, v, P * t:P * (t + 1)], c_ar[:, w, 4 * i:4 * i + 4, :],
                                        start=(q == 0), stop=(q == 2))
                    ins.then_inc(c_scm, 1)
                if t:
                    pe.wait_ge(c_rpc, t)
                for a in range(2):
                    ins = pe.matmul(pair[2][:, a, :], xnT[:, xtile(t)], c_wvT[:, 8 * a:8 * (a + 1), :])
                ins.then_inc(c_vm, 1)
                if t:
                    finish(t - 1)
                pe.wait_ge(c_vc, t + 1)
                for j in range(NH // 2):
                    o = bank[6 + j // 4][:, P * (j % 4):P * (j % 4 + 1)]
                    if j == 4 and t:
                        cla_added(pe, t - 1)
                    if t and j % 2 == 0:
                        pe.wait_ge(c_kvd, 4 * (t - 1) + j // 2 + 1)
                    if t:
                        for i in range(2):
                            pe.matmul(o[CD * i:CD * (i + 1), :], c_kv[:, 2 * j + i, :], c_a[:, 2 * j + i, :],
                                      start=True, stop=False, tile_position=(0, CD * i))
                    if j % 2 == 0:
                        pe.wait_ge(c_scd, 4 * t + j // 2 + 1)
                    for i in range(2):
                        ins = pe.matmul(o[CD * i:CD * (i + 1), :], c_v[:, t % 2, 2 * j + i, :], c_s[:, 2 * j + i, :],
                                        start=(t == 0), stop=True, tile_position=(0, CD * i))
                    if j % 2 == 1:
                        ins.then_inc(c_num, 1)
                pe.wait_ge(c_zd, 4 * t + 4)
                for j in range(4):
                    for i in range(4):
                        ins = pe.matmul(bank[4][32 * i:32 * (i + 1), 0:P], c_unit[:, j, :], c_z[:, 4 * i + j, :],
                                        start=(j == 0), stop=(j == 3), tile_position=(0, 32 * i))
                ins.then_inc(c_dm, 1)
                if t < T - 1:
                    for i in range(4):
                        pe.matmul(bank[i][:, 0:4 * CD], xn[:, t, :], c_v[:, t % 2, 4 * i:4 * i + 4, :]).then_inc(c_kvm, 1)
            repeat(T - 1)
            finish(T - 1)
            cla_added(pe, T - 1)

        arena.reset()
        g_lg = arena.take(20, T, NE)
        g_red = arena.take(8, T)
        g_s = arena.take(3, NB)
        g_h = arena.take(3, 2, NB)
        assert arena.at <= LATER_AT

        rounded.at = XR_WORDS
        g_wr = rounded.take(2, 2, 2, GI)
        g_whi = sem("g_whi")
        g_wlo = sem("g_wlo")
        g_c = sem("g_c")
        g_gate = sem("g_gate")
        g_gd = sem("g_gd")
        g_ge = sem("g_ge")
        g_hm = sem("g_hm")
        g_silu = sem("g_silu")
        g_mul = sem("g_mul")
        g_y = sem("g_y")
        g_add = sem("g_add")
        count["g_c"] = 0
        MIDDLE = 4 * (NX - 1)
        STEPS = 4 * NX

        def moe_high(act, rep, e):
            if rep == 0 and e == 0:
                act.wait_ge(later_load, LATER)
                act.wait_ge(x_ready, 20)
            elif e == 0:
                act.wait_ge(x_ready, 28)
            elif e >= 2:
                act.wait_ge(g_hm, 2 * STEPS * rep + 8 * (e - 1))
            act.activation(g_wr[:, e % 2, 0], g_w13[:, :, e, :], ACT.Copy).then_inc(g_whi, 1)

        def moe_low(pool, rep, e):
            pool.wait_ge(g_whi, NX * rep + e + 1)
            pool.tensor_tensor(g_wr[:, e % 2, 1], g_w13[:, :, e, :], g_wr[:, e % 2, 0].bitcast(F32), ALU.subtract
                               ).then_inc(g_wlo, 1)

        def moe_gpsimd(pool, rep):
            for e in range(1, NX):
                moe_low(pool, rep, e)

        def moe_scalar(act, rep):
            for n in range(STEPS):
                if n % 4 == 1 and n // 4 + 1 < NX:
                    moe_high(act, rep, n // 4 + 1)
                if n == 2:
                    act.wait_ge(g_gd, rep + 1)
                    act.activation(g_lg[:, 2], g_lg[:, 1], ACT.Exp).then_inc(g_ge, 1)
                for i in range(2):
                    m = 2 * STEPS * rep + 2 * n + i
                    act.wait_ge(g_hm, m + 1)
                    if m >= 3:
                        act.wait_ge(g_mul, m - 2)
                    act.activation(g_s[:, m % 3, :], pair[m % 3][:, 0, :], ACT.Silu).then_inc(g_silu, 1)

        def moe_vector(dve, rep):
            c = lambda ins: link(dve, g_c, "g_c", ins)
            L = g_lg
            over = lambda col: col.unsqueeze(2).broadcast_to([P, T, NE])
            along = lambda row: row.unsqueeze(1).broadcast_to([P, T, NE])
            k = 5 + 2 * rep
            lg = bank[7][:, 0:T * NE].rearrange("p (t e) -> p t e", e=NE)

            def gate_logits():
                dve.wait_ge(g_gate, rep + 1)
                c(dve.tensor_reduce(g_red[:, 0], lg, AX.X, ALU.max))
                dve.tensor_tensor(L[:, 1], lg, over(g_red[:, 0]), ALU.subtract).then_inc(g_gd, 1)

            def gate_softmax():
                dve.wait_ge(g_ge, rep + 1)
                c(dve.tensor_reduce(g_red[:, 1], L[:, 2], AX.X, ALU.add))
                c(dve.reciprocal(g_red[:, 2], g_red[:, 1]))
                c(dve.tensor_tensor(L[:, 3], L[:, 2], over(g_red[:, 2]), ALU.mult))
                c(dve.tensor_tensor(L[:, 4], L[:, 3], along(g_gb), ALU.add))

            def best(src, at, red):
                c(dve.tensor_reduce(g_red[:, red], L[:, src], AX.X, ALU.max))
                c(dve.tensor_tensor(L[:, at], L[:, src], over(g_red[:, red]), ALU.is_equal))
                c(dve.tensor_tensor(L[:, at + 1], L[:, at], along(g_pref), ALU.mult))
                c(dve.tensor_reduce(g_red[:, red + 1], L[:, at + 1], AX.X, ALU.max))
                c(dve.tensor_tensor(L[:, at + 2], L[:, at + 1], over(g_red[:, red + 1]), ALU.is_equal))

            def gate_second():
                c(dve.scalar_tensor_tensor(L[:, 8], L[:, 7], -1e30, L[:, 4], ALU.mult, ALU.add))
                best(8, 9, 5)

            def gate_weights():
                c(dve.tensor_tensor(L[:, 12], L[:, 7], L[:, 11], ALU.add))
                c(dve.tensor_tensor(L[:, 13], L[:, 3], L[:, 12], ALU.mult))

            def add(n):
                e, b = divmod(n, 4)
                dve.wait_ge(g_y, STEPS * rep + n + 1)
                if e:
                    dve.wait_ge(g_add, MIDDLE * rep + n - 3)
                y = bank[6 + n % 2]
                for i in range(4):
                    t = 4 * b + i
                    w = L[:, 13, t, e - 1:e] if e else 1.0
                    ins = dve.scalar_tensor_tensor(x[:, t, :], y[:, P * i:P * (i + 1)], w, x[:, t, :], ALU.mult, ALU.add)
                ins.then_inc(x_ready if n >= MIDDLE else g_add, 1)
                if n >= MIDDLE:
                    ln_follow(dve, k + 1, b)

            if rep == 0:
                dve.wait_ge(later_load, LATER)
            dve.wait_ge(ln_xn, 4 * k + 4)
            for n in range(STEPS):
                for i in range(2):
                    m = 2 * STEPS * rep + 2 * n + i
                    nn = STEPS * rep + n
                    dve.wait_ge(g_silu, m + 1)
                    if nn >= 3:
                        dve.wait_ge(g_y, nn - 2)
                    dve.tensor_tensor(g_h[:, nn % 3, i, :], pair[m % 3][:, 1, :], g_s[:, m % 3, :], ALU.mult
                                      ).then_inc(g_mul, 1)
                if n == 1:
                    gate_logits()
                if n:
                    add(n - 1)
                if n == 2:
                    gate_softmax()
                    best(4, 5, 3)
                if n == 3:
                    gate_second()
                    gate_weights()
            add(STEPS - 1)

        def moe_tensor(pe, rep):
            k = 5 + 2 * rep
            pe.wait_ge(later_load, LATER)

            def up(n):
                e, b = divmod(n, 4)
                if e == 0:
                    pe.wait_ge(ln_lo, 4 * (k - SPLIT) + b + 1)
                if b == 0:
                    pe.wait_ge(g_wlo, NX * rep + e + 1)
                for i in range(2):
                    m = 2 * STEPS * rep + 2 * n + i
                    if m >= 3:
                        pe.wait_ge(g_mul, m - 2)
                    for a in range(2):
                        for q, (w, v) in enumerate(PARTS):
                            ins = pe.matmul(pair[m % 3][:, a, :], g_wr[:, e % 2, w, a, P * i:P * (i + 1)],
                                            xr[:, v, NB * b:NB * (b + 1)], start=(q == 0), stop=(q == 2))
                    ins.then_inc(g_hm, 1)

            def gate():
                pe.wait_ge(ln_xnT, 4 * k + 4)
                for t in range(T):
                    ins = pe.matmul(bank[7][:, NE * t:NE * (t + 1)], xnT[:, xtile(t)], g_gw)
                ins.then_inc(g_gate, 1)

            def down(n):
                e, b = divmod(n, 4)
                nn = STEPS * rep + n
                pe.wait_ge(g_mul, 2 * nn + 2)
                if n == 1:
                    pe.wait_ge(g_gd, rep + 1)
                if n >= MIDDLE + 2:
                    pe.wait_ge(x_ready, 4 * k + n - MIDDLE - 1)
                elif n >= 2:
                    pe.wait_ge(g_add, MIDDLE * rep + n - 1)
                for i in range(4):
                    for j in range(2):
                        ins = pe.matmul(bank[6 + n % 2][:, P * i:P * (i + 1)], g_h[:, nn % 3, j, P * i:P * (i + 1)],
                                        g_w2[:, e, j, :], start=(j == 0), stop=(j == 1))
                ins.then_inc(g_y, 1)

            for n in range(STEPS):
                up(n)
                if n == 1:
                    gate()
                if n:
                    down(n - 1)
            down(STEPS - 1)
            pe.wait_ge(x_ready, 4 * (k + 1))

        arena.reset()
        d_a = arena.take(P)
        d_b = arena.take(P)
        rounded.at = XR_WORDS
        d_aT = rounded.take(2, S)
        d_v = arena.take(T, P)
        d_p = arena.take(2, S)
        d_pT = arena.take(4, NB)
        d_m = arena.take(T, 8)
        assert arena.at <= LATER_AT
        d_c = sem("d_c")
        d_fold = sem("d_fold")
        d_foldc = sem("d_foldc")
        d_pre = sem("d_pre")
        d_prec = sem("d_prec")
        d_low = sem("d_low")
        d_s = sem("d_s")
        d_max = sem("d_max")
        d_bias = sem("d_bias")
        d_exp = sem("d_exp")
        d_tr = sem("d_tr")
        d_trA = sem("d_trA")
        d_trB = sem("d_trB")
        d_pv = sem("d_pv")
        d_x = sem("d_x")
        count["d_c"] = 0
        SC7 = float(np.float32(1.0) / np.sqrt(np.float32(P)))

        def soft_scalar(act):
            act.wait_ge(d_fold, 1)
            act.activation(d_a, bank[0][:, 0:P], ACT.Copy)
            act.activation(d_b, bank[0][:, P:2 * P], ACT.Copy).then_inc(d_foldc, 1)
            for n in range(8):
                act.wait_ge(d_pre, n + 1)
                dst = d_aT[:, 0, NB * n:NB * (n + 1)] if n < 4 else d_v[:, 4 * (n - 4):4 * (n - 3), :].rearrange("p t n -> p (t n)")
                act.activation(dst, bank[n % 4], ACT.Copy).then_inc(d_prec, 1)

            def turned(t):
                for i in range(2):
                    j = 4 * t + i
                    act.wait_ge(d_tr, j + 1)
                    if t:
                        act.wait_ge(d_pv, j - 3)
                    act.activation(d_pT[:, i, :], bank[4 + i], ACT.Copy).then_inc(d_trA, 1)

            for t in range(T):
                if t:
                    turned(t - 1)
                act.wait_ge(d_bias, t + 1)
                if t >= 2:
                    act.wait_ge(d_tr, 4 * (t - 1))
                for a in range(2):
                    act.activation(d_p[:, t % 2, 2 * NB * a:2 * NB * (a + 1)].rearrange("p (a n) -> p a n", a=2),
                                   pair[a][:, :, :], ACT.Exp, bias=d_m[:, t, 3:4], scale=SC7,
                                   accum_out=d_m[:, t, 4 + a:5 + a]).then_inc(d_exp, 1)
            turned(T - 1)

        def soft_vector(dve):
            c = lambda ins: link(dve, d_c, "d_c", ins)

            def turned(t):
                for i in range(2, 4):
                    j = 4 * t + i
                    dve.wait_ge(d_tr, j + 1)
                    if t:
                        dve.wait_ge(d_pv, j - 3)
                    dve.tensor_copy(d_pT[:, i, :], bank[4 + i % 2]).then_inc(d_trB, 1)

            def finish(t):
                dve.wait_ge(d_exp, 2 * t + 2)
                c(dve.tensor_reduce(d_m[:, t, 6:7], d_m[:, t, 4:6], AX.X, ALU.add))
                c(dve.reciprocal(d_m[:, t, 7:8], d_m[:, t, 6:7]))
                dve.wait_ge(d_pv, 4 * t + 4)
                ins = dve.scalar_tensor_tensor(x[:, t, :], bank[6 + t % 2][:, 0:P], d_m[:, t, 7:8], x[:, t, :],
                                               ALU.mult, ALU.add)
                ins.then_inc(x_ready if t % 4 == 3 else d_x, 1)
                if t % 4 == 3:
                    ln_follow(dve, 7, t // 4)

            dve.wait_ge(ln_xn, 28)
            for n in range(4):
                dve.wait_ge(d_prec, n + 1)
                dve.tensor_tensor(d_aT[:, 1, NB * n:NB * (n + 1)], bank[n],
                                  d_aT[:, 0, NB * n:NB * (n + 1)].bitcast(F32), ALU.subtract).then_inc(d_low, 1)
            for t in range(T):
                for a in range(2):
                    dve.wait_ge(d_s, 2 * t + a + 1)
                    dve.tensor_reduce(d_m[:, t, a:a + 1], pair[a][:, :, :], AX.XY, ALU.max).then_inc(d_max, 1)
                dve.wait_ge(d_max, 2 * t + 2)
                c(dve.tensor_reduce(d_m[:, t, 2:3], d_m[:, t, 0:2], AX.X, ALU.max))
                dve.tensor_scalar(d_m[:, t, 3:4], d_m[:, t, 2:3], -SC7, None, ALU.mult).then_inc(d_bias, 1)
                if t:
                    turned(t - 1)
                if t >= 1:
                    finish(t - 1)
            turned(T - 1)
            finish(T - 1)

        def soft_added(engine, t):
            if t % 4 == 3:
                engine.wait_ge(x_ready, 24 + t // 4 + 1)
            else:
                engine.wait_ge(d_x, 3 * (t // 4) + t % 4 + 1)

        def soft_tensor(pe):
            pe.wait_ge(ln_xnT, 25)
            pe.matmul(bank[0][:, 0:P], d_w[:, 0, :], d_w[:, 1, :])
            pe.matmul(bank[0][:, P:2 * P], d_w[:, 2, :], d_w[:, 3, :]).then_inc(d_fold, 1)
            pe.wait_ge(d_foldc, 1)
            for n in range(8):
                pe.wait_ge(ln_xnT, 24 + n % 4 + 1)
                if n >= 4:
                    pe.wait_ge(d_low, n - 3)
                if n < 4:
                    ins = pe.matmul(bank[n % 4], d_a, xnT[:, xcol(n)])
                else:
                    for i in range(4):
                        ins = pe.matmul(bank[n % 4][:, P * i:P * (i + 1)], xnT[:, xtile(4 * (n - 4) + i)], d_b)
                ins.then_inc(d_pre, 1)
            pe.wait_ge(d_prec, 8)
            pe.wait_ge(ln_lo, 4 * (6 - SPLIT) + 4)

            def scores(t, a):
                if t:
                    pe.wait_ge(d_exp, 2 * (t - 1) + a + 1)
                for b in range(2):
                    for q, (w, v) in enumerate(PARTS):
                        ins = pe.matmul(pair[a][:, b, :], d_aT[:, w, P * t:P * (t + 1)],
                                        xr[:, v, NB * (2 * a + b):NB * (2 * a + b + 1)], start=(q == 0), stop=(q == 2))
                ins.then_inc(d_s, 1)

            def turn(t, i):
                if i % 2 == 0:
                    pe.wait_ge(d_exp, 2 * t + i // 2 + 1)
                if i >= 2:
                    pe.wait_ge(d_trA, 2 * t + i - 1)
                elif t:
                    pe.wait_ge(d_trB, 2 * (t - 1) + i + 1)
                for q in range(4):
                    ins = pe.transpose(bank[4 + i % 2][:, P * q:P * (q + 1)],
                                       d_p[:, t % 2, NB * i + P * q:NB * i + P * (q + 1)], ident[:, :])
                ins.then_inc(d_tr, 1)

            def values(t, i):
                pe.wait_ge(d_trA if i < 2 else d_trB, 2 * t + i % 2 + 1)
                if i == 0 and t >= 2:
                    soft_added(pe, t - 2)
                for q in range(4):
                    ins = pe.matmul(bank[6 + t % 2][:, 0:P], d_pT[:, i, P * q:P * (q + 1)], d_v[:, 4 * i + q, :],
                                    start=(i == 0 and q == 0), stop=(i == 3 and q == 3))
                ins.then_inc(d_pv, 1)

            scores(0, 0)
            scores(0, 1)
            for t in range(T):
                if t + 1 < T:
                    scores(t + 1, 0)
                turn(t, 0)
                turn(t, 1)
                if t + 1 < T:
                    scores(t + 1, 1)
                for i in range(4):
                    values(t, i)
                    if i < 2:
                        turn(t, i + 2)
            soft_added(pe, T - 2)
            soft_added(pe, T - 1)

        def later_stages(n):
            ffn = lambda rep: {"pool": lambda e: ffn_gpsimd(e, rep), "act": lambda e: ffn_scalar(e, rep),
                               "dve": lambda e: ffn_vector(e, rep), "pe": lambda e: ffn_tensor(e, rep)}
            dla = {"pool": dla_gpsimd, "act": dla_scalar, "dve": dla_vector, "pe": dla_tensor}
            moe = lambda rep: {"act": lambda e: moe_scalar(e, rep), "pool": lambda e: moe_gpsimd(e, rep),
                               "dve": lambda e: moe_vector(e, rep), "pe": lambda e: moe_tensor(e, rep)}
            cla = {"pool": cla_gpsimd, "act": cla_scalar, "dve": cla_vector, "pe": cla_tensor}
            soft = {"pool": lambda e: None, "act": soft_scalar, "dve": soft_vector, "pe": soft_tensor}
            return [ffn(0), dla, ffn(1), cla, moe(0), soft, moe(1)][:n - 1]

        block = ctx.enter_context(nc.Block())

        @block.sync
        def _(sp):
            for g in range(G):
                sp.dma_start(x[:, 4 * g:4 * g + 4, :], I["x"][NB * g:NB * (g + 1), :].rearrange("(t p) d -> p t d", p=P)
                             ).then_inc(x_in[g], 16)
            mla_load(sp)
            ffn_load(sp)
            dla_load(sp)
            mla_sync(sp)
            if STAGES > 4:
                later_weights(sp)
            for g in range(G):
                sp.wait_ge(x_ready, 4 * (STAGES - 1) + g + 1)
                sp.dma_start(out[NB * g:NB * (g + 1), :].rearrange("(t p) d -> p t d", p=P),
                             x[:, 4 * g:4 * g + 4, :]).then_inc(stored, 16)
            sp.wait_ge(stored, 64)

        @block.gpsimd
        def _(pool):
            pool.memset(ident[:, :], 0.0).then_inc(ident_done, 1)
            pool.memset(mhalf[:, :], -0.5).then_inc(ident_done, 1)
            pool.wait_ge(ident_done, 2)
            pool.affine_select(out=ident[:, :], in_=ident[:, :], compare_op=ALU.not_equal, fill=1.0, base=0,
                               pattern=[[-1, P]], channel_multiplier=1).then_inc(ident_done, 1)
            pool.memset(vpad, 0.0).then_inc(a_vzero, 1)
            pool.wait_ge(a_vzero, 1)
            pool.memset(vpad[:, :, :, DH:DH + 1], 1.0).then_inc(a_vzero, 1)
            ln_gpsimd(pool, 0)

            def prepare(n):
                g, qb, kt = UNITS[n]
                if (g, qb, kt) == (0, 1, 7):
                    for part in range(4):
                        pool.wait_ge(a_parts[part], 16 * G)
                    pool.memset(stack[1][0].bitcast(F32), 0.0)
                    pool.memset(stack[1][1].bitcast(F32), 0.0).then_inc(a_zero, 1)
                if (g, qb, kt) == (0, 2, 11):
                    ffn_rows_gpsimd(pool)
                if (g, qb, kt) == (1, 2, 11):
                    ffn_tokens_gpsimd(pool)
                if g == 3 and qb < 3 and kt == 4 * qb + 3:
                    if qb == 0:
                        pool.wait_ge(a_pv, last_unit[(2, G - 1)] + 1)
                    ffn_onehots_gpsimd(pool, qb)

            mla_gpsimd(pool, prepare)
            for k, stage in enumerate(later_stages(STAGES)):
                ln_gpsimd(pool, k + 1)
                if k + 1 in (5, 7):
                    moe_low(pool, (k + 1) // 7, 0)
                if k + 1 >= SPLIT:
                    ln_low(pool, k + 1)
                stage["pool"](pool)

        @block.scalar
        def _(act):
            mla_fold_scalar(act)
            ln_scalar(act, 0)
            mla_scalar(act)
            for k, stage in enumerate(later_stages(STAGES)):
                if k + 1 == 4:
                    cla_high(act)
                if k + 1 in (5, 7):
                    moe_high(act, (k + 1) // 7, 0)
                ln_scalar(act, k + 1)
                stage["act"](act)

        @block.vector
        def _(dve):
            dve.memset(xnT[:, 0:XO], 0.0)
            for g in range(G):
                ln_follow(dve, 0, g)
            dla_decay_vector(dve, 0)
            mla_vector(dve)
            for k, stage in enumerate(later_stages(STAGES)):
                stage["dve"](dve)

        @block.tensor
        def _(pe):
            pe.wait_ge(ident_done, 3)
            mla_fold_tensor(pe)
            ln_tensor(pe, 0)
            mla_tensor(pe)
            for k, stage in enumerate(later_stages(STAGES)):
                if k + 1 in (1, 3):
                    ln_tensor(pe, k + 1, lambda g: ffn_gather(pe, (k + 1) // 2, g))
                else:
                    ln_tensor(pe, k + 1)
                stage["pe"](pe)


def host_layout(inputs):
    f = lambda name: np.asarray(inputs[name])
    z = lambda *shape: np.zeros(shape, np.float32)
    A = {}
    A["x"] = f("L0_attn_a_x").reshape(S, P)
    wdq, wdkv = f("L0_attn_a_W_DQ"), f("L0_attn_a_W_DKV")
    wqr, wkr = f("L0_attn_a_W_QR"), f("L0_attn_a_W_KR")
    A["WDQT"], A["WDKVT"] = wdq.T, wdkv.T
    swap = np.arange(HR).reshape(-1, 2)[:, ::-1].reshape(-1)
    A["WQR2"] = np.concatenate([wqr, wqr[:, swap]], axis=1)
    ab = z(2, P, P - HR)
    ab[0, :, 0:DR] = wkr
    ab[1, :, 0:DR] = wkr[:, swap[:DR]]
    ab[0, :, 32:64] = wdq
    A["WABr"] = ab
    A["WUV"] = f("L0_attn_a_W_UV")
    uk = z(DL, NH, DQK)
    uk[:, :, 0:DH] = f("L0_attn_a_W_UK").reshape(DL, NH, DH)
    A["WUKc"] = uk.reshape(DL, NH * DQK)
    wq, wks = z(P, NH, DQK), z(P, NH, DQK)
    wq[96:P, :, 0:DH] = f("L0_attn_a_W_UQ").reshape(DL, NH, DH)
    for h in range(NH):
        for i in range(DR):
            wq[DR * h + i, h, DH + i] = 1.0
            wks[HR + i, h, DH + i] = 1.0
    A["WQc"], A["WKsel"] = wq.reshape(P, -1), wks.reshape(P, -1)
    A["WO"] = f("L0_attn_a_W_O")
    inv = np.float32(10000.0) ** (-np.arange(0, DR, 2, dtype=np.float32) / np.float32(DR))
    angle = np.arange(S, dtype=np.float32)[:, None] * inv
    cos, sin = z(96, S), z(96, S)
    for r in range(HR + DR):
        cos[r] = np.cos(angle[:, (r % DR) // 2])
        sin[r] = np.sin(angle[:, (r % DR) // 2]) * (1.0 if r % 2 else -1.0)
    A["cosT"], A["sinT"] = cos, sin
    e1, e2, e3 = f("L0_ffn_ew1"), f("L0_ffn_ew2"), f("L0_ffn_ew3")
    w12 = z(P, 2, NE + 1, FH)
    b12 = z(2, NE + 1, FH)
    for a, (w, b, sw, sb) in enumerate(((e1, "L0_ffn_eb1", "L0_ffn_sw1", "L0_ffn_sb1"),
                                        (e2, "L0_ffn_eb2", "L0_ffn_sw2", "L0_ffn_sb2"))):
        w12[:, a, 0:NE] = w.transpose(2, 0, 1)
        w12[:, a, NE] = f(sw).T
        b12[a, 0:NE], b12[a, NE] = f(b), f(sb)
    A["F_w12"], A["F_b12"] = w12, b12.reshape(-1)
    w3 = z(P, 5, P)
    w3[:, 0:4] = e3.transpose(0, 2, 1).reshape(4, P, P).transpose(1, 0, 2)
    w3[0:FH, 4] = f("L0_ffn_sw3").T
    w3[FH, 4] = f("L0_ffn_sb3")
    w3[FH + 1:FH + 1 + NE, 4] = f("L0_ffn_eb3")
    A["F_w3"] = w3
    bsel, gcol = z(P, 5, NE + 1), z(P, 5)
    for kt in range(4):
        for half in range(2):
            rows = slice(FH * half, FH * (half + 1))
            bsel[rows, kt, 1 + 2 * kt + half] = f("L0_ffn_sel_ln_b")
            gcol[rows, kt] = f("L0_ffn_sel_ln_g")
    bsel[0:FH, 4, 0] = f("L0_ffn_s_ln_b")
    gcol[0:FH, 4] = f("L0_ffn_s_ln_g")
    A["F_bsel"], A["F_gcol"] = bsel, gcol
    A["F_wg"] = np.concatenate([f("L0_ffn_eg_w").T, f("L0_ffn_sg_w").T], axis=1)
    A["F_bg"] = np.concatenate([f("L0_ffn_eg_b"), f("L0_ffn_sg_b")])
    A["F_bx"] = f("L0_ffn_exp_bias")
    A["F_pref"] = np.arange(NE, 0, -1).astype(np.float32)
    for name, rows in (("F_ib", f("L0_ffn_index_b")), ("F_it", f("L0_ffn_index_t"))):
        A[name], A[name + "c"] = rows, rows.reshape(2, P).T
    A["B_ww"], A["B_wrT"] = f("L0_attn_b_W_write"), f("L0_attn_b_W_read").T
    A["B_decay"], A["B_la"] = f("L0_attn_b_decay").reshape(1), f("L0_attn_b_log_alpha").reshape(1)
    wq, wk, wv, wo = (f("L1_attn_a_" + n) for n in ("Wq", "Wk", "Wv", "Wo"))
    A["C_wnat"] = np.stack([w.reshape(NH // 2, P, P).transpose(1, 0, 2) for w in (wq, wk)], axis=1)
    A["C_wqkT"] = np.stack([wq.T, wk.T], axis=1)
    A["C_wvT"] = wv.T.reshape(P, NH, CD)
    A["C_woT"] = wo.T.reshape(NH // 2, P, P).transpose(1, 0, 2)
    A["C_bo"] = f("L1_attn_a_bo")
    w13, w2 = z(P, 2, NX, GI), z(P, NX, 2, P)
    for a, n in enumerate(("1", "3")):
        w13[:, a, 1:NX] = f("L1_ffn_w" + n).transpose(2, 0, 1)
        w13[:, a, 0] = f("L1_ffn_sw" + n).T
    w2[:, 1:NX] = f("L1_ffn_w2").transpose(0, 2, 1).reshape(NE, 2, P, P).transpose(2, 0, 1, 3)
    w2[:, 0] = f("L1_ffn_sw2").T.reshape(2, P, P).transpose(1, 0, 2)
    A["G_w13"], A["G_w2"] = w13, w2
    A["G_gw"], A["G_gb"] = f("L1_ffn_gate_w").T, f("L1_ffn_gate_bias")
    qkv = f("L1_attn_b_W_qkv")
    A["D_w"] = np.stack([qkv[0::3], qkv[1::3], qkv[2::3], f("L1_attn_b_W_out").T], axis=1)
    return {k: np.ascontiguousarray(v) for k, v in A.items()}


def kernel(**inputs):
    import concourse.bacc as _bacc
    from concourse.bass_utils import run_bass_kernel_spmd as _run

    nc = _bacc.Bacc("TRN2", target_bir_lowering=False, num_devices=1)
    arrays = host_layout(inputs)
    aps = {name: nc.dram_tensor(f"in_{name}", a.shape, mybir.dt.from_np(a.dtype), kind="ExternalInput").ap()
           for name, a in arrays.items()}
    out = nc.dram_tensor("out", (S, P), F32, kind="ExternalOutput").ap()
    program(nc, aps, out)
    r = _run(nc, [{f"in_{name}": a for name, a in arrays.items()}], core_ids=[0])
    return r.results[0]["out"].reshape(1, S, P)
```
